# Optimizing a Trainium2 kernel written in Bass

```python
import numpy as np
import jax
import jax.numpy as jnp

def _softmax(x, axis=-1):
    return jax.nn.softmax(x, axis=axis)

def _gelu(x):
    return jax.nn.gelu(x, approximate=True)

def _silu(x):
    return jax.nn.silu(x)

def _sigmoid(x):
    return jax.nn.sigmoid(x)

def _layernorm(x, axis=-1, eps=1e-05):
    m = jnp.mean(x, axis=axis, keepdims=True)
    v = jnp.var(x, axis=axis, keepdims=True)
    return (x - m) / jnp.sqrt(v + eps)

def _scatter_add(tgt, idx, src, axis=0):
    return tgt.at[idx].add(src)

def _segment_sum(src, seg, n):
    return jax.ops.segment_sum(src, seg, n)
kernel_name = 'mk_gnn_preln_d2_gnn_r32_39b532'

def setup_inputs(seed: int=0):
    np.random.seed(seed)
    _w = jnp.asarray

    def _rec_inputs():
        import jax
        import jax.numpy as jnp
        _gk = jax.random.key(seed)
        x = -0.0003713 + 1 * jax.random.normal(jax.random.fold_in(_gk, 1), (50000, 256), jnp.float32)
        src = jax.random.randint(jax.random.fold_in(_gk, 2), (25000,), 0, 50000, jnp.int32)
        dst = jnp.minimum((50000 * jax.random.uniform(jax.random.fold_in(_gk, 3), (25000,)) ** 2.0).astype(jnp.int32), 49999)
        _o = jnp.argsort(dst, stable=True)
        src = src[_o]
        dst = dst[_o]
        edge_attr_10 = jax.random.uniform(jax.random.fold_in(_gk, 12), (25000, 10), jnp.float32, 0.0, 1)
        edge_attr_4 = 0.00109026 + 0.999989 * jax.random.normal(jax.random.fold_in(_gk, 13), (25000, 4), jnp.float32)
        return (x, src, dst, edge_attr_10, edge_attr_4)
    x, src, dst, edge_attr_10, edge_attr_4 = _rec_inputs()

    def _L0_gnn_setup():
        import jax, jax.numpy as jnp
        import numpy as np
        MUL = 64
        N_NODES = 50000
        N_EDGES = 25000
        NUM_NEIGHBORS = 16.0
        SILU_NORM = 1.679177
        key = jax.random.key(seed)
        ks = jax.random.split(key, 9)
        node_in = jax.random.normal(ks[0], (N_NODES, 4 * MUL), dtype=jnp.float32)
        edge_src = jax.random.randint(ks[1], (N_EDGES,), 0, N_NODES)
        edge_dst = jax.random.randint(ks[2], (N_EDGES,), 0, N_NODES)
        edge_attr = jax.random.normal(ks[3], (N_EDGES, 4), dtype=jnp.float32)
        edge_len_emb = jax.random.uniform(ks[4], (N_EDGES, 10), dtype=jnp.float32)
        w_00_0 = jax.random.normal(ks[5], (MUL, MUL), dtype=jnp.float32)
        w_11_0 = jax.random.normal(ks[6], (MUL, MUL), dtype=jnp.float32)
        w_01_1 = jax.random.normal(ks[7], (MUL, MUL), dtype=jnp.float32)
        w_10_1 = jax.random.normal(ks[8], (MUL, MUL), dtype=jnp.float32)
        kf = jax.random.split(jax.random.fold_in(key, 1), 2)
        fc_w1 = jax.random.normal(kf[0], (10, 64), dtype=jnp.float32)
        fc_w2 = jax.random.normal(kf[1], (64, 1), dtype=jnp.float32)
        return {'node_in': node_in, 'edge_attr': edge_attr, 'edge_len_emb': edge_len_emb, 'w_00_0': w_00_0, 'w_11_0': w_11_0, 'w_01_1': w_01_1, 'w_10_1': w_10_1, 'fc_w1': fc_w1, 'fc_w2': fc_w2, 'edge_src': edge_src, 'edge_dst': edge_dst}
    _L0_gnn_all = _L0_gnn_setup()
    _L0_gnn_in = {k: v for k, v in _L0_gnn_all.items() if k in ('w_00_0', 'w_11_0', 'w_01_1', 'w_10_1', 'fc_w1', 'fc_w2')}
    del _L0_gnn_all

    def _L1_gnn_setup():
        import jax, jax.numpy as jnp
        import numpy as np
        ALPHA = 0.2
        N_NODES, N_EDGES, N_FEAT, N_HID, N_HEADS = (50000, 25000, 256, 32, 8)
        key = jax.random.key(seed)
        k_h, k_w, k_a, k_s, k_d = jax.random.split(key, 5)
        h = jax.random.normal(k_h, (N_NODES, N_FEAT), dtype=jnp.float32)
        W = jax.random.normal(k_w, (N_HEADS, N_FEAT, N_HID), dtype=jnp.float32) * 0.05
        a = jax.random.normal(k_a, (N_HEADS, 2 * N_HID), dtype=jnp.float32) * 0.05
        src = jax.random.randint(k_s, (N_EDGES,), 0, N_NODES, dtype=jnp.int32)
        dst = jax.random.randint(k_d, (N_EDGES,), 0, N_NODES, dtype=jnp.int32)
        return {'h': h, 'W': W, 'a': a, 'src': src, 'dst': dst}
    _L1_gnn_all = _L1_gnn_setup()
    _L1_gnn_in = {k: v for k, v in _L1_gnn_all.items() if k in ('W', 'a')}
    del _L1_gnn_all
    return {'x': x, 'src': src, 'dst': dst, 'edge_attr_10': edge_attr_10, 'edge_attr_4': edge_attr_4, 'L0_gnn_w_00_0': _L0_gnn_in['w_00_0'], 'L0_gnn_w_11_0': _L0_gnn_in['w_11_0'], 'L0_gnn_w_01_1': _L0_gnn_in['w_01_1'], 'L0_gnn_w_10_1': _L0_gnn_in['w_10_1'], 'L0_gnn_fc_w1': _L0_gnn_in['fc_w1'], 'L0_gnn_fc_w2': _L0_gnn_in['fc_w2'], 'L1_gnn_W': _L1_gnn_in['W'], 'L1_gnn_a': _L1_gnn_in['a']}

def reference(x, src, dst, edge_attr_10, edge_attr_4, L0_gnn_w_00_0, L0_gnn_w_11_0, L0_gnn_w_01_1, L0_gnn_w_10_1, L0_gnn_fc_w1, L0_gnn_fc_w2, L1_gnn_W, L1_gnn_a):
    import jax
    import jax.numpy as jnp

    def _L0_gnn_ref(node_in, edge_attr, edge_len_emb, w_00_0, w_11_0, w_01_1, w_10_1, fc_w1, fc_w2, edge_src, edge_dst):
        import jax, jax.numpy as jnp
        import numpy as np
        MUL = 64
        N_NODES = 50000
        N_EDGES = 25000
        NUM_NEIGHBORS = 16.0
        SILU_NORM = 1.679177
        src = node_in[edge_src]
        s0 = src[:, :MUL]
        s1 = src[:, MUL:].reshape(-1, MUL, 3)
        a0 = edge_attr[:, 0:1]
        a1 = edge_attr[:, 1:4]
        alpha = np.float32(1.0 / np.sqrt(2.0 * MUL))
        inv_sqrt3 = np.float32(1.0 / np.sqrt(3.0))
        out0 = alpha * (jnp.einsum('ei,io->eo', s0 * a0, w_00_0) + inv_sqrt3 * jnp.einsum('eim,em,io->eo', s1, a1, w_11_0))
        out1 = alpha * (jnp.einsum('ei,io,em->eom', s0, w_01_1, a1) + jnp.einsum('eim,io->eom', s1 * a0[:, :, None], w_10_1))
        msg_ang = jnp.concatenate([out0, out1.reshape(-1, 3 * MUL)], axis=1)
        h = jax.nn.silu(edge_len_emb @ fc_w1 / np.float32(np.sqrt(10.0))) * np.float32(SILU_NORM)
        msg_rad = h @ fc_w2 / np.float32(np.sqrt(64.0))
        messages = msg_ang * msg_rad
        agg = jax.ops.segment_sum(messages, edge_dst, num_segments=node_in.shape[0])
        return agg / np.float32(np.sqrt(NUM_NEIGHBORS))

    def _L1_gnn_ref(h, W, a, src, dst):
        import jax, jax.numpy as jnp
        import numpy as np
        ALPHA = 0.2
        N_NODES, N_EDGES, N_FEAT, N_HID, N_HEADS = (50000, 25000, 256, 32, 8)
        N = h.shape[0]
        H, _, D = W.shape
        Wh = jnp.einsum('nf,hfd->hnd', h, W)
        a1, a2 = (a[:, :D], a[:, D:])
        s1 = jnp.einsum('hnd,hd->hn', Wh, a1)
        s2 = jnp.einsum('hnd,hd->hn', Wh, a2)
        e = jax.nn.leaky_relu(s1[:, src] + s2[:, dst], ALPHA)
        seg_max = jax.vmap(lambda x: jax.ops.segment_max(x, dst, num_segments=N))(e)
        ex = jnp.exp(e - seg_max[:, dst])
        denom = jax.vmap(lambda x: jax.ops.segment_sum(x, dst, num_segments=N))(ex)
        attn = ex / denom[:, dst]
        msg = attn[:, :, None] * Wh[:, src]
        out = jax.vmap(lambda m: jax.ops.segment_sum(m, dst, num_segments=N))(msg)
        return jnp.transpose(out, (1, 0, 2)).reshape(N, H * D)
    h = jnp.maximum(_layernorm(x, axis=-1), 0.0)
    x = x + _L0_gnn_ref(h, edge_attr_4, edge_attr_10, L0_gnn_w_00_0, L0_gnn_w_11_0, L0_gnn_w_01_1, L0_gnn_w_10_1, L0_gnn_fc_w1, L0_gnn_fc_w2, src, dst)
    h = jnp.maximum(_layernorm(x, axis=-1), 0.0)
    x = x + _L1_gnn_ref(h, L1_gnn_W, L1_gnn_a, src, dst)
    return x

_drawn_inputs = setup_inputs


def setup_inputs(seed=0):
    import zlib

    import numpy as np

    out = dict(_drawn_inputs(seed))
    spreads = {}
    factors = {'L1_gnn_a': 8.0}
    for name, (base, spread) in spreads.items():
        noise = np.random.default_rng([zlib.crc32(name.encode()), seed]).standard_normal(out[name].shape)
        drawn = base * np.exp(spread * noise) if base else spread * noise
        out[name] = jnp.asarray(drawn.astype(out[name].dtype))
    for name, factor in factors.items():
        out[name] = (out[name] * factor).astype(out[name].dtype)
    return out
```

```python
from contextlib import ExitStack

import numpy as np

import concourse.bass as bass
from concourse import mybir

P = 128
NODES, EDGES, FEAT = 50000, 25000, 256
MUL = 64
HEADS, HID = 8, 32
HIDDEN = 64
TILES = -(-EDGES // P)
EPAD = TILES * P
G = 4
NG = TILES // G
HALF = TILES // 2
GE = G * P
FW = FEAT + HEADS
PAD_NODE = NODES
DUMMY = NODES + 1
DUMMY_TILES = 4 * G
OUT_ROWS = DUMMY + DUMMY_TILES * P
SKIP = NODES + 10000
BIG = 1.0e30
EPS = 1e-5
SLOPE = 0.2
LEN_IN = 10
STEPS = 8
RECORD = 2 + 4 + LEN_IN
COPY_ROWS = 1024
COPY_LAST = NODES - (NG - 1) * COPY_ROWS
COPY_RUN = 16
assert TILES % G == 0 and TILES % 2 == 0 and COPY_LAST % COPY_RUN == 0 and 0 < COPY_LAST <= COPY_ROWS

W_SCALE = float(1.0 / np.sqrt(2.0 * MUL) * 1.679177 / np.sqrt(64.0) / np.sqrt(16.0))
W_SCALE_11 = float(W_SCALE / np.sqrt(3.0))
RADIAL_SCALE = float(1.0 / np.sqrt(10.0))

ALU = mybir.AluOpType
ACT = mybir.ActivationFunctionType
AX_X = mybir.AxisListType.X
F32 = mybir.dt.float32
I32 = mybir.dt.int32

SRC, LAST_ROW, FIRST_ROW, DST, END, START, FROM_PREV, FROM_NEXT = range(8)


def wait_past(eng, sem, value):
    if not isinstance(value, int) or value > 0:
        eng.wait_ge(sem, value)


def wait_apart(eng, ticks, sem, value):
    if not isinstance(value, int) or value > 0:
        eng.wait_ge(sem, value)
        eng.sem_inc(ticks)


def for_groups(eng, depth, body):
    end = (NG - 2) // depth * depth
    for g in range(depth):
        body(g, g, 0)
    with eng.Fori(1, end // depth) as n:
        for slot in range(depth):
            body(n * depth + slot, slot, n)
    for g in range(end, NG):
        body(g, g % depth, g // depth)


def after(slot, n, depth, by=1):
    return (slot + by) % depth, n + (slot + by) // depth


def there(g):
    return not isinstance(g, int) or g < NG


def over_heads(ap, g=G):
    return ap.unsqueeze(3).broadcast_to([P, g, HEADS, HID])


def tiles_of(g):
    return bass.ds(g * G, G)


def edges_of(g):
    return bass.ds(g * GE, GE)


class Shared:
    pass


def order_edges(nc, io):
    PARTS = 4
    PART = EPAD // PARTS
    with ExitStack() as ctx:
        sb = lambda name, shape, dt=F32: ctx.enter_context(nc.sbuf_tensor(f"order_{name}", shape, dt))
        sem = lambda name: ctx.enter_context(nc.semaphore(f"order_{name}"))
        seen = sb("seen", [HALF, 2, 2, P], I32)
        seen_f = sb("seen_f", [HALF, 2, 2, P])
        falls = sb("falls", [HALF, 2 * P])
        fell = sb("fell", [HALF, 1])
        ones = sb("ones", [HALF, 1])
        unsorted = sb("unsorted", [1, 1], I32)
        part_i = sb("part_i", [P, PART], I32)
        compared = sb("compared", [P, PART])
        twice = sb("twice", [P, EPAD])
        own_i = sb("own_i", [P, TILES], I32)
        own = sb("own", [P, TILES])
        lower = sb("lower", [P, P])
        counts = sb("counts", [P, PARTS + 1])
        rank_f = sb("rank_f", [P, 1])
        rank = sb("rank", [P, 1], I32)
        record = sb("record", [P, RECORD], I32)
        seen_in = sem("seen_in")
        checked = sem("checked")
        counted = sem("counted")
        flag_set = sem("flag_set")
        part_in = sem("part_in")
        part_used = sem("part_used")
        own_in = sem("own_in")
        lower_made = sem("lower_made")
        record_in = sem("record_in")
        dve_step = sem("dve_step")
        ranked = sem("ranked")
        sent = sem("sent")
        table_full = sem("table_full")
        working = sem("working")
        ticks = sem("ticks")
        ctx.enter_context(nc.allow_non_contiguous_dma(reason="single columns of the records, where edges are unsorted"))
        block = ctx.enter_context(nc.Block())

        def is_unsorted(eng):
            eng.wait_ge(flag_set, 1)
            return eng.value_load(unsorted[0:1, 0:1]) > 0

        @block.sync
        def _(sp):
            for k in range(2):
                sp.dma_start(seen[:, k], io.dst[k:k + EPAD].rearrange("(h q p) -> q h p", h=2, p=P)).then_inc(seen_in, 16)
            with sp.If(is_unsorted(sp)):
                for c in range(PARTS):
                    if c:
                        sp.wait_ge(part_used, c)
                    sp.dma_start(part_i[:], io.dst[1 + c * PART:1 + (c + 1) * PART].partition_broadcast(P)).then_inc(part_in, 16)
                sp.dma_start(own_i[:], io.dst[1:1 + EPAD].rearrange("(t p) -> p t", p=P)).then_inc(own_in, 16)
                with sp.Fori(0, TILES) as t:
                    edges = bass.ds(t * P, P)
                    later = bass.ds(t * P + 1, P)
                    sp.dma_start(record[:, 0:1], io.src[edges].unsqueeze(1)).then_inc(record_in, 16)
                    sp.dma_start(record[:, 1:2], io.dst[later].unsqueeze(1)).then_inc(record_in, 16)
                    sp.dma_start(record[:, 2:6].bitcast(F32), io.attr_rows[edges]).then_inc(record_in, 16)
                    sp.dma_start(record[:, 6:RECORD].bitcast(F32), io.lens_rows[edges]).then_inc(record_in, 16)
                    wait_apart(sp, ticks, sent, t * 16 + 16)
                sp.wait_ge(table_full, 1)
                whole = io.table.bitcast(F32)
                sp.dma_start(io.src_w, io.table[:, 0]).then_inc(working, 16)
                sp.dma_start(io.dst_w[1:1 + EPAD], io.table[:, 1]).then_inc(working, 16)
                sp.dma_start(io.attr_w, whole[:, 2:6].rearrange("(t p) c -> p t c", p=P)).then_inc(working, 16)
                for c in range(LEN_IN):
                    sp.dma_start(io.lens_w[c], whole[:, 6 + c]).then_inc(working, 16)
                for at in (0, EPAD + 1):
                    sp.dma_start(io.dst_w[at:at + 1], io.dst[at:at + 1]).then_inc(working, 16)
                sp.wait_ge(working, 16 * (5 + LEN_IN))
            with sp.Else():
                sp.dma_start(io.src_w, io.src).then_inc(working, 16)
                sp.dma_start(io.dst_w, io.dst).then_inc(working, 16)
                sp.dma_start(io.attr_w, io.attr).then_inc(working, 16)
                sp.dma_start(io.lens_w, io.lens).then_inc(working, 16)
                sp.wait_ge(working, 64)

        @block.gpsimd
        def _(pool):
            pool.memset(ones[:], 1.0).then_inc(lower_made, 1)
            pool.memset(lower[:], 1.0).then_inc(lower_made, 1)
            pool.wait_ge(lower_made, 2)
            pool.affine_select(out=lower[:], in_=lower[:], compare_op=ALU.is_gt, fill=0.0, base=0,
                               pattern=[[-1, P]], channel_multiplier=1).then_inc(lower_made, 1)
            with pool.If(is_unsorted(pool)):
                with pool.Fori(0, TILES) as t:
                    wait_apart(pool, ticks, record_in, t * 64 + 64)
                    wait_apart(pool, ticks, ranked, t + 1)
                    pool.indirect_dma_start(io.table, bass.IndirectOffsetOnAxis(ap=rank[:], axis=0), record[:], None,
                                            bounds_check=EPAD - 1, oob_is_err=True).then_inc(sent, 16)
                pool.wait_ge(sent, 16 * TILES)
                pool.sem_inc(table_full)
            with pool.Else():
                pool.sem_inc(ticks)

        @block.tensor
        def _(pe):
            pe.wait_ge(lower_made, 1)
            pe.wait_ge(checked, 1)
            pe.matmul(io.psum[0:1, 0, 0:1], fell[:], ones[:], start=True, stop=True).then_inc(counted, 1)

        @block.vector
        def _(dve):
            steps = [0]

            def chain(ins):
                steps[0] += 1
                ins.then_inc(dve_step, 1)
                dve.wait_ge(dve_step, steps[0])

            dve.wait_ge(seen_in, 32)
            chain(dve.tensor_copy(seen_f[:], seen[:]))
            chain(dve.tensor_tensor(falls[:].rearrange("q (h p) -> q h p", h=2), seen_f[:, 1], seen_f[:, 0], ALU.is_lt))
            dve.tensor_reduce(fell[:], falls[:], AX_X, ALU.add).then_inc(checked, 1)
            dve.wait_ge(counted, 1)
            dve.tensor_copy(unsorted[:], io.psum[0:1, 0, 0:1]).then_inc(flag_set, 1)
            with dve.If(is_unsorted(dve)):
                for c in range(PARTS):
                    dve.wait_ge(part_in, 16 * (c + 1))
                    dve.tensor_scalar(twice[:, c * PART:(c + 1) * PART], part_i[:], 2.0, None, ALU.mult).then_inc(part_used, 1)
                dve.wait_ge(own_in, 16)
                dve.tensor_scalar(own[:], own_i[:], 2.0, None, ALU.mult).then_inc(part_used, 1)
                dve.wait_ge(part_used, PARTS + 1)
                dve.wait_ge(lower_made, 3)
                with dve.Fori(0, TILES) as t:
                    mine = own[:, bass.ds(t, 1)]
                    tile = twice[:, bass.ds(t * P, P)]
                    for c in range(PARTS):
                        dve.tensor_scalar(compared[:], twice[:, c * PART:(c + 1) * PART], mine, 0.0, ALU.is_lt, ALU.add,
                                          accum_out=counts[:, c:c + 1]).then_inc(dve_step, 1)
                        wait_apart(dve, ticks, dve_step, t * STEPS + 3 + c)
                    dve.scalar_tensor_tensor(compared[:, 0:P], tile, mine, lower[:], ALU.is_equal, ALU.mult).then_inc(dve_step, 1)
                    wait_apart(dve, ticks, dve_step, t * STEPS + 3 + PARTS)
                    dve.tensor_reduce(counts[:, PARTS:PARTS + 1], compared[:, 0:P], AX_X, ALU.add).then_inc(dve_step, 1)
                    wait_apart(dve, ticks, dve_step, t * STEPS + 4 + PARTS)
                    dve.tensor_reduce(rank_f[:], counts[:], AX_X, ALU.add).then_inc(dve_step, 1)
                    wait_apart(dve, ticks, dve_step, t * STEPS + 5 + PARTS)
                    dve.tensor_scalar(tile, tile, -1.0, None, ALU.add).then_inc(dve_step, 1)
                    wait_apart(dve, ticks, dve_step, t * STEPS + 6 + PARTS)
                    dve.tensor_copy(rank[:], rank_f[:]).then_inc(ranked, 1)
                    wait_apart(dve, ticks, sent, t * 16 + 16)
            with dve.Else():
                dve.sem_inc(ticks)


def prepare(nc, io, sh):
    with ExitStack() as ctx:
        sb = lambda name, shape, dt=F32: ctx.enter_context(nc.sbuf_tensor(f"prepare_{name}", shape, dt))
        sem = lambda name: ctx.enter_context(nc.semaphore(f"prepare_{name}"))
        raw_place = sb("raw_place", [HALF, 2, P], I32)
        raw = sb("raw", [HALF, 4, 2, P], I32)
        own = sb("own", [HALF, 2, P])
        prv = sb("prv", [HALF, 2, P])
        nxt = sb("nxt", [HALF, 2, P])
        is_first = sb("is_first", [HALF, 2, P])
        is_last = sb("is_last", [HALF, 2, P])
        first_mask = sb("first_mask", [HALF, 2, P])
        last_mask = sb("last_mask", [HALF, 2, P])
        place = sb("place", [HALF, 2, P])
        dummy_i = sb("dummy_i", [HALF, 2, P], I32)
        dummy = sb("dummy", [HALF, 2, P])
        work = sb("work", [HALF, 2, P])
        ends = sb("ends", [HALF, 2, P])
        starts = sb("starts", [HALF, 2, P])
        cols = sb("cols", [HALF, 8, 2, P])
        one = sb("one", [HALF, 2, 1])
        a_all = sb("a_all", [P, HEADS, 2 * HID])
        wprod = sb("wprod", [P, HEADS, HID])
        attr = sb("attr", [P, TILES, 4])
        fc1 = sb("fc1", [LEN_IN, HIDDEN])
        fc2 = sb("fc2", [HIDDEN, 1])
        lens = sb("lens", [LEN_IN, 4, GE])
        hidden = sb("hidden", [HIDDEN, 2, GE])
        zeros = sb("zeros", [P, FEAT])

        edges_in = sem("edges_in")
        weights_in = sem("weights_in")
        lens_in = [sem(f"lens_in{s}") for s in range(4)]
        copied = sem("copied")
        masks_out = sem("masks_out")
        made = sem("made")
        dve_step = sem("dve_step")
        masks_made = sem("masks_made")
        cols_made = sem("cols_made")
        cols_turned = sem("cols_turned")
        hidden_in = sem("hidden_in")
        hidden_done = sem("hidden_done")
        factor_in = sem("factor_in")
        factor_used = sem("factor_used")
        block = ctx.enter_context(nc.Block())
        ps = sh.psum

        @block.sync
        def _(sp):
            for k, shift in enumerate((None, 0, 1, 2)):
                flat = io.src_w if shift is None else io.dst_w[shift:shift + EPAD]
                sp.dma_start(raw[:, k], flat.rearrange("(h q p) -> q h p", h=2, p=P)).then_inc(edges_in, 16)
            sp.dma_start(dummy_i[:], io.spare_rows).then_inc(edges_in, 16)
            sp.dma_start(fc1[:], io.fc_w1).then_inc(weights_in, 16)
            sp.dma_start(fc2[:], io.fc_w2).then_inc(weights_in, 16)
            sp.dma_start(sh.w_a[:], io.w_a).then_inc(weights_in, 16)
            sp.dma_start(sh.w_b[:], io.w_b).then_inc(weights_in, 16)
            sp.dma_start(sh.w_c[:, :, 0:FEAT], io.w_c.rearrange("(c p) n -> p c n", p=P)).then_inc(weights_in, 16)
            sp.dma_start(a_all[:], io.a.partition_broadcast(P)).then_inc(weights_in, 16)
            sp.dma_start(attr[:], io.attr_w).then_inc(weights_in, 16)

            def load(g, slot):
                wait_past(sp, hidden_in, g - 3)
                sp.dma_start(lens[:, slot], io.lens_w[:, edges_of(g)]).then_inc(lens_in[slot], 16)

            def group(g, slot, n):
                if there(g + 3):
                    load(g + 3, (slot + 3) % 4)
                rows = bass.ds(g * COPY_ROWS, COPY_LAST if isinstance(g, int) and g == NG - 1 else COPY_ROWS)
                sp.dma_start(io.nodes[rows].rearrange("(a b) c -> a (b c)", b=COPY_RUN),
                             io.x[rows].rearrange("(a b) c -> a (b c)", b=COPY_RUN)).then_inc(copied, 16)
            for g in range(3):
                load(g, g)
            for_groups(sp, 4, group)
            sp.wait_ge(masks_made, 2)
            sp.dma_start(io.first_mask.rearrange("(h q p) -> q h p", h=2, p=P), first_mask[:]).then_inc(masks_out, 16)
            sp.dma_start(io.last_mask.rearrange("(h q p) -> q h p", h=2, p=P), last_mask[:]).then_inc(masks_out, 16)
            sp.wait_ge(made, 3)
            sp.dma_start(io.nodes[PAD_NODE:DUMMY], zeros[0:1]).then_inc(copied, 16)
            sp.dma_start(io.nodes[DUMMY:OUT_ROWS].rearrange("(a p) c -> p a c", p=P),
                         zeros[:].unsqueeze(1).broadcast_to([P, DUMMY_TILES, FEAT])).then_inc(copied, 16)
            sp.wait_ge(copied, 16 * (NG + 2))
            sp.wait_ge(masks_out, 32)

        @block.gpsimd
        def _(pool):
            pool.iota(sh.iota_i[:], [[1, P]], base=0, channel_multiplier=0).then_inc(made, 1)
            pool.iota(raw_place[:], [[0, 2], [1, P]], base=0, channel_multiplier=0).then_inc(made, 1)
            pool.memset(zeros[:], 0.0).then_inc(made, 1)
            pool.memset(sh.ident[:], 0.0).then_inc(made, 1)
            pool.memset(sh.minus_half[:], -0.5).then_inc(made, 1)
            pool.wait_ge(made, 4)
            pool.affine_select(out=sh.ident[:], in_=sh.ident[:], compare_op=ALU.not_equal, fill=1.0, base=0,
                               pattern=[[-1, P]], channel_multiplier=1).then_inc(made, 1)

        @block.vector
        def _(dve):
            steps = [0]

            def chain(ins):
                steps[0] += 1
                ins.then_inc(dve_step, 1)
                dve.wait_ge(dve_step, steps[0])

            dve.wait_ge(made, 5)
            dve.tensor_copy(sh.iota[:], sh.iota_i[:]).then_inc(dve_step, 1)
            dve.tensor_copy(place[:], raw_place[:]).then_inc(dve_step, 1)
            steps[0] += 2
            dve.wait_ge(edges_in, 80)
            dve.tensor_copy(cols[:, SRC], raw[:, 0]).then_inc(dve_step, 1)
            dve.tensor_copy(prv[:], raw[:, 1]).then_inc(dve_step, 1)
            dve.tensor_copy(own[:], raw[:, 2]).then_inc(dve_step, 1)
            steps[0] += 3
            chain(dve.tensor_copy(nxt[:], raw[:, 3]))
            dve.tensor_tensor(is_first[:], own[:], prv[:], ALU.not_equal).then_inc(dve_step, 1)
            dve.tensor_scalar(cols[:, DST], own[:], float(NODES - 1), None, ALU.min).then_inc(dve_step, 1)
            dve.tensor_copy(dummy[:], dummy_i[:]).then_inc(dve_step, 1)
            steps[0] += 3
            chain(dve.tensor_tensor(is_last[:], own[:], nxt[:], ALU.not_equal))
            dve.tensor_scalar(first_mask[:], is_first[:], -BIG, None, ALU.mult).then_inc(masks_made, 1)
            dve.tensor_scalar(last_mask[:], is_last[:], -BIG, None, ALU.mult).then_inc(masks_made, 1)
            chain(dve.tensor_tensor(work[:], own[:], dummy[:], ALU.subtract))
            chain(dve.tensor_tensor(work[:], work[:], is_last[:], ALU.mult))
            chain(dve.tensor_tensor(cols[:, LAST_ROW], work[:], dummy[:], ALU.add))
            chain(dve.scalar_tensor_tensor(work[:], own[:], float(-SKIP), is_first[:], ALU.add, ALU.mult))
            chain(dve.tensor_scalar(cols[:, FIRST_ROW], work[:], float(SKIP), None, ALU.add))
            chain(dve.tensor_scalar(work[:], is_last[:], -999.0, 999.0, ALU.mult, ALU.add))
            chain(dve.tensor_tensor(work[:], work[:], place[:], ALU.add))
            chain(dve.memset(work[:, :, P - 1:P], float(P - 1)))
            for h in range(2):
                chain(dve.tensor_tensor_scan(ends[:, h, ::-1], work[:, h, ::-1], work[:, h, ::-1], 999.0, ALU.min, ALU.min))
            chain(dve.scalar_tensor_tensor(work[:], place[:], 1.0, is_first[:], ALU.add, ALU.mult))
            chain(dve.memset(work[:, :, 0:1], 1.0))
            for h in range(2):
                chain(dve.tensor_tensor_scan(starts[:, h, :], work[:, h, :], work[:, h, :], 0.0, ALU.max, ALU.max))
            chain(dve.tensor_scalar(starts[:], starts[:], -1.0, None, ALU.add))
            chain(dve.tensor_copy(cols[:, END], ends[:]))
            chain(dve.tensor_copy(cols[:, START], starts[:]))
            for col, flag, near, into, at in ((FROM_PREV, is_first, 0, ends, P - 1), (FROM_NEXT, is_last, P - 1, starts, 0)):
                chain(dve.memset(cols[:, col], -1.0))
                chain(dve.tensor_scalar(one[:], flag[:, :, near:near + 1], -1.0, 1.0, ALU.mult, ALU.add))
                chain(dve.scalar_tensor_tensor(one[:], into[:, :, near:near + 1], 1.0, one[:], ALU.add, ALU.mult))
                chain(dve.tensor_scalar(cols[:, col, :, at:at + 1], one[:], -1.0, None, ALU.add))
            dve.tensor_copy(one[:], one[:]).then_inc(cols_made, 1)

            dve.wait_ge(weights_in, 112)
            chain(dve.tensor_scalar(sh.w_a[0:MUL], sh.w_a[0:MUL], W_SCALE, None, ALU.mult))
            chain(dve.tensor_scalar(sh.w_a[MUL:P], sh.w_a[MUL:P], W_SCALE_11, None, ALU.mult))
            chain(dve.tensor_scalar(sh.w_b[:], sh.w_b[:], W_SCALE, None, ALU.mult))
            for c in range(2):
                wc = sh.w_c[:, c, 0:FEAT].rearrange("p (h d) -> p h d", h=HEADS)
                for k, out in ((0, sh.w_c[:, c, FEAT:FW]), (1, sh.w_dst[:, c])):
                    chain(dve.tensor_tensor(wprod[:], wc, a_all[:, :, k * HID:(k + 1) * HID], ALU.mult))
                    chain(dve.tensor_reduce(out, wprod[:], AX_X, ALU.add))

            for half in range(4):
                dve.wait_ge(cols_turned, half + 1)
                for k in (2 * half, 2 * half + 1):
                    at = k % 2 * TILES
                    dve.tensor_copy(sh.index[k][:], ps[:, half, at:at + TILES])

            def group(g, slot, n):
                dve.wait_ge(factor_in, g + 1)
                dve.tensor_tensor(sh.coef[:, tiles_of(g), :], attr[:, tiles_of(g), :],
                                  ps[:, 6 + slot % 2, 0:G].unsqueeze(2).broadcast_to([P, G, 4]), ALU.mult).then_inc(factor_used, 1)
            for_groups(dve, 4, group)

        @block.tensor
        def _(pe):
            pe.wait_ge(made, 6)
            pe.wait_ge(cols_made, 1)
            for k in range(8):
                for h in range(2):
                    at = (k % 2 * 2 + h) * HALF
                    last = pe.transpose(ps[:, k // 2, at:at + HALF], cols[:, k, h], sh.ident[0:HALF, 0:HALF])
                if k % 2:
                    last.then_inc(cols_turned, 1)
            pe.wait_ge(weights_in, 112)

            def hid(g, slot, n):
                pe.wait_ge(lens_in[slot], n * 16 + 16)
                wait_past(pe, hidden_done, g - 1)
                pe.matmul(ps[0:HIDDEN, 4 + slot % 2, :], fc1[:], lens[:, slot], start=True, stop=True).then_inc(hidden_in, 1)

            def group(g, slot, n):
                if there(g + 1):
                    hid(g + 1, *after(slot, n, 4))
                pe.wait_ge(hidden_done, g + 1)
                wait_past(pe, factor_used, g - 1)
                for u in range(G):
                    last = pe.matmul(ps[:, 6 + slot % 2, u:u + 1], hidden[:, slot % 2, u * P:(u + 1) * P], fc2[:],
                                     start=True, stop=True)
                last.then_inc(factor_in, 1)
            hid(0, 0, 0)
            for_groups(pe, 4, group)

        @block.scalar
        def _(act):
            def group(g, slot, n):
                act.wait_ge(hidden_in, g + 1)
                wait_past(act, factor_in, g - 1)
                act.activation(hidden[:, slot % 2], ps[0:HIDDEN, 4 + slot % 2, :], ACT.Silu, scale=RADIAL_SCALE).then_inc(hidden_done, 1)
            for_groups(act, 4, group)


def start_stats(ctx, nc, depth, phase):
    ln = Shared()
    ln.depth = depth
    sb = lambda name, shape, dt=F32: ctx.enter_context(nc.sbuf_tensor(f"{phase}_{name}", shape, dt))
    sem = lambda name: ctx.enter_context(nc.semaphore(f"{phase}_{name}"))
    ln.rows = sb("rows", [P, depth, G, FEAT])
    ln.parts = sb("parts", [P, depth, G, 6])
    ln.mean_var = sb("mean_var", [P, depth, G, 2])
    ln.spare = sb("spare", [P, 1])
    ln.var_eps = sb("var_eps", [P, depth, G])
    ln.rstd = sb("rstd", [P, depth, G])
    ln.rows_in = [sem(f"rows_in{s}") for s in range(depth)]
    ln.parts_done = sem("parts_done")
    ln.mean_done = sem("mean_done")
    ln.var_ready = sem("var_ready")
    ln.rstd_ready = sem("rstd_ready")
    ln.relu_done = sem("relu_done")
    ln.bound = None
    return ln


def norm_relu(dve, ln, out, j, slot, n):
    dve.wait_ge(ln.rows_in[slot], n * 16 * G + 16 * G)
    for u in range(G):
        last = dve.bn_stats(ln.parts[:, slot, u], ln.rows[:, slot, u])
    last.then_inc(ln.parts_done, 1)
    dve.wait_ge(ln.parts_done, j + 1)
    dve.memset(ln.spare[:], 0.0)
    for u in range(G):
        last = dve.bn_aggr(ln.mean_var[:, slot, u], ln.parts[:, slot, u])
    last.then_inc(ln.mean_done, 1)
    dve.wait_ge(ln.mean_done, j + 1)
    wait_past(dve, ln.rstd_ready, j - ln.depth + 1)
    dve.tensor_scalar(ln.var_eps[:, slot], ln.mean_var[:, slot, :, 1], EPS, None, ALU.add).then_inc(ln.var_ready, 1)
    for u in range(G):
        last = dve.tensor_scalar(out[:, slot, u], ln.rows[:, slot, u], ln.mean_var[:, slot, u, 0:1], 0.0,
                                 ALU.subtract, ALU.max)
    last.then_inc(ln.relu_done, 1)


def gather_rows(pool, ln, table, index_slot, slot, tiles=range(G)):
    for u in tiles:
        pool.indirect_dma_start(ln.rows[:, slot, u], None, table,
                                bass.IndirectOffsetOnAxis(ap=index_slot[:, u:u + 1], axis=0),
                                bounds_check=ln.bound, oob_is_err=False).then_inc(ln.rows_in[slot], 16)


def inverse_std(pool, ln, sh, ticks, j, slot):
    wait_apart(pool, ticks, ln.var_ready, j + 1)
    pool.tensor_tensor(ln.rstd[:, slot], ln.var_eps[:, slot], sh.minus_half[:], ALU.pow).then_inc(ln.rstd_ready, 1)


def layer0(nc, io, sh):
    D = 4
    UW = 4 * P
    with ExitStack() as ctx:
        sb = lambda name, shape, dt=F32: ctx.enter_context(nc.sbuf_tensor(f"layer0_{name}", shape, dt))
        sem = lambda name: ctx.enter_context(nc.semaphore(f"layer0_{name}"))
        ln = start_stats(ctx, nc, D, "layer0")
        src_slot = sb("src_slot", [P, D, G], I32)
        dst_slot = sb("dst_slot", [P, D, G], I32)
        scaled = sb("scaled", [P, 2, G, 4])
        by_part = sb("by_part", [P, G, MUL, 3])
        prod = sb("prod", [P, 2, G, UW])
        sel = sb("sel", [P, 2, 2, G, P])
        summed = sb("summed", [P, 2, UW])
        msg = sb("msg", [P, D, G, FEAT])
        src_copied = sem("src_copied")
        dst_copied = sem("dst_copied")
        scattered = [sem(f"scattered{s}") for s in range(D)]
        scaled_done = sem("scaled_done")
        parts_made = sem("parts_made")
        zeroed = sem("zeroed")
        prod_ready = sem("prod_ready")
        sum_done = sem("sum_done")
        sum_out = sem("sum_out")
        msg_done = sem("msg_done")
        msg_out = sem("msg_out")
        ticks = sem("ticks")
        block = ctx.enter_context(nc.Block())
        ps = sh.psum
        acc = [ps[:, q] for q in range(2)]

        @block.gpsimd
        def _(pool):
            ln.bound = pool.to_reg(NODES - 1)
            out_bound = pool.to_reg(OUT_ROWS - 1)

            def take_sources(g, slot):
                wait_apart(pool, ticks, prod_ready, g - D + 1)
                pool.tensor_copy(src_slot[:, slot], sh.index[SRC][:, tiles_of(g)]).then_inc(src_copied, 1)
                wait_apart(pool, ticks, src_copied, g + 1)

            def group(g, slot, n):
                if there(g + 3):
                    take_sources(g + 3, (slot + 3) % D)
                wait_apart(pool, ticks, scattered[slot], n * 16 * G)
                pool.tensor_copy(dst_slot[:, slot], sh.index[LAST_ROW][:, tiles_of(g)]).then_inc(dst_copied, 1)
                wait_apart(pool, ticks, dst_copied, g + 1)
                for u in range(G):
                    if there(g + 3):
                        gather_rows(pool, ln, io.x, src_slot[:, (slot + 3) % D], (slot + 3) % D, (u,))
                    wait_apart(pool, ticks, msg_out, g * G + u + 1)
                    pool.indirect_dma_start(io.nodes, bass.IndirectOffsetOnAxis(ap=dst_slot[:, slot, u:u + 1], axis=0),
                                            msg[:, slot, u], None, bounds_check=out_bound,
                                            compute_op=ALU.add).then_inc(scattered[slot], 16)
                    if u == 1 and there(g + 2):
                        inverse_std(pool, ln, sh, ticks, g + 2, (slot + 2) % D)
            pool.memset(msg[:, D - 1, G - 1], 0.0).then_inc(zeroed, 1)
            for g in range(3):
                take_sources(g, g)
                gather_rows(pool, ln, io.x, src_slot[:, g], g)
            for g in range(2):
                inverse_std(pool, ln, sh, ticks, g, g)
            for_groups(pool, D, group)
            for slot in range(D):
                pool.wait_ge(scattered[slot], 16 * G * len(range(slot, NG, D)))

        @block.vector
        def _(dve):
            def products(g, slot, q):
                dve.wait_ge(ln.relu_done, g + 1)
                wait_past(dve, msg_done, (g - 1) * G)
                dve.wait_ge(ln.rstd_ready, g + 1)
                dve.tensor_tensor(scaled[:, q], sh.coef[:, tiles_of(g)],
                                  ln.rstd[:, slot].unsqueeze(2).broadcast_to([P, G, 4]), ALU.mult).then_inc(scaled_done, 1)
                for k, col in enumerate((END, FROM_PREV)):
                    dve.tensor_tensor(sel[:, q, k], sh.iota[:].unsqueeze(1).broadcast_to([P, G, P]),
                                      sh.index[col][:, tiles_of(g)].unsqueeze(2).broadcast_to([P, G, P]), ALU.is_equal)
                dve.wait_ge(scaled_done, g + 1)
                s0 = ln.rows[:, slot, :, 0:MUL]
                s1 = ln.rows[:, slot, :, MUL:FEAT].rearrange("p g (i m) -> p g i m", m=3)
                c0 = scaled[:, q, :, 0:1]
                c1 = scaled[:, q, :, 1:4]
                out = prod[:, q]
                mixed = out[:, :, P:UW].rearrange("p g (m k i) -> p g m k i", m=3, k=2)
                dve.tensor_tensor(by_part[:], s1, c1.unsqueeze(2).broadcast_to([P, G, MUL, 3]), ALU.mult).then_inc(parts_made, 1)
                dve.tensor_tensor(out[:, :, 0:MUL], s0, c0.broadcast_to([P, G, MUL]), ALU.mult)
                dve.tensor_tensor(mixed[:, :, :, 0], s0.unsqueeze(2).broadcast_to([P, G, 3, MUL]),
                                  c1.unsqueeze(3).broadcast_to([P, G, 3, MUL]), ALU.mult)
                dve.tensor_tensor(mixed[:, :, :, 1], s1.rearrange("p g i m -> p g m i"),
                                  c0.unsqueeze(3).broadcast_to([P, G, 3, MUL]), ALU.mult)
                dve.wait_ge(parts_made, g + 1)
                dve.tensor_reduce(out[:, :, MUL:P], by_part[:], AX_X, ALU.add).then_inc(prod_ready, 1)

            def group(g, slot, n):
                if there(g + 1):
                    norm_relu(dve, ln, ln.rows, g + 1, *after(slot, n, D))
                products(g, slot, slot % 2)
            norm_relu(dve, ln, ln.rows, 0, 0, 0)
            for_groups(dve, D, group)

        @block.tensor
        def _(pe):
            def sum_runs(g, q, u):
                k = g * G + u
                if u == 0:
                    pe.wait_ge(prod_ready, g + 1)
                wait_past(pe, sum_out, k - 1)
                for c in range(UW // P):
                    last = pe.matmul(acc[u % 2][:, c * P:(c + 1) * P], prod[:, q, u, c * P:(c + 1) * P],
                                     sel[:, q, 0, u], start=(c == 0), stop=True, skip_group_check=True)
                last.then_inc(sum_done, 1)

            def messages(g, slot, u):
                k = g * G + u
                out = ps[:, 4 + u % 2, 0:FEAT]
                vec = out[:, MUL:FEAT].rearrange("p (o m) -> p m o", m=3)
                part = lambda c: summed[:, u % 2, c * P:(c + 1) * P]
                pe.wait_ge(sum_out, k + 1)
                pe.matmul(out[:, 0:MUL], part(0), sh.w_a[:], start=True, stop=False, skip_group_check=True)
                for m in range(3):
                    pe.matmul(vec[:, m], part(1 + m), sh.w_b[:], start=False, stop=False, skip_group_check=True)
                if isinstance(k, int) and k == 0:
                    pe.wait_ge(zeroed, 1)
                else:
                    pe.wait_ge(msg_out, k)
                before = msg[:, slot, u - 1] if u else msg[:, (slot + D - 1) % D, G - 1]
                pe.matmul(out, sel[:, slot % 2, 1, u], before, start=False, stop=True,
                          skip_group_check=True).then_inc(msg_done, 1)

            def group(g, slot, n):
                for u in range(G):
                    if u < G - 1:
                        sum_runs(g, slot % 2, u + 1)
                    elif there(g + 1):
                        sum_runs(g + 1, (slot + 1) % 2, 0)
                    messages(g, slot, u)
            sum_runs(0, 0, 0)
            for_groups(pe, D, group)

        @block.scalar
        def _(act):
            def sums_out(g, u):
                k = g * G + u
                act.wait_ge(sum_done, k + 1)
                wait_past(act, msg_done, k - 1)
                act.activation(summed[:, u % 2], acc[u % 2], ACT.Copy).then_inc(sum_out, 1)

            def group(g, slot, n):
                for u in range(G):
                    if u < G - 1:
                        sums_out(g, u + 1)
                    elif there(g + 1):
                        sums_out(g + 1, 0)
                    if u == 0:
                        wait_past(act, scattered[slot], n * 16 * G)
                    act.wait_ge(msg_done, g * G + u + 1)
                    act.activation(msg[:, slot, u], ps[:, 4 + u % 2, 0:FEAT], ACT.Copy).then_inc(msg_out, 1)
            sums_out(0, 0)
            for_groups(act, D, group)


def project(nc, io, sh):
    D = 4
    with ExitStack() as ctx:
        sb = lambda name, shape, dt=F32: ctx.enter_context(nc.sbuf_tensor(f"project_{name}", shape, dt))
        sem = lambda name: ctx.enter_context(nc.semaphore(f"project_{name}"))
        ln = start_stats(ctx, nc, D, "project")
        src_slot = sb("src_slot", [P, D, G], I32)
        turned = sb("turned", [P, 2, 2 * P])
        wh = sb("wh", [P, D, G, FW])
        mask = sb("mask", [HEADS, D, GE])
        top = sb("top", [HEADS, D, GE])
        src_copied = sem("src_copied")
        mask_in = [sem(f"mask_in{s}") for s in range(D)]
        wh_stored = [sem(f"wh_stored{s}") for s in range(D)]
        top_stored = [sem(f"top_stored{s}") for s in range(D)]
        turn_done = sem("turn_done")
        turn_out = sem("turn_out")
        wh_done = sem("wh_done")
        wh_out = sem("wh_out")
        score_turned = sem("score_turned")
        top_done = sem("top_done")
        ticks = sem("ticks")
        block = ctx.enter_context(nc.Block())
        ps = sh.psum

        @block.sync
        def _(sp):
            def load_mask(g, slot):
                wait_apart(sp, ticks, top_done, g - D + 1)
                sp.dma_start(mask[:, slot], io.first_mask[edges_of(g)].partition_broadcast(HEADS)).then_inc(mask_in[slot], 16)

            def group(g, slot, n):
                if there(g + 2):
                    load_mask(g + 2, (slot + 2) % D)
                wait_apart(sp, ticks, wh_out, (g + 1) * G)
                sp.dma_start(io.wh[edges_of(g)].rearrange("(u p) f -> p u f", p=P), wh[:, slot]).then_inc(wh_stored[slot], 16)
                wait_apart(sp, ticks, top_done, g + 1)
                sp.dma_start(io.top[:, edges_of(g)], top[:, slot]).then_inc(top_stored[slot], 16)
            for g in range(2):
                load_mask(g, g)
            for_groups(sp, D, group)
            for slot in range(D):
                sp.wait_ge(wh_stored[slot], 16 * len(range(slot, NG, D)))
                sp.wait_ge(top_stored[slot], 16 * len(range(slot, NG, D)))

        @block.gpsimd
        def _(pool):
            ln.bound = pool.to_reg(NODES - 1)

            def gather(g, slot):
                wait_apart(pool, ticks, turn_done, (g - D + 1) * G)
                pool.tensor_copy(src_slot[:, slot], sh.index[SRC][:, tiles_of(g)]).then_inc(src_copied, 1)
                wait_apart(pool, ticks, src_copied, g + 1)
                gather_rows(pool, ln, io.nodes, src_slot[:, slot], slot)

            def group(g, slot, n):
                if there(g + 3):
                    gather(g + 3, (slot + 3) % D)
                if there(g + 2):
                    wait_apart(pool, ticks, wh_out, (g - 1) * G)
                    inverse_std(pool, ln, sh, ticks, g + 2, (slot + 2) % D)
            for g in range(3):
                gather(g, g)
            for g in range(2):
                inverse_std(pool, ln, sh, ticks, g, g)
            for_groups(pool, D, group)

        @block.vector
        def _(dve):
            def running_max(g, slot, n):
                dve.wait_ge(score_turned, (g + 1) * G)
                dve.wait_ge(mask_in[slot], n * 16 + 16)
                wait_past(dve, top_stored[slot], n * 16)
                if isinstance(g, int) and g == 0:
                    initial = -BIG
                else:
                    dve.wait_ge(top_done, g)
                    initial = top[:, (slot + D - 1) % D, GE - 1:GE]
                dve.tensor_tensor_scan(top[:, slot], mask[:, slot], ps[0:HEADS, 6 + slot % 2], initial,
                                       ALU.add, ALU.max).then_inc(top_done, 1)

            def group(g, slot, n):
                if there(g + 2):
                    norm_relu(dve, ln, ln.rows, g + 2, *after(slot, n, D, 2))
                if not isinstance(g, int) or g > 0:
                    running_max(g - 1, *after(slot, n - 1, D, D - 1))
            norm_relu(dve, ln, ln.rows, 0, 0, 0)
            norm_relu(dve, ln, ln.rows, 1, 1, 0)
            for_groups(dve, D, group)
            running_max(NG - 1, (NG - 1) % D, (NG - 1) // D)

        @block.tensor
        def _(pe):
            def turn(g, slot, u):
                if u == 0:
                    pe.wait_ge(ln.relu_done, g + 1)
                wait_past(pe, turn_out, g * G + u - 1)
                for c in range(2):
                    last = pe.transpose(ps[:, u % 2, c * P:(c + 1) * P], ln.rows[:, slot, u, c * P:(c + 1) * P], sh.ident[:])
                last.then_inc(turn_done, 1)

            def product(g, slot, u):
                k = g * G + u
                pe.wait_ge(turn_out, k + 1)
                wait_past(pe, wh_out, k - 1)
                for c in range(2):
                    last = pe.matmul(ps[:, 2 + u % 2, 0:FW], turned[:, u % 2, c * P:(c + 1) * P], sh.w_c[:, c],
                                     start=(c == 0), stop=(c == 1))
                last.then_inc(wh_done, 1)

            def turn_score(g, slot, u):
                if u == 0:
                    wait_past(pe, top_done, g - 1)
                pe.wait_ge(wh_out, g * G + u + 1)
                pe.transpose(ps[0:HEADS, 6 + slot % 2, u * P:(u + 1) * P], wh[:, slot, u, FEAT:FW],
                             sh.ident[:]).then_inc(score_turned, 1)

            def group(g, slot, n):
                for u in range(G):
                    if u < G - 1:
                        turn(g, slot, u + 1)
                    elif there(g + 1):
                        turn(g + 1, (slot + 1) % D, 0)
                    product(g, slot, u)
                    if u:
                        turn_score(g, slot, u - 1)
                    elif not isinstance(g, int) or g > 0:
                        turn_score(g - 1, (slot + D - 1) % D, G - 1)
            turn(0, 0, 0)
            for_groups(pe, D, group)
            turn_score(NG - 1, (NG - 1) % D, G - 1)

        @block.scalar
        def _(act):
            def rows_out(g, u):
                k = g * G + u
                act.wait_ge(turn_done, k + 1)
                wait_past(act, wh_done, k - 1)
                act.activation(turned[:, u % 2], ps[:, u % 2, 0:2 * P], ACT.Copy).then_inc(turn_out, 1)

            def group(g, slot, n):
                for u in range(G):
                    if u < G - 1:
                        rows_out(g, u + 1)
                    elif there(g + 1):
                        rows_out(g + 1, 0)
                    if u == 0:
                        act.wait_ge(ln.rstd_ready, g + 1)
                        wait_past(act, wh_stored[slot], n * 16)
                        wait_past(act, score_turned, (g - D + 1) * G)
                    act.wait_ge(wh_done, g * G + u + 1)
                    act.activation(wh[:, slot, u], ps[:, 2 + u % 2, 0:FW], ACT.Copy,
                                   scale=ln.rstd[:, slot, u:u + 1]).then_inc(wh_out, 1)
            rows_out(0, 0)
            for_groups(act, D, group)


def layer1(nc, io, sh):
    D = 3
    with ExitStack() as ctx:
        sb = lambda name, shape, dt=F32: ctx.enter_context(nc.sbuf_tensor(f"layer1_{name}", shape, dt))
        sem = lambda name: ctx.enter_context(nc.semaphore(f"layer1_{name}"))
        ln = start_stats(ctx, nc, D, "layer1")
        dst_slot = sb("dst_slot", [P, D, G], I32)
        out_slot = sb("out_slot", [P, D, G], I32)
        normed = sb("normed", [P, D, G, FEAT])
        turned = sb("turned", [P, 2, 2 * P])
        wh = sb("wh", [P, D, G, FW])
        mask = sb("mask", [HEADS, D, GE])
        top = sb("top", [HEADS, D, GE])
        run_top = sb("run_top", [HEADS, D, GE])
        sel = sb("sel", [P, D, 2, G, P])
        dst_score = sb("dst_score", [P, G, HEADS])
        logit = sb("logit", [P, G, 2 * HEADS])
        leaky = sb("leaky", [P, G, 2 * HEADS])
        below = sb("below", [P, D, G, HEADS])
        weighted = sb("weighted", [P, D, G, FW])
        total = sb("total", [P, D, G, FW])
        denom = sb("denom", [P, G, HEADS])
        inv = sb("inv", [P, G, HEADS])
        result = sb("result", [P, D, G, FEAT])
        dst_copied = sem("dst_copied")
        out_copied = sem("out_copied")
        wh_in = [sem(f"wh_in{s}") for s in range(D)]
        tops_in = [sem(f"tops_in{s}") for s in range(D)]
        scattered = [sem(f"scattered{s}") for s in range(D)]
        turn_done = sem("turn_done")
        turn_out = sem("turn_out")
        scored = sem("scored")
        top_done = sem("top_done")
        sel_ready = sem("sel_ready")
        score_step = sem("score_step")
        below_ready = sem("below_ready")
        exp_done = sem("exp_done")
        weighted_ready = sem("weighted_ready")
        zeroed = sem("zeroed")
        total_done = sem("total_done")
        total_out = sem("total_out")
        result_step = sem("result_step")
        result_ready = sem("result_ready")
        ticks = sem("ticks")
        block = ctx.enter_context(nc.Block())
        ps = sh.psum
        SCORE_BANK = (2, 3, 6)
        scores = [ps[:, b, 0:G * 2 * HEADS].rearrange("p (u k) -> p u k", u=G) for b in SCORE_BANK]

        group_of = lambda j: (NG - 1) - j

        @block.sync
        def _(sp):
            def load(j, slot):
                wait_apart(sp, ticks, weighted_ready, j - D + 1)
                edges = edges_of(group_of(j))
                sp.dma_start(mask[:, slot], io.last_mask[edges].partition_broadcast(HEADS)).then_inc(tops_in[slot], 16)
                sp.dma_start(top[:, slot], io.top[:, edges]).then_inc(tops_in[slot], 16)
                sp.dma_start(wh[:, slot], io.wh[edges].rearrange("(u p) f -> p u f", p=P)).then_inc(wh_in[slot], 16)

            def group(j, slot, n):
                if there(j + 2):
                    load(j + 2, (slot + 2) % D)
            load(0, 0)
            load(1, 1)
            for_groups(sp, D, group)

        @block.gpsimd
        def _(pool):
            ln.bound = pool.to_reg(NODES - 1)

            def gather(j, slot):
                wait_apart(pool, ticks, result_ready, j - D + 1)
                pool.tensor_copy(dst_slot[:, slot], sh.index[DST][:, tiles_of(group_of(j))]).then_inc(dst_copied, 1)
                wait_apart(pool, ticks, dst_copied, j + 1)
                gather_rows(pool, ln, io.nodes, dst_slot[:, slot], slot)

            def group(j, slot, n):
                if there(j + 2):
                    gather(j + 2, (slot + 2) % D)
                if there(j + 1):
                    wait_apart(pool, ticks, weighted_ready, j - 1)
                    inverse_std(pool, ln, sh, ticks, j + 1, (slot + 1) % D)
                wait_apart(pool, ticks, scattered[slot], n * 16 * G)
                pool.tensor_copy(out_slot[:, slot], sh.index[FIRST_ROW][:, tiles_of(group_of(j))]).then_inc(out_copied, 1)
                wait_apart(pool, ticks, out_copied, j + 1)
                wait_apart(pool, ticks, result_ready, j + 1)
                for u in reversed(range(G)):
                    pool.indirect_dma_start(io.nodes, bass.IndirectOffsetOnAxis(ap=out_slot[:, slot, u:u + 1], axis=0),
                                            result[:, slot, u], None, bounds_check=NODES - 1,
                                            oob_is_err=False).then_inc(scattered[slot], 16)
            pool.memset(total[:, D - 1, 0], 0.0).then_inc(zeroed, 1)
            gather(0, 0)
            gather(1, 1)
            inverse_std(pool, ln, sh, ticks, 0, 0)
            for_groups(pool, D, group)
            for slot in range(D):
                pool.wait_ge(scattered[slot], 16 * G * len(range(slot, NG, D)))

        @block.vector
        def _(dve):
            def prepare_group(j, slot, n):
                norm_relu(dve, ln, normed, j, slot, n)
                dve.wait_ge(tops_in[slot], n * 32 + 32)
                wait_past(dve, scored, (j - D + 1) * G)
                if isinstance(j, int) and j == 0:
                    initial = -BIG
                else:
                    dve.wait_ge(top_done, j)
                    initial = run_top[:, (slot + 2) % D, 0:1]
                dve.tensor_tensor_scan(run_top[:, slot, ::-1], mask[:, slot, ::-1], top[:, slot, ::-1], initial,
                                       ALU.add, ALU.max).then_inc(top_done, 1)
                wait_apart(dve, ticks, total_done, (j - D + 1) * G)
                for k, col in enumerate((START, FROM_NEXT)):
                    last = dve.tensor_tensor(sel[:, slot, k], sh.iota[:].unsqueeze(1).broadcast_to([P, G, P]),
                                             sh.index[col][:, tiles_of(group_of(j))].unsqueeze(2).broadcast_to([P, G, P]),
                                             ALU.is_equal)
                last.then_inc(sel_ready, 1)

            def weights(j, slot, n):
                dve.wait_ge(scored, (j + 1) * G)
                dve.wait_ge(wh_in[slot], n * 16 + 16)
                dve.wait_ge(ln.rstd_ready, j + 1)
                dve.tensor_tensor(dst_score[:], scores[slot][:, :, 0:HEADS],
                                  ln.rstd[:, slot].unsqueeze(2).broadcast_to([P, G, HEADS]), ALU.mult).then_inc(score_step, 1)
                dve.wait_ge(score_step, j * 3 + 1)
                dve.tensor_tensor(logit[:, :, 0:HEADS], wh[:, slot, :, FEAT:FW], dst_score[:], ALU.add)
                dve.tensor_tensor(logit[:, :, HEADS:2 * HEADS], scores[slot][:, :, HEADS:2 * HEADS], dst_score[:],
                                  ALU.add).then_inc(score_step, 1)
                dve.wait_ge(score_step, j * 3 + 2)
                dve.scalar_tensor_tensor(leaky[:], logit[:], SLOPE, logit[:], ALU.mult, ALU.max).then_inc(score_step, 1)
                dve.wait_ge(score_step, j * 3 + 3)
                dve.tensor_tensor(below[:, slot], leaky[:, :, 0:HEADS], leaky[:, :, HEADS:2 * HEADS],
                                  ALU.subtract).then_inc(below_ready, 1)
                dve.wait_ge(exp_done, j + 1)
                dve.tensor_tensor(weighted[:, slot, :, 0:FEAT].rearrange("p g (h d) -> p g h d", h=HEADS),
                                  wh[:, slot, :, 0:FEAT].rearrange("p g (h d) -> p g h d", h=HEADS),
                                  over_heads(weighted[:, slot, :, FEAT:FW]), ALU.mult).then_inc(weighted_ready, 1)

            def results(j, slot, n):
                dve.wait_ge(total_out, (j + 1) * G)
                dve.tensor_scalar(denom[:], total[:, slot, :, FEAT:FW], 1e-30, None, ALU.max).then_inc(result_step, 1)
                dve.wait_ge(result_step, j * 3 + 1)
                dve.reciprocal(inv[:], denom[:]).then_inc(result_step, 1)
                dve.wait_ge(result_step, j * 3 + 2)
                wait_past(dve, scattered[slot], n * 16 * G)
                dve.tensor_tensor(result[:, slot].rearrange("p g (h d) -> p g h d", h=HEADS),
                                  total[:, slot, :, 0:FEAT].rearrange("p g (h d) -> p g h d", h=HEADS),
                                  over_heads(inv[:]), ALU.mult).then_inc(result_step, 1)
                dve.wait_ge(result_step, j * 3 + 3)
                dve.tensor_tensor(result[:, slot], result[:, slot], ln.rows[:, slot], ALU.add).then_inc(result_ready, 1)

            def group(j, slot, n):
                weights(j, slot, n)
                if there(j + 1):
                    prepare_group(j + 1, *after(slot, n, D))
                results(j, slot, n)
            prepare_group(0, 0, 0)
            for_groups(dve, D, group)

        @block.tensor
        def _(pe):
            def turn(j, slot, v):
                if v == 0:
                    pe.wait_ge(ln.relu_done, j + 1)
                wait_past(pe, turn_out, j * G + v - 1)
                u = G - 1 - v
                for c in range(2):
                    last = pe.transpose(ps[:, v % 2, c * P:(c + 1) * P], normed[:, slot, u, c * P:(c + 1) * P], sh.ident[:])
                last.then_inc(turn_done, 1)

            def score(j, slot, v):
                u = G - 1 - v
                if v == 0:
                    wait_past(pe, weighted_ready, j - D + 1)
                    pe.wait_ge(top_done, j + 1)
                pe.wait_ge(turn_out, j * G + v + 1)
                for c in range(2):
                    pe.matmul(scores[slot][:, u, 0:HEADS], turned[:, v % 2, c * P:(c + 1) * P], sh.w_dst[:, c],
                              start=(c == 0), stop=(c == 1))
                pe.transpose(scores[slot][:, u, HEADS:2 * HEADS], run_top[:, slot, u * P:(u + 1) * P],
                             sh.ident[0:HEADS, 0:HEADS]).then_inc(scored, 1)

            def sum_runs(j, slot, v):
                u = G - 1 - v
                k = j * G + v
                out = ps[:, 4 + v % 2, 0:FW]
                if v == 0:
                    pe.wait_ge(weighted_ready, j + 1)
                    pe.wait_ge(sel_ready, j + 1)
                wait_past(pe, total_out, k - 1)
                pe.matmul(out, sel[:, slot, 0, u], weighted[:, slot, u], start=True, stop=False)
                if isinstance(k, int) and k == 0:
                    pe.wait_ge(zeroed, 1)
                else:
                    pe.wait_ge(total_out, k)
                before = total[:, slot, u + 1] if v else total[:, (slot + 2) % D, 0]
                pe.matmul(out, sel[:, slot, 1, u], before, start=False, stop=True).then_inc(total_done, 1)

            def score_group(j, slot):
                turn(j, slot, 0)
                for v in range(G):
                    if v < G - 1:
                        turn(j, slot, v + 1)
                    score(j, slot, v)

            def group(j, slot, n):
                for v in range(G):
                    sum_runs(j, slot, v)
                if there(j + 1):
                    score_group(j + 1, (slot + 1) % D)
            score_group(0, 0)
            for_groups(pe, D, group)

        @block.scalar
        def _(act):
            def rows_out(j, v):
                k = j * G + v
                act.wait_ge(turn_done, k + 1)
                wait_past(act, scored, k - 1)
                act.activation(turned[:, v % 2], ps[:, v % 2, 0:2 * P], ACT.Copy).then_inc(turn_out, 1)

            def group(j, slot, n):
                act.wait_ge(below_ready, j + 1)
                wait_past(act, total_done, (j - D + 1) * G)
                act.activation(weighted[:, slot, :, FEAT:FW], below[:, slot], ACT.Exp).then_inc(exp_done, 1)
                for v in range(G):
                    if v == 0:
                        wait_past(act, result_ready, j - D + 1)
                    act.wait_ge(total_done, j * G + v + 1)
                    act.activation(total[:, slot, G - 1 - v], ps[:, 4 + v % 2, 0:FW], ACT.Copy).then_inc(total_out, 1)
                if there(j + 1):
                    for v in range(G):
                        rows_out(j + 1, v)
            for v in range(G):
                rows_out(0, v)
            for_groups(act, D, group)


INPUTS = (("x", (NODES, FEAT), F32), ("src", (EPAD,), I32), ("dst", (EPAD + 2,), I32), ("spare_rows", (HALF, 2, P), I32),
          ("attr", (P, TILES, 4), F32),
          ("lens", (LEN_IN, EPAD), F32), ("attr_rows", (EPAD, 4), F32), ("lens_rows", (EPAD, LEN_IN), F32), ("w_a", (P, MUL), F32), ("w_b", (P, MUL), F32),
          ("fc_w1", (LEN_IN, HIDDEN), F32), ("fc_w2", (HIDDEN, 1), F32), ("w_c", (FEAT, FEAT), F32),
          ("a", (HEADS, 2 * HID), F32))


def build(nc):
    io, sh = Shared(), Shared()
    (io.x, io.src, io.dst, io.spare_rows, io.attr, io.lens, io.attr_rows, io.lens_rows, io.w_a, io.w_b, io.fc_w1,
     io.fc_w2, io.w_c, io.a) = [nc.dram_tensor(name, shape, dt, kind="ExternalInput").ap() for name, shape, dt in INPUTS]
    io.nodes = nc.dram_tensor("nodes", (OUT_ROWS, FEAT), F32, kind="ExternalOutput").ap()
    io.table = nc.dram_tensor("edge_table", (EPAD, RECORD), I32, kind="Internal").ap()
    io.src_w = nc.dram_tensor("src_work", (EPAD,), I32, kind="Internal").ap()
    io.dst_w = nc.dram_tensor("dst_work", (EPAD + 2,), I32, kind="Internal").ap()
    io.attr_w = nc.dram_tensor("attr_work", (P, TILES, 4), F32, kind="Internal").ap()
    io.lens_w = nc.dram_tensor("lens_work", (LEN_IN, EPAD), F32, kind="Internal").ap()
    io.first_mask = nc.dram_tensor("first_mask_rows", (EPAD,), F32, kind="Internal").ap()
    io.last_mask = nc.dram_tensor("last_mask_rows", (EPAD,), F32, kind="Internal").ap()
    io.wh = nc.dram_tensor("wh_rows", (EPAD, FW), F32, kind="Internal").ap()
    io.top = nc.dram_tensor("top_rows", (HEADS, EPAD), F32, kind="Internal").ap()
    with ExitStack() as ctx:
        sb = lambda name, shape, dt=F32: ctx.enter_context(nc.sbuf_tensor(name, shape, dt))
        sh.psum = io.psum = ctx.enter_context(nc.psum_tensor("psum", [P, 8, 512], F32))
        order_edges(nc, io)
        sh.iota_i = sb("iota_i", [P, P], I32)
        sh.iota = sb("iota", [P, P])
        sh.ident = sb("ident", [P, P])
        sh.minus_half = sb("minus_half", [P, G])
        sh.index = [sb(f"index{k}", [P, TILES], I32 if k < END else F32) for k in range(8)]
        sh.coef = sb("coef", [P, TILES, 4])
        sh.w_a = sb("w_a_sb", [P, MUL])
        sh.w_b = sb("w_b_sb", [P, MUL])
        sh.w_c = sb("w_c_sb", [P, 2, FW])
        sh.w_dst = sb("w_dst_sb", [P, 2, HEADS])
        prepare(nc, io, sh)
        layer0(nc, io, sh)
        project(nc, io, sh)
        layer1(nc, io, sh)


def layout(x, src, dst, edge_attr_10, edge_attr_4, L0_gnn_w_00_0, L0_gnn_w_11_0, L0_gnn_w_01_1, L0_gnn_w_10_1,
           L0_gnn_fc_w1, L0_gnn_fc_w2, L1_gnn_W, L1_gnn_a):
    pad = EPAD - EDGES
    attr_rows = np.concatenate([edge_attr_4, np.zeros((pad, 4), edge_attr_4.dtype)])
    lens_rows = np.concatenate([edge_attr_10, np.zeros((pad, LEN_IN), edge_attr_10.dtype)])
    return {
        "x": x,
        "src": np.concatenate([src, np.zeros(pad, src.dtype)]),
        "dst": np.concatenate([np.full(1, -1, dst.dtype), dst, np.full(pad, PAD_NODE, dst.dtype),
                               np.full(1, PAD_NODE + 1, dst.dtype)]),
        "spare_rows": (DUMMY + np.arange(EPAD, dtype=dst.dtype) % (DUMMY_TILES * P)).reshape(2, HALF, P).transpose(1, 0, 2),
        "attr": attr_rows.reshape(TILES, P, 4).transpose(1, 0, 2),
        "attr_rows": attr_rows,
        "lens": lens_rows.T,
        "lens_rows": lens_rows,
        "w_a": np.concatenate([L0_gnn_w_00_0, L0_gnn_w_11_0]),
        "w_b": np.concatenate([L0_gnn_w_01_1, L0_gnn_w_10_1]),
        "fc_w1": L0_gnn_fc_w1,
        "fc_w2": L0_gnn_fc_w2,
        "w_c": L1_gnn_W.transpose(1, 0, 2).reshape(FEAT, FEAT),
        "a": L1_gnn_a,
    }


def kernel(**inputs):
    import concourse.bacc as bacc
    from concourse.bass_utils import run_bass_kernel_spmd

    nc = bacc.Bacc("TRN2", target_bir_lowering=False, num_devices=1)
    build(nc)
    arrays = {k: np.ascontiguousarray(v) for k, v in layout(**{k: np.asarray(v) for k, v in inputs.items()}).items()}
    r = run_bass_kernel_spmd(nc, [arrays], core_ids=[0])
    return r.results[0]["nodes"][:NODES]
```

```python
from contextlib import ExitStack

import numpy as np

import concourse.bass as bass
from concourse import mybir

P = 128
NODES, EDGES, FEAT = 50000, 25000, 256
MUL = 64
HEADS, HID = 8, 32
HIDDEN = 64
TILES = -(-EDGES // P)
EPAD = TILES * P
G = 4
NG = TILES // G
HALF = TILES // 2
GE = G * P
FW = FEAT + HEADS
PAD_NODE = NODES
DUMMY = NODES + 1
DUMMY_TILES = 4 * G
OUT_ROWS = DUMMY + DUMMY_TILES * P
BIG = 1.0e30
EPS = 1e-5
SLOPE = 0.2
LEN_IN = 10
STEPS = 8
RECORD = 2 + 4 + LEN_IN
COPY_ROWS = 1024
COPY_LAST = NODES - (NG - 1) * COPY_ROWS
COPY_RUN = 16
assert TILES % G == 0 and TILES % 2 == 0 and COPY_LAST % COPY_RUN == 0 and 0 < COPY_LAST <= COPY_ROWS

W_SCALE = float(1.0 / np.sqrt(2.0 * MUL) * 1.679177 / np.sqrt(64.0) / np.sqrt(16.0))
W_SCALE_11 = float(W_SCALE / np.sqrt(3.0))
RADIAL_SCALE = float(1.0 / np.sqrt(10.0))

ALU = mybir.AluOpType
ACT = mybir.ActivationFunctionType
AX_X = mybir.AxisListType.X
F32 = mybir.dt.float32
I32 = mybir.dt.int32

SRC, LAST_ROW, FIRST_ROW, DST, END, START, FROM_PREV, FROM_NEXT = range(8)


def wait_past(eng, sem, value):
    if not isinstance(value, int) or value > 0:
        eng.wait_ge(sem, value)


def wait_apart(eng, ticks, sem, value):
    if not isinstance(value, int) or value > 0:
        eng.wait_ge(sem, value)
        eng.sem_inc(ticks)


def for_groups(eng, depth, body):
    end = (NG - 2) // depth * depth
    for g in range(depth):
        body(g, g, 0)
    with eng.Fori(1, end // depth) as n:
        for slot in range(depth):
            body(n * depth + slot, slot, n)
    for g in range(end, NG):
        body(g, g % depth, g // depth)


def after(slot, n, depth, by=1):
    return (slot + by) % depth, n + (slot + by) // depth


def there(g):
    return not isinstance(g, int) or g < NG


def over_heads(ap, g=G):
    return ap.unsqueeze(3).broadcast_to([P, g, HEADS, HID])


def tiles_of(g):
    return bass.ds(g * G, G)


def edges_of(g):
    return bass.ds(g * GE, GE)


class Shared:
    pass


def order_edges(nc, io):
    PARTS = 4
    PART = EPAD // PARTS
    with ExitStack() as ctx:
        sb = lambda name, shape, dt=F32: ctx.enter_context(nc.sbuf_tensor(f"order_{name}", shape, dt))
        sem = lambda name: ctx.enter_context(nc.semaphore(f"order_{name}"))
        seen = sb("seen", [HALF, 2, 2, P], I32)
        seen_f = sb("seen_f", [HALF, 2, 2, P])
        falls = sb("falls", [HALF, 2 * P])
        fell = sb("fell", [HALF, 1])
        ones = sb("ones", [HALF, 1])
        unsorted = sb("unsorted", [1, 1], I32)
        part_i = sb("part_i", [P, PART], I32)
        compared = sb("compared", [P, PART])
        twice = sb("twice", [P, EPAD])
        own_i = sb("own_i", [P, TILES], I32)
        own = sb("own", [P, TILES])
        lower = sb("lower", [P, P])
        counts = sb("counts", [P, PARTS + 1])
        rank_f = sb("rank_f", [P, 1])
        rank = sb("rank", [P, 1], I32)
        record = sb("record", [P, RECORD], I32)
        seen_in = sem("seen_in")
        checked = sem("checked")
        counted = sem("counted")
        flag_set = sem("flag_set")
        part_in = sem("part_in")
        part_used = sem("part_used")
        own_in = sem("own_in")
        lower_made = sem("lower_made")
        record_in = sem("record_in")
        dve_step = sem("dve_step")
        ranked = sem("ranked")
        sent = sem("sent")
        table_full = sem("table_full")
        working = sem("working")
        ticks = sem("ticks")
        ctx.enter_context(nc.allow_non_contiguous_dma(reason="single columns of the records, where edges are unsorted"))
        block = ctx.enter_context(nc.Block())

        def is_unsorted(eng):
            eng.wait_ge(flag_set, 1)
            return eng.value_load(unsorted[0:1, 0:1]) > 0

        @block.sync
        def _(sp):
            for k in range(2):
                sp.dma_start(seen[:, k], io.dst[k:k + EPAD].rearrange("(h q p) -> q h p", h=2, p=P)).then_inc(seen_in, 16)
            with sp.If(is_unsorted(sp)):
                for c in range(PARTS):
                    if c:
                        sp.wait_ge(part_used, c)
                    sp.dma_start(part_i[:], io.dst[1 + c * PART:1 + (c + 1) * PART].partition_broadcast(P)).then_inc(part_in, 16)
                sp.dma_start(own_i[:], io.dst[1:1 + EPAD].rearrange("(t p) -> p t", p=P)).then_inc(own_in, 16)
                with sp.Fori(0, TILES) as t:
                    edges = bass.ds(t * P, P)
                    later = bass.ds(t * P + 1, P)
                    sp.dma_start(record[:, 0:1], io.src[edges].unsqueeze(1)).then_inc(record_in, 16)
                    sp.dma_start(record[:, 1:2], io.dst[later].unsqueeze(1)).then_inc(record_in, 16)
                    sp.dma_start(record[:, 2:6].bitcast(F32), io.attr_rows[edges]).then_inc(record_in, 16)
                    sp.dma_start(record[:, 6:RECORD].bitcast(F32), io.lens_rows[edges]).then_inc(record_in, 16)
                    wait_apart(sp, ticks, sent, t * 16 + 16)
                sp.wait_ge(table_full, 1)
                whole = io.table.bitcast(F32)
                sp.dma_start(io.src_w, io.table[:, 0]).then_inc(working, 16)
                sp.dma_start(io.dst_w[1:1 + EPAD], io.table[:, 1]).then_inc(working, 16)
                sp.dma_start(io.attr_w, whole[:, 2:6].rearrange("(t p) c -> p t c", p=P)).then_inc(working, 16)
                for c in range(LEN_IN):
                    sp.dma_start(io.lens_w[c], whole[:, 6 + c]).then_inc(working, 16)
                for at in (0, EPAD + 1):
                    sp.dma_start(io.dst_w[at:at + 1], io.dst[at:at + 1]).then_inc(working, 16)
                sp.wait_ge(working, 16 * (5 + LEN_IN))
            with sp.Else():
                sp.dma_start(io.src_w, io.src).then_inc(working, 16)
                sp.dma_start(io.dst_w, io.dst).then_inc(working, 16)
                sp.dma_start(io.attr_w, io.attr).then_inc(working, 16)
                sp.dma_start(io.lens_w, io.lens).then_inc(working, 16)
                sp.wait_ge(working, 64)

        @block.gpsimd
        def _(pool):
            pool.memset(ones[:], 1.0).then_inc(lower_made, 1)
            pool.memset(lower[:], 1.0).then_inc(lower_made, 1)
            pool.wait_ge(lower_made, 2)
            pool.affine_select(out=lower[:], in_=lower[:], compare_op=ALU.is_gt, fill=0.0, base=0,
                               pattern=[[-1, P]], channel_multiplier=1).then_inc(lower_made, 1)
            with pool.If(is_unsorted(pool)):
                with pool.Fori(0, TILES) as t:
                    wait_apart(pool, ticks, record_in, t * 64 + 64)
                    wait_apart(pool, ticks, ranked, t + 1)
                    pool.indirect_dma_start(io.table, bass.IndirectOffsetOnAxis(ap=rank[:], axis=0), record[:], None,
                                            bounds_check=EPAD - 1, oob_is_err=True).then_inc(sent, 16)
                pool.wait_ge(sent, 16 * TILES)
                pool.sem_inc(table_full)
            with pool.Else():
                pool.sem_inc(ticks)

        @block.tensor
        def _(pe):
            pe.wait_ge(lower_made, 1)
            pe.wait_ge(checked, 1)
            pe.matmul(io.psum[0:1, 0, 0:1], fell[:], ones[:], start=True, stop=True).then_inc(counted, 1)

        @block.vector
        def _(dve):
            steps = [0]

            def chain(ins):
                steps[0] += 1
                ins.then_inc(dve_step, 1)
                dve.wait_ge(dve_step, steps[0])

            dve.wait_ge(seen_in, 32)
            chain(dve.tensor_copy(seen_f[:], seen[:]))
            chain(dve.tensor_tensor(falls[:].rearrange("q (h p) -> q h p", h=2), seen_f[:, 1], seen_f[:, 0], ALU.is_lt))
            dve.tensor_reduce(fell[:], falls[:], AX_X, ALU.add).then_inc(checked, 1)
            dve.wait_ge(counted, 1)
            dve.tensor_copy(unsorted[:], io.psum[0:1, 0, 0:1]).then_inc(flag_set, 1)
            with dve.If(is_unsorted(dve)):
                for c in range(PARTS):
                    dve.wait_ge(part_in, 16 * (c + 1))
                    dve.tensor_scalar(twice[:, c * PART:(c + 1) * PART], part_i[:], 2.0, None, ALU.mult).then_inc(part_used, 1)
                dve.wait_ge(own_in, 16)
                dve.tensor_scalar(own[:], own_i[:], 2.0, None, ALU.mult).then_inc(part_used, 1)
                dve.wait_ge(part_used, PARTS + 1)
                dve.wait_ge(lower_made, 3)
                with dve.Fori(0, TILES) as t:
                    mine = own[:, bass.ds(t, 1)]
                    tile = twice[:, bass.ds(t * P, P)]
                    for c in range(PARTS):
                        dve.tensor_scalar(compared[:], twice[:, c * PART:(c + 1) * PART], mine, 0.0, ALU.is_lt, ALU.add,
                                          accum_out=counts[:, c:c + 1]).then_inc(dve_step, 1)
                        wait_apart(dve, ticks, dve_step, t * STEPS + 3 + c)
                    dve.scalar_tensor_tensor(compared[:, 0:P], tile, mine, lower[:], ALU.is_equal, ALU.mult).then_inc(dve_step, 1)
                    wait_apart(dve, ticks, dve_step, t * STEPS + 3 + PARTS)
                    dve.tensor_reduce(counts[:, PARTS:PARTS + 1], compared[:, 0:P], AX_X, ALU.add).then_inc(dve_step, 1)
                    wait_apart(dve, ticks, dve_step, t * STEPS + 4 + PARTS)
                    dve.tensor_reduce(rank_f[:], counts[:], AX_X, ALU.add).then_inc(dve_step, 1)
                    wait_apart(dve, ticks, dve_step, t * STEPS + 5 + PARTS)
                    dve.tensor_scalar(tile, tile, -1.0, None, ALU.add).then_inc(dve_step, 1)
                    wait_apart(dve, ticks, dve_step, t * STEPS + 6 + PARTS)
                    dve.tensor_copy(rank[:], rank_f[:]).then_inc(ranked, 1)
                    wait_apart(dve, ticks, sent, t * 16 + 16)
            with dve.Else():
                dve.sem_inc(ticks)


def prepare(nc, io, sh):
    with ExitStack() as ctx:
        sb = lambda name, shape, dt=F32: ctx.enter_context(nc.sbuf_tensor(f"prepare_{name}", shape, dt))
        sem = lambda name: ctx.enter_context(nc.semaphore(f"prepare_{name}"))
        raw_place = sb("raw_place", [HALF, 2, P], I32)
        raw = sb("raw", [HALF, 4, 2, P], I32)
        own = sb("own", [HALF, 2, P])
        prv = sb("prv", [HALF, 2, P])
        nxt = sb("nxt", [HALF, 2, P])
        is_first = sb("is_first", [HALF, 2, P])
        is_last = sb("is_last", [HALF, 2, P])
        first_mask = sb("first_mask", [HALF, 2, P])
        last_mask = sb("last_mask", [HALF, 2, P])
        place = sb("place", [HALF, 2, P])
        dummy_i = sb("dummy_i", [HALF, 2, P], I32)
        dummy = sb("dummy", [HALF, 2, P])
        work = sb("work", [HALF, 2, P])
        ends = sb("ends", [HALF, 2, P])
        starts = sb("starts", [HALF, 2, P])
        cols = sb("cols", [HALF, 8, 2, P])
        one = sb("one", [HALF, 2, 1])
        a_all = sb("a_all", [P, HEADS, 2 * HID])
        wprod = sb("wprod", [P, HEADS, HID])
        attr = sb("attr", [P, TILES, 4])
        fc1 = sb("fc1", [LEN_IN, HIDDEN])
        fc2 = sb("fc2", [HIDDEN, 1])
        lens = sb("lens", [LEN_IN, 4, GE])
        hidden = sb("hidden", [HIDDEN, 2, GE])
        zeros = sb("zeros", [P, FEAT])

        edges_in = sem("edges_in")
        weights_in = sem("weights_in")
        lens_in = [sem(f"lens_in{s}") for s in range(4)]
        copied = sem("copied")
        masks_out = sem("masks_out")
        made = sem("made")
        dve_step = sem("dve_step")
        masks_made = sem("masks_made")
        cols_made = sem("cols_made")
        cols_turned = sem("cols_turned")
        hidden_in = sem("hidden_in")
        hidden_done = sem("hidden_done")
        factor_in = sem("factor_in")
        factor_used = sem("factor_used")
        block = ctx.enter_context(nc.Block())
        ps = sh.psum

        @block.sync
        def _(sp):
            for k, shift in enumerate((None, 0, 1, 2)):
                flat = io.src_w if shift is None else io.dst_w[shift:shift + EPAD]
                sp.dma_start(raw[:, k], flat.rearrange("(h q p) -> q h p", h=2, p=P)).then_inc(edges_in, 16)
            sp.dma_start(dummy_i[:], io.spare_rows).then_inc(edges_in, 16)
            sp.dma_start(fc1[:], io.fc_w1).then_inc(weights_in, 16)
            sp.dma_start(fc2[:], io.fc_w2).then_inc(weights_in, 16)
            sp.dma_start(sh.w_a[:], io.w_a).then_inc(weights_in, 16)
            sp.dma_start(sh.w_b[:], io.w_b).then_inc(weights_in, 16)
            sp.dma_start(sh.w_c[:, :, 0:FEAT], io.w_c.rearrange("(c p) n -> p c n", p=P)).then_inc(weights_in, 16)
            sp.dma_start(a_all[:], io.a.partition_broadcast(P)).then_inc(weights_in, 16)
            sp.dma_start(attr[:], io.attr_w).then_inc(weights_in, 16)

            def load(g, slot):
                wait_past(sp, hidden_in, g - 3)
                sp.dma_start(lens[:, slot], io.lens_w[:, edges_of(g)]).then_inc(lens_in[slot], 16)

            def group(g, slot, n):
                if there(g + 3):
                    load(g + 3, (slot + 3) % 4)
                rows = bass.ds(g * COPY_ROWS, COPY_LAST if isinstance(g, int) and g == NG - 1 else COPY_ROWS)
                sp.dma_start(io.nodes[rows].rearrange("(a b) c -> a (b c)", b=COPY_RUN),
                             io.x[rows].rearrange("(a b) c -> a (b c)", b=COPY_RUN)).then_inc(copied, 16)
            for g in range(3):
                load(g, g)
            for_groups(sp, 4, group)
            sp.wait_ge(masks_made, 2)
            sp.dma_start(io.first_mask.rearrange("(h q p) -> q h p", h=2, p=P), first_mask[:]).then_inc(masks_out, 16)
            sp.dma_start(io.last_mask.rearrange("(h q p) -> q h p", h=2, p=P), last_mask[:]).then_inc(masks_out, 16)
            sp.wait_ge(made, 3)
            sp.dma_start(io.nodes[PAD_NODE:DUMMY], zeros[0:1]).then_inc(copied, 16)
            sp.dma_start(io.nodes[DUMMY:OUT_ROWS].rearrange("(a p) c -> p a c", p=P),
                         zeros[:].unsqueeze(1).broadcast_to([P, DUMMY_TILES, FEAT])).then_inc(copied, 16)
            sp.wait_ge(copied, 16 * (NG + 2))
            sp.wait_ge(masks_out, 32)

        @block.gpsimd
        def _(pool):
            pool.iota(sh.iota_i[:], [[1, P]], base=0, channel_multiplier=0).then_inc(made, 1)
            pool.iota(raw_place[:], [[0, 2], [1, P]], base=0, channel_multiplier=0).then_inc(made, 1)
            pool.memset(zeros[:], 0.0).then_inc(made, 1)
            pool.memset(sh.ident[:], 0.0).then_inc(made, 1)
            pool.wait_ge(made, 4)
            pool.affine_select(out=sh.ident[:], in_=sh.ident[:], compare_op=ALU.not_equal, fill=1.0, base=0,
                               pattern=[[-1, P]], channel_multiplier=1).then_inc(made, 1)

        @block.vector
        def _(dve):
            steps = [0]

            def chain(ins):
                steps[0] += 1
                ins.then_inc(dve_step, 1)
                dve.wait_ge(dve_step, steps[0])

            dve.wait_ge(made, 4)
            dve.tensor_copy(sh.iota[:], sh.iota_i[:]).then_inc(dve_step, 1)
            dve.tensor_copy(place[:], raw_place[:]).then_inc(dve_step, 1)
            steps[0] += 2
            dve.wait_ge(edges_in, 80)
            dve.tensor_copy(cols[:, SRC], raw[:, 0]).then_inc(dve_step, 1)
            dve.tensor_copy(prv[:], raw[:, 1]).then_inc(dve_step, 1)
            dve.tensor_copy(own[:], raw[:, 2]).then_inc(dve_step, 1)
            steps[0] += 3
            chain(dve.tensor_copy(nxt[:], raw[:, 3]))
            dve.tensor_tensor(is_first[:], own[:], prv[:], ALU.not_equal).then_inc(dve_step, 1)
            dve.tensor_scalar(cols[:, DST], own[:], float(NODES - 1), None, ALU.min).then_inc(dve_step, 1)
            dve.tensor_copy(dummy[:], dummy_i[:]).then_inc(dve_step, 1)
            steps[0] += 3
            chain(dve.tensor_tensor(is_last[:], own[:], nxt[:], ALU.not_equal))
            dve.tensor_scalar(first_mask[:], is_first[:], -BIG, None, ALU.mult).then_inc(masks_made, 1)
            dve.tensor_scalar(last_mask[:], is_last[:], -BIG, None, ALU.mult).then_inc(masks_made, 1)
            chain(dve.tensor_tensor(work[:], own[:], dummy[:], ALU.subtract))
            chain(dve.tensor_tensor(work[:], work[:], is_last[:], ALU.mult))
            chain(dve.tensor_tensor(cols[:, LAST_ROW], work[:], dummy[:], ALU.add))
            chain(dve.tensor_tensor(work[:], own[:], dummy[:], ALU.subtract))
            chain(dve.tensor_tensor(work[:], work[:], is_first[:], ALU.mult))
            chain(dve.tensor_tensor(cols[:, FIRST_ROW], work[:], dummy[:], ALU.add))
            chain(dve.tensor_scalar(work[:], is_last[:], -999.0, 999.0, ALU.mult, ALU.add))
            chain(dve.tensor_tensor(work[:], work[:], place[:], ALU.add))
            chain(dve.memset(work[:, :, P - 1:P], float(P - 1)))
            for h in range(2):
                chain(dve.tensor_tensor_scan(ends[:, h, ::-1], work[:, h, ::-1], work[:, h, ::-1], 999.0, ALU.min, ALU.min))
            chain(dve.scalar_tensor_tensor(work[:], place[:], 1.0, is_first[:], ALU.add, ALU.mult))
            chain(dve.memset(work[:, :, 0:1], 1.0))
            for h in range(2):
                chain(dve.tensor_tensor_scan(starts[:, h, :], work[:, h, :], work[:, h, :], 0.0, ALU.max, ALU.max))
            chain(dve.tensor_scalar(starts[:], starts[:], -1.0, None, ALU.add))
            chain(dve.tensor_copy(cols[:, END], ends[:]))
            chain(dve.tensor_copy(cols[:, START], starts[:]))
            for col, flag, near, into, at in ((FROM_PREV, is_first, 0, ends, P - 1), (FROM_NEXT, is_last, P - 1, starts, 0)):
                chain(dve.memset(cols[:, col], -1.0))
                chain(dve.tensor_scalar(one[:], flag[:, :, near:near + 1], -1.0, 1.0, ALU.mult, ALU.add))
                chain(dve.scalar_tensor_tensor(one[:], into[:, :, near:near + 1], 1.0, one[:], ALU.add, ALU.mult))
                chain(dve.tensor_scalar(cols[:, col, :, at:at + 1], one[:], -1.0, None, ALU.add))
            dve.tensor_copy(one[:], one[:]).then_inc(cols_made, 1)

            dve.wait_ge(weights_in, 112)
            chain(dve.tensor_scalar(sh.w_a[0:MUL], sh.w_a[0:MUL], W_SCALE, None, ALU.mult))
            chain(dve.tensor_scalar(sh.w_a[MUL:P], sh.w_a[MUL:P], W_SCALE_11, None, ALU.mult))
            chain(dve.tensor_scalar(sh.w_b[:], sh.w_b[:], W_SCALE, None, ALU.mult))
            for c in range(2):
                wc = sh.w_c[:, c, 0:FEAT].rearrange("p (h d) -> p h d", h=HEADS)
                for k, out in ((0, sh.w_c[:, c, FEAT:FW]), (1, sh.w_dst[:, c])):
                    chain(dve.tensor_tensor(wprod[:], wc, a_all[:, :, k * HID:(k + 1) * HID], ALU.mult))
                    chain(dve.tensor_reduce(out, wprod[:], AX_X, ALU.add))

            for half in range(4):
                dve.wait_ge(cols_turned, half + 1)
                for k in (2 * half, 2 * half + 1):
                    at = k % 2 * TILES
                    dve.tensor_copy(sh.index[k][:], ps[:, half, at:at + TILES])

            def group(g, slot, n):
                dve.wait_ge(factor_in, g + 1)
                dve.tensor_tensor(sh.coef[:, tiles_of(g), :], attr[:, tiles_of(g), :],
                                  ps[:, 6 + slot % 2, 0:G].unsqueeze(2).broadcast_to([P, G, 4]), ALU.mult).then_inc(factor_used, 1)
            for_groups(dve, 4, group)

        @block.tensor
        def _(pe):
            pe.wait_ge(made, 5)
            pe.wait_ge(cols_made, 1)
            for k in range(8):
                for h in range(2):
                    at = (k % 2 * 2 + h) * HALF
                    last = pe.transpose(ps[:, k // 2, at:at + HALF], cols[:, k, h], sh.ident[0:HALF, 0:HALF])
                if k % 2:
                    last.then_inc(cols_turned, 1)
            pe.wait_ge(weights_in, 112)

            def hid(g, slot, n):
                pe.wait_ge(lens_in[slot], n * 16 + 16)
                wait_past(pe, hidden_done, g - 1)
                pe.matmul(ps[0:HIDDEN, 4 + slot % 2, :], fc1[:], lens[:, slot], start=True, stop=True).then_inc(hidden_in, 1)

            def group(g, slot, n):
                if there(g + 1):
                    hid(g + 1, *after(slot, n, 4))
                pe.wait_ge(hidden_done, g + 1)
                wait_past(pe, factor_used, g - 1)
                for u in range(G):
                    last = pe.matmul(ps[:, 6 + slot % 2, u:u + 1], hidden[:, slot % 2, u * P:(u + 1) * P], fc2[:],
                                     start=True, stop=True)
                last.then_inc(factor_in, 1)
            hid(0, 0, 0)
            for_groups(pe, 4, group)

        @block.scalar
        def _(act):
            def group(g, slot, n):
                act.wait_ge(hidden_in, g + 1)
                wait_past(act, factor_in, g - 1)
                act.activation(hidden[:, slot % 2], ps[0:HIDDEN, 4 + slot % 2, :], ACT.Silu, scale=RADIAL_SCALE).then_inc(hidden_done, 1)
            for_groups(act, 4, group)


def start_stats(ctx, nc, depth, phase):
    ln = Shared()
    ln.depth = depth
    sb = lambda name, shape, dt=F32: ctx.enter_context(nc.sbuf_tensor(f"{phase}_{name}", shape, dt))
    sem = lambda name: ctx.enter_context(nc.semaphore(f"{phase}_{name}"))
    ln.rows = sb("rows", [P, depth, G, FEAT])
    ln.parts = sb("parts", [P, depth, G, 6])
    ln.mean_var = sb("mean_var", [P, depth, G, 2])
    ln.minus_mean = sb("minus_mean", [P, depth, G])
    ln.spare = sb("spare", [P, 1])
    ln.var_eps = sb("var_eps", [P, depth, G])
    ln.std = sb("std", [P, depth, G])
    ln.guess = sb("guess", [P, G])
    ln.factor = sb("factor", [P, G])
    ln.rstd = sb("rstd", [P, depth, G])
    ln.rows_in = [sem(f"rows_in{s}") for s in range(depth)]
    ln.parts_done = sem("parts_done")
    ln.mean_done = sem("mean_done")
    ln.var_ready = sem("var_ready")
    ln.std_ready = sem("std_ready")
    ln.guess_step = sem("guess_step")
    ln.rstd_ready = sem("rstd_ready")
    ln.relu_done = sem("relu_done")
    ln.bound = None
    return ln


def gather_rows(pool, ln, table, index_slot, slot, tiles=range(G)):
    for u in tiles:
        pool.indirect_dma_start(ln.rows[:, slot, u], None, table,
                                bass.IndirectOffsetOnAxis(ap=index_slot[:, u:u + 1], axis=0),
                                bounds_check=ln.bound, oob_is_err=False).then_inc(ln.rows_in[slot], 16)


def statistics(dve, ln, j, slot, n, by_act=False):
    dve.wait_ge(ln.rows_in[slot], n * 16 * G + 16 * G)
    for u in range(G):
        last = dve.bn_stats(ln.parts[:, slot, u], ln.rows[:, slot, u])
    last.then_inc(ln.parts_done, 1)
    dve.wait_ge(ln.parts_done, j + 1)
    dve.memset(ln.spare[:], 0.0)
    for u in range(G):
        last = dve.bn_aggr(ln.mean_var[:, slot, u], ln.parts[:, slot, u])
    last.then_inc(ln.mean_done, 1)
    dve.wait_ge(ln.mean_done, j + 1)
    wait_past(dve, ln.std_ready, j - ln.depth + 1)
    if by_act:
        dve.tensor_scalar(ln.minus_mean[:, slot], ln.mean_var[:, slot, :, 0], -1.0, None, ALU.mult)
    dve.tensor_scalar(ln.var_eps[:, slot], ln.mean_var[:, slot, :, 1], EPS, None, ALU.add).then_inc(ln.var_ready, 1)


def relu(dve, ln, slot):
    for u in range(G):
        last = dve.tensor_scalar(ln.rows[:, slot, u], ln.rows[:, slot, u], ln.mean_var[:, slot, u, 0:1], 0.0,
                                 ALU.subtract, ALU.max)
    last.then_inc(ln.relu_done, 1)


def relu_by_act(act, ln, j, slot):
    act.wait_ge(ln.var_ready, j + 1)
    for u in range(G):
        last = act.activation(ln.rows[:, slot, u], ln.rows[:, slot, u], ACT.Relu, bias=ln.minus_mean[:, slot, u:u + 1])
    last.then_inc(ln.relu_done, 1)


def standard_deviation(act, ln, j, slot):
    act.wait_ge(ln.var_ready, j + 1)
    wait_past(act, ln.rstd_ready, j - ln.depth + 1)
    act.activation(ln.std[:, slot], ln.var_eps[:, slot], ACT.Sqrt).then_inc(ln.std_ready, 1)


def inverse_std(dve, ln, j, slot):
    dve.wait_ge(ln.std_ready, j + 1)
    wait_past(dve, ln.rstd_ready, j)
    dve.reciprocal(ln.guess[:], ln.std[:, slot]).then_inc(ln.guess_step, 1)
    dve.wait_ge(ln.guess_step, j * 3 + 1)
    dve.scalar_tensor_tensor(ln.factor[:], ln.var_eps[:, slot], -0.5, ln.guess[:], ALU.mult, ALU.mult).then_inc(ln.guess_step, 1)
    dve.wait_ge(ln.guess_step, j * 3 + 2)
    dve.tensor_tensor(ln.factor[:], ln.factor[:], ln.guess[:], ALU.mult).then_inc(ln.guess_step, 1)
    dve.wait_ge(ln.guess_step, j * 3 + 3)
    dve.scalar_tensor_tensor(ln.rstd[:, slot], ln.factor[:], 1.5, ln.guess[:], ALU.add, ALU.mult).then_inc(ln.rstd_ready, 1)


def layer0(nc, io, sh):
    D = 4
    UW = 4 * P
    with ExitStack() as ctx:
        sb = lambda name, shape, dt=F32: ctx.enter_context(nc.sbuf_tensor(f"layer0_{name}", shape, dt))
        sem = lambda name: ctx.enter_context(nc.semaphore(f"layer0_{name}"))
        ln = start_stats(ctx, nc, D, "layer0")
        src_slot = sb("src_slot", [P, D, G], I32)
        dst_slot = sb("dst_slot", [P, D, G], I32)
        scaled = sb("scaled", [P, 2, G, 4])
        by_part = sb("by_part", [P, G, MUL, 3])
        prod = sb("prod", [P, 2, G, UW])
        sel = sb("sel", [P, 2, 2, G, P])
        summed = sb("summed", [P, 2, UW])
        msg = sb("msg", [P, D, G, FEAT])
        src_copied = sem("src_copied")
        dst_copied = sem("dst_copied")
        scattered = [sem(f"scattered{s}") for s in range(D)]
        scaled_done = sem("scaled_done")
        parts_made = sem("parts_made")
        zeroed = sem("zeroed")
        prod_ready = sem("prod_ready")
        sum_done = sem("sum_done")
        sum_out = sem("sum_out")
        msg_done = sem("msg_done")
        msg_out = sem("msg_out")
        ticks = sem("ticks")
        block = ctx.enter_context(nc.Block())
        ps = sh.psum
        acc = [ps[:, q] for q in range(2)]

        @block.gpsimd
        def _(pool):
            ln.bound = pool.to_reg(NODES - 1)
            out_bound = pool.to_reg(OUT_ROWS - 1)

            def take_sources(g, slot):
                wait_apart(pool, ticks, prod_ready, g - D + 1)
                pool.tensor_copy(src_slot[:, slot], sh.index[SRC][:, tiles_of(g)]).then_inc(src_copied, 1)
                wait_apart(pool, ticks, src_copied, g + 1)

            def take_targets(g, slot, n):
                wait_apart(pool, ticks, scattered[slot], n * 16 * G)
                pool.tensor_copy(dst_slot[:, slot], sh.index[LAST_ROW][:, tiles_of(g)]).then_inc(dst_copied, 1)
                wait_apart(pool, ticks, dst_copied, g + 1)

            def scatter(g, slot, u):
                wait_apart(pool, ticks, msg_out, g * G + u + 1)
                pool.indirect_dma_start(io.nodes, bass.IndirectOffsetOnAxis(ap=dst_slot[:, slot, u:u + 1], axis=0),
                                        msg[:, slot, u], None, bounds_check=out_bound,
                                        compute_op=ALU.add).then_inc(scattered[slot], 16)

            def group(g, slot, n):
                near = (slot + 3) % D
                behind = not isinstance(g, int) or g > 0
                if there(g + 3):
                    take_sources(g + 3, near)
                if behind:
                    take_targets(g - 1, *after(slot, n - 1, D, 3))
                for u in range(G):
                    if there(g + 3):
                        gather_rows(pool, ln, io.x, src_slot[:, near], near, (u,))
                    if behind:
                        scatter(g - 1, near, u)
            pool.memset(msg[:, D - 1, G - 1], 0.0).then_inc(zeroed, 1)
            for g in range(3):
                take_sources(g, g)
                gather_rows(pool, ln, io.x, src_slot[:, g], g)
            for_groups(pool, D, group)
            last = NG - 1
            take_targets(last, last % D, last // D)
            for u in range(G):
                scatter(last, last % D, u)
            for slot in range(D):
                pool.wait_ge(scattered[slot], 16 * G * len(range(slot, NG, D)))

        @block.vector
        def _(dve):
            def products(g, slot, q):
                inverse_std(dve, ln, g, slot)
                dve.wait_ge(ln.relu_done, g + 1)
                wait_past(dve, msg_done, (g - 1) * G)
                dve.wait_ge(ln.rstd_ready, g + 1)
                dve.tensor_tensor(scaled[:, q], sh.coef[:, tiles_of(g)],
                                  ln.rstd[:, slot].unsqueeze(2).broadcast_to([P, G, 4]), ALU.mult).then_inc(scaled_done, 1)
                for k, col in enumerate((END, FROM_PREV)):
                    dve.tensor_tensor(sel[:, q, k], sh.iota[:].unsqueeze(1).broadcast_to([P, G, P]),
                                      sh.index[col][:, tiles_of(g)].unsqueeze(2).broadcast_to([P, G, P]), ALU.is_equal)
                dve.wait_ge(scaled_done, g + 1)
                s0 = ln.rows[:, slot, :, 0:MUL]
                s1 = ln.rows[:, slot, :, MUL:FEAT].rearrange("p g (i m) -> p g i m", m=3)
                c0 = scaled[:, q, :, 0:1]
                c1 = scaled[:, q, :, 1:4]
                out = prod[:, q]
                mixed = out[:, :, P:UW].rearrange("p g (m k i) -> p g m k i", m=3, k=2)
                dve.tensor_tensor(by_part[:], s1, c1.unsqueeze(2).broadcast_to([P, G, MUL, 3]), ALU.mult).then_inc(parts_made, 1)
                dve.tensor_tensor(out[:, :, 0:MUL], s0, c0.broadcast_to([P, G, MUL]), ALU.mult)
                dve.tensor_tensor(mixed[:, :, :, 0], s0.unsqueeze(2).broadcast_to([P, G, 3, MUL]),
                                  c1.unsqueeze(3).broadcast_to([P, G, 3, MUL]), ALU.mult)
                dve.tensor_tensor(mixed[:, :, :, 1], s1.rearrange("p g i m -> p g m i"),
                                  c0.unsqueeze(3).broadcast_to([P, G, 3, MUL]), ALU.mult)
                dve.wait_ge(parts_made, g + 1)
                dve.tensor_reduce(out[:, :, MUL:P], by_part[:], AX_X, ALU.add).then_inc(prod_ready, 1)

            def group(g, slot, n):
                if there(g + 1):
                    statistics(dve, ln, g + 1, *after(slot, n, D))
                    relu(dve, ln, (slot + 1) % D)
                products(g, slot, slot % 2)
            statistics(dve, ln, 0, 0, 0)
            relu(dve, ln, 0)
            for_groups(dve, D, group)

        @block.tensor
        def _(pe):
            def sum_runs(g, q, u):
                k = g * G + u
                if u == 0:
                    pe.wait_ge(prod_ready, g + 1)
                wait_past(pe, sum_out, k - 1)
                for c in range(UW // P):
                    last = pe.matmul(acc[u % 2][:, c * P:(c + 1) * P], prod[:, q, u, c * P:(c + 1) * P],
                                     sel[:, q, 0, u], start=(c == 0), stop=True, skip_group_check=True)
                last.then_inc(sum_done, 1)

            def messages(g, slot, u):
                k = g * G + u
                out = ps[:, 4 + u % 2, 0:FEAT]
                vec = out[:, MUL:FEAT].rearrange("p (o m) -> p m o", m=3)
                part = lambda c: summed[:, u % 2, c * P:(c + 1) * P]
                pe.wait_ge(sum_out, k + 1)
                pe.matmul(out[:, 0:MUL], part(0), sh.w_a[:], start=True, stop=False, skip_group_check=True)
                for m in range(3):
                    pe.matmul(vec[:, m], part(1 + m), sh.w_b[:], start=False, stop=False, skip_group_check=True)
                if isinstance(k, int) and k == 0:
                    pe.wait_ge(zeroed, 1)
                else:
                    pe.wait_ge(msg_out, k)
                before = msg[:, slot, u - 1] if u else msg[:, (slot + D - 1) % D, G - 1]
                pe.matmul(out, sel[:, slot % 2, 1, u], before, start=False, stop=True,
                          skip_group_check=True).then_inc(msg_done, 1)

            def group(g, slot, n):
                for u in range(G):
                    if u < G - 1:
                        sum_runs(g, slot % 2, u + 1)
                    elif there(g + 1):
                        sum_runs(g + 1, (slot + 1) % 2, 0)
                    messages(g, slot, u)
            sum_runs(0, 0, 0)
            for_groups(pe, D, group)

        @block.scalar
        def _(act):
            def sums_out(g, u):
                k = g * G + u
                act.wait_ge(sum_done, k + 1)
                wait_past(act, msg_done, k - 1)
                act.activation(summed[:, u % 2], acc[u % 2], ACT.Copy).then_inc(sum_out, 1)

            def group(g, slot, n):
                for u in range(G):
                    if u < G - 1:
                        sums_out(g, u + 1)
                    elif there(g + 1):
                        sums_out(g + 1, 0)
                    if u == 0:
                        wait_past(act, scattered[slot], n * 16 * G)
                    act.wait_ge(msg_done, g * G + u + 1)
                    act.activation(msg[:, slot, u], ps[:, 4 + u % 2, 0:FEAT], ACT.Copy).then_inc(msg_out, 1)
                    if u == 2 and there(g + 2):
                        standard_deviation(act, ln, g + 2, (slot + 2) % D)
            for g in range(2):
                standard_deviation(act, ln, g, g)
            sums_out(0, 0)
            for_groups(act, D, group)


def project(nc, io, sh):
    D = 4
    with ExitStack() as ctx:
        sb = lambda name, shape, dt=F32: ctx.enter_context(nc.sbuf_tensor(f"project_{name}", shape, dt))
        sem = lambda name: ctx.enter_context(nc.semaphore(f"project_{name}"))
        ln = start_stats(ctx, nc, D, "project")
        src_slot = sb("src_slot", [P, D, G], I32)
        turned = sb("turned", [P, 2, 2 * P])
        wh = sb("wh", [P, D, G, FW])
        mask = sb("mask", [HEADS, D, GE])
        top = sb("top", [HEADS, D, GE])
        src_copied = sem("src_copied")
        mask_in = [sem(f"mask_in{s}") for s in range(D)]
        wh_stored = [sem(f"wh_stored{s}") for s in range(D)]
        top_stored = [sem(f"top_stored{s}") for s in range(D)]
        turn_done = sem("turn_done")
        turn_out = sem("turn_out")
        wh_done = sem("wh_done")
        wh_out = sem("wh_out")
        score_turned = sem("score_turned")
        top_done = sem("top_done")
        ticks = sem("ticks")
        block = ctx.enter_context(nc.Block())
        ps = sh.psum

        @block.sync
        def _(sp):
            def load_mask(g, slot):
                wait_apart(sp, ticks, top_done, g - D + 1)
                sp.dma_start(mask[:, slot], io.first_mask[edges_of(g)].partition_broadcast(HEADS)).then_inc(mask_in[slot], 16)

            def group(g, slot, n):
                if there(g + 2):
                    load_mask(g + 2, (slot + 2) % D)
                wait_apart(sp, ticks, wh_out, (g + 1) * G)
                sp.dma_start(io.wh[edges_of(g)].rearrange("(u p) f -> p u f", p=P), wh[:, slot]).then_inc(wh_stored[slot], 16)
                wait_apart(sp, ticks, top_done, g + 1)
                sp.dma_start(io.top[:, edges_of(g)], top[:, slot]).then_inc(top_stored[slot], 16)
            for g in range(2):
                load_mask(g, g)
            for_groups(sp, D, group)
            for slot in range(D):
                sp.wait_ge(wh_stored[slot], 16 * len(range(slot, NG, D)))
                sp.wait_ge(top_stored[slot], 16 * len(range(slot, NG, D)))

        @block.gpsimd
        def _(pool):
            ln.bound = pool.to_reg(NODES - 1)

            def gather(g, slot):
                wait_apart(pool, ticks, turn_done, (g - D + 1) * G)
                pool.tensor_copy(src_slot[:, slot], sh.index[SRC][:, tiles_of(g)]).then_inc(src_copied, 1)
                wait_apart(pool, ticks, src_copied, g + 1)
                gather_rows(pool, ln, io.nodes, src_slot[:, slot], slot)

            def group(g, slot, n):
                if there(g + 3):
                    gather(g + 3, (slot + 3) % D)
            for g in range(3):
                gather(g, g)
            for_groups(pool, D, group)

        @block.vector
        def _(dve):
            def running_max(g, slot, n):
                dve.wait_ge(score_turned, (g + 1) * G)
                dve.wait_ge(mask_in[slot], n * 16 + 16)
                wait_past(dve, top_stored[slot], n * 16)
                if isinstance(g, int) and g == 0:
                    initial = -BIG
                else:
                    dve.wait_ge(top_done, g)
                    initial = top[:, (slot + D - 1) % D, GE - 1:GE]
                dve.tensor_tensor_scan(top[:, slot], mask[:, slot], ps[0:HEADS, 6 + slot % 2], initial,
                                       ALU.add, ALU.max).then_inc(top_done, 1)

            def group(g, slot, n):
                if there(g + 2):
                    statistics(dve, ln, g + 2, *after(slot, n, D, 2))
                    relu(dve, ln, (slot + 2) % D)
                if there(g + 1):
                    wait_past(dve, wh_out, (g - 2) * G)
                    inverse_std(dve, ln, g + 1, (slot + 1) % D)
                if not isinstance(g, int) or g > 0:
                    running_max(g - 1, *after(slot, n - 1, D, D - 1))
            for g in range(2):
                statistics(dve, ln, g, g, 0)
                relu(dve, ln, g)
            inverse_std(dve, ln, 0, 0)
            for_groups(dve, D, group)
            running_max(NG - 1, (NG - 1) % D, (NG - 1) // D)

        @block.tensor
        def _(pe):
            def turn(g, slot, u):
                if u == 0:
                    pe.wait_ge(ln.relu_done, g + 1)
                wait_past(pe, turn_out, g * G + u - 1)
                for c in range(2):
                    last = pe.transpose(ps[:, u % 2, c * P:(c + 1) * P], ln.rows[:, slot, u, c * P:(c + 1) * P], sh.ident[:])
                last.then_inc(turn_done, 1)

            def product(g, slot, u):
                k = g * G + u
                pe.wait_ge(turn_out, k + 1)
                wait_past(pe, wh_out, k - 1)
                for c in range(2):
                    last = pe.matmul(ps[:, 2 + u % 2, 0:FW], turned[:, u % 2, c * P:(c + 1) * P], sh.w_c[:, c],
                                     start=(c == 0), stop=(c == 1))
                last.then_inc(wh_done, 1)

            def turn_score(g, slot, u):
                if u == 0:
                    wait_past(pe, top_done, g - 1)
                pe.wait_ge(wh_out, g * G + u + 1)
                pe.transpose(ps[0:HEADS, 6 + slot % 2, u * P:(u + 1) * P], wh[:, slot, u, FEAT:FW],
                             sh.ident[:]).then_inc(score_turned, 1)

            def group(g, slot, n):
                for u in range(G):
                    if u < G - 1:
                        turn(g, slot, u + 1)
                    elif there(g + 1):
                        turn(g + 1, (slot + 1) % D, 0)
                    product(g, slot, u)
                    if u:
                        turn_score(g, slot, u - 1)
                    elif not isinstance(g, int) or g > 0:
                        turn_score(g - 1, (slot + D - 1) % D, G - 1)
            turn(0, 0, 0)
            for_groups(pe, D, group)
            turn_score(NG - 1, (NG - 1) % D, G - 1)

        @block.scalar
        def _(act):
            def rows_out(g, u):
                k = g * G + u
                act.wait_ge(turn_done, k + 1)
                wait_past(act, wh_done, k - 1)
                act.activation(turned[:, u % 2], ps[:, u % 2, 0:2 * P], ACT.Copy).then_inc(turn_out, 1)

            def group(g, slot, n):
                for u in range(G):
                    if u < G - 1:
                        rows_out(g, u + 1)
                    elif there(g + 1):
                        rows_out(g + 1, 0)
                    if u == 0:
                        act.wait_ge(ln.rstd_ready, g + 1)
                        wait_past(act, wh_stored[slot], n * 16)
                        wait_past(act, score_turned, (g - D + 1) * G)
                    act.wait_ge(wh_done, g * G + u + 1)
                    act.activation(wh[:, slot, u], ps[:, 2 + u % 2, 0:FW], ACT.Copy,
                                   scale=ln.rstd[:, slot, u:u + 1]).then_inc(wh_out, 1)
                    if u == 1 and there(g + 2):
                        standard_deviation(act, ln, g + 2, (slot + 2) % D)
            for g in range(2):
                standard_deviation(act, ln, g, g)
            rows_out(0, 0)
            for_groups(act, D, group)


def layer1(nc, io, sh):
    D = 4
    with ExitStack() as ctx:
        sb = lambda name, shape, dt=F32: ctx.enter_context(nc.sbuf_tensor(f"layer1_{name}", shape, dt))
        sem = lambda name: ctx.enter_context(nc.semaphore(f"layer1_{name}"))
        ln = start_stats(ctx, nc, D, "layer1")
        dst_slot = sb("dst_slot", [P, D, G], I32)
        out_slot = sb("out_slot", [P, D, G], I32)
        turned = sb("turned", [P, 2, 2 * P])
        wh = sb("wh", [P, D, G, FW])
        mask = sb("mask", [HEADS, D, GE])
        top = sb("top", [HEADS, D, GE])
        run_top = sb("run_top", [HEADS, D, GE])
        sel = sb("sel", [P, 2, 2, G, P])
        dst_score = sb("dst_score", [P, G, HEADS])
        logit = sb("logit", [P, G, 2 * HEADS])
        leaky = sb("leaky", [P, G, 2 * HEADS])
        below = sb("below", [P, 2, G, HEADS])
        weighted = sb("weighted", [P, 2, G, FW])
        total = sb("total", [P, D, G, FW])
        denom = sb("denom", [P, G, HEADS])
        inv = sb("inv", [P, G, HEADS])
        result = sb("result", [P, D, G, FEAT])
        dst_copied = sem("dst_copied")
        out_copied = sem("out_copied")
        wh_in = [sem(f"wh_in{s}") for s in range(D)]
        tops_in = [sem(f"tops_in{s}") for s in range(D)]
        scattered = [sem(f"scattered{s}") for s in range(D)]
        turn_done = sem("turn_done")
        turn_out = sem("turn_out")
        scored = sem("scored")
        top_done = sem("top_done")
        sel_ready = sem("sel_ready")
        score_step = sem("score_step")
        below_ready = sem("below_ready")
        exp_done = sem("exp_done")
        weighted_ready = sem("weighted_ready")
        zeroed = sem("zeroed")
        total_done = sem("total_done")
        total_out = sem("total_out")
        result_step = sem("result_step")
        result_ready = sem("result_ready")
        ticks = sem("ticks")
        block = ctx.enter_context(nc.Block())
        ps = sh.psum
        scores = [ps[:, b, 0:G * 2 * HEADS].rearrange("p (u k) -> p u k", u=G) for b in (2, 3)]

        group_of = lambda j: (NG - 1) - j
        starts = lambda j: isinstance(j, int) and j == 0

        @block.sync
        def _(sp):
            def load(j, slot):
                wait_apart(sp, ticks, weighted_ready, j - D + 1)
                edges = edges_of(group_of(j))
                sp.dma_start(mask[:, slot], io.last_mask[edges].partition_broadcast(HEADS)).then_inc(tops_in[slot], 16)
                sp.dma_start(top[:, slot], io.top[:, edges]).then_inc(tops_in[slot], 16)
                sp.dma_start(wh[:, slot], io.wh[edges].rearrange("(u p) f -> p u f", p=P)).then_inc(wh_in[slot], 16)

            def group(j, slot, n):
                if there(j + 3):
                    load(j + 3, (slot + 3) % D)
            for j in range(3):
                load(j, j)
            for_groups(sp, D, group)

        @block.gpsimd
        def _(pool):
            ln.bound = pool.to_reg(NODES - 1)
            out_bound = pool.to_reg(OUT_ROWS - 1)

            def take_targets(j, slot):
                wait_apart(pool, ticks, turn_done, (j - D + 1) * G)
                pool.tensor_copy(dst_slot[:, slot], sh.index[DST][:, tiles_of(group_of(j))]).then_inc(dst_copied, 1)
                wait_apart(pool, ticks, dst_copied, j + 1)

            def take_firsts(j, slot, n):
                wait_apart(pool, ticks, scattered[slot], n * 16 * G)
                pool.tensor_copy(out_slot[:, slot], sh.index[FIRST_ROW][:, tiles_of(group_of(j))]).then_inc(out_copied, 1)
                wait_apart(pool, ticks, out_copied, j + 1)
                wait_apart(pool, ticks, result_ready, j + 1)

            def scatter(slot, u):
                pool.indirect_dma_start(io.nodes, bass.IndirectOffsetOnAxis(ap=out_slot[:, slot, u:u + 1], axis=0),
                                        result[:, slot, u], None, bounds_check=out_bound,
                                        compute_op=ALU.add).then_inc(scattered[slot], 16)

            def group(j, slot, n):
                near, back = (slot + 3) % D, (slot + 2) % D
                behind = not isinstance(j, int) or j >= 2
                if there(j + 3):
                    take_targets(j + 3, near)
                for v in range(G):
                    if there(j + 3):
                        gather_rows(pool, ln, io.nodes, dst_slot[:, near], near, (v,))
                    if behind:
                        if v == 0:
                            take_firsts(j - 2, *after(slot, n - 1, D, 2))
                        scatter(back, G - 1 - v)
            pool.memset(total[:, D - 1, 0], 0.0).then_inc(zeroed, 1)
            for j in range(3):
                take_targets(j, j)
                gather_rows(pool, ln, io.nodes, dst_slot[:, j], j)
            for_groups(pool, D, group)
            for j in (NG - 2, NG - 1):
                take_firsts(j, j % D, j // D)
                for v in range(G):
                    scatter(j % D, G - 1 - v)
            for slot in range(D):
                pool.wait_ge(scattered[slot], 16 * G * len(range(slot, NG, D)))

        @block.vector
        def _(dve):
            def prepare_group(j, slot, n):
                statistics(dve, ln, j, slot, n, by_act=True)
                dve.wait_ge(tops_in[slot], n * 32 + 32)
                wait_past(dve, scored, (j - D + 1) * G)
                if starts(j):
                    initial = -BIG
                else:
                    dve.wait_ge(top_done, j)
                    initial = run_top[:, (slot + D - 1) % D, 0:1]
                dve.tensor_tensor_scan(run_top[:, slot, ::-1], mask[:, slot, ::-1], top[:, slot, ::-1], initial,
                                       ALU.add, ALU.max).then_inc(top_done, 1)

            def logits(j, slot, n):
                inverse_std(dve, ln, j, slot)
                dve.wait_ge(scored, (j + 1) * G)
                dve.wait_ge(wh_in[slot], n * 16 + 16)
                dve.wait_ge(ln.rstd_ready, j + 1)
                dve.tensor_tensor(dst_score[:], scores[slot % 2][:, :, 0:HEADS],
                                  ln.rstd[:, slot].unsqueeze(2).broadcast_to([P, G, HEADS]), ALU.mult).then_inc(score_step, 1)
                dve.wait_ge(score_step, j * 3 + 1)
                dve.tensor_tensor(logit[:, :, 0:HEADS], wh[:, slot, :, FEAT:FW], dst_score[:], ALU.add)
                dve.tensor_tensor(logit[:, :, HEADS:2 * HEADS], scores[slot % 2][:, :, HEADS:2 * HEADS], dst_score[:],
                                  ALU.add).then_inc(score_step, 1)
                dve.wait_ge(score_step, j * 3 + 2)
                dve.scalar_tensor_tensor(leaky[:], logit[:], SLOPE, logit[:], ALU.mult, ALU.max).then_inc(score_step, 1)
                dve.wait_ge(score_step, j * 3 + 3)
                dve.tensor_tensor(below[:, slot % 2], leaky[:, :, 0:HEADS], leaky[:, :, HEADS:2 * HEADS],
                                  ALU.subtract).then_inc(below_ready, 1)

            def selections(j, q):
                wait_apart(dve, ticks, total_done, (j - 1) * G)
                for k, col in enumerate((START, FROM_NEXT)):
                    last = dve.tensor_tensor(sel[:, q, k], sh.iota[:].unsqueeze(1).broadcast_to([P, G, P]),
                                             sh.index[col][:, tiles_of(group_of(j))].unsqueeze(2).broadcast_to([P, G, P]),
                                             ALU.is_equal)
                last.then_inc(sel_ready, 1)

            def weigh(j, slot):
                dve.wait_ge(exp_done, j + 1)
                out = weighted[:, slot % 2]
                dve.tensor_tensor(out[:, :, 0:FEAT].rearrange("p g (h d) -> p g h d", h=HEADS),
                                  wh[:, slot, :, 0:FEAT].rearrange("p g (h d) -> p g h d", h=HEADS),
                                  over_heads(out[:, :, FEAT:FW]), ALU.mult).then_inc(weighted_ready, 1)

            def quotients(j, slot, n):
                dve.wait_ge(total_out, (j + 1) * G)
                dve.tensor_scalar(denom[:], total[:, slot, :, FEAT:FW], 1e-30, None, ALU.max).then_inc(result_step, 1)
                dve.wait_ge(result_step, j * 2 + 1)
                dve.reciprocal(inv[:], denom[:]).then_inc(result_step, 1)
                dve.wait_ge(result_step, j * 2 + 2)
                wait_past(dve, scattered[slot], n * 16 * G)
                dve.tensor_tensor(result[:, slot].rearrange("p g (h d) -> p g h d", h=HEADS),
                                  total[:, slot, :, 0:FEAT].rearrange("p g (h d) -> p g h d", h=HEADS),
                                  over_heads(inv[:]), ALU.mult).then_inc(result_ready, 1)

            def group(j, slot, n):
                logits(j, slot, n)
                if not isinstance(j, int) or j >= 2:
                    quotients(j - 2, *after(slot, n - 1, D, 2))
                selections(j, slot % 2)
                weigh(j, slot)
                if there(j + 2):
                    prepare_group(j + 2, *after(slot, n, D, 2))
            for j in range(2):
                prepare_group(j, j, 0)
            for_groups(dve, D, group)
            for j in (NG - 2, NG - 1):
                quotients(j, j % D, j // D)

        @block.tensor
        def _(pe):
            def turn(j, slot, v):
                if v == 0:
                    pe.wait_ge(ln.relu_done, j + 1)
                wait_past(pe, turn_out, j * G + v - 1)
                u = G - 1 - v
                for c in range(2):
                    last = pe.transpose(ps[:, v % 2, c * P:(c + 1) * P], ln.rows[:, slot, u, c * P:(c + 1) * P], sh.ident[:])
                last.then_inc(turn_done, 1)

            def score(j, slot, v):
                u = G - 1 - v
                if v == 0:
                    wait_past(pe, below_ready, j - 1)
                    pe.wait_ge(top_done, j + 1)
                pe.wait_ge(turn_out, j * G + v + 1)
                for c in range(2):
                    pe.matmul(scores[slot % 2][:, u, 0:HEADS], turned[:, v % 2, c * P:(c + 1) * P], sh.w_dst[:, c],
                              start=(c == 0), stop=(c == 1))
                pe.transpose(scores[slot % 2][:, u, HEADS:2 * HEADS], run_top[:, slot, u * P:(u + 1) * P],
                             sh.ident[0:HEADS, 0:HEADS]).then_inc(scored, 1)

            def sum_runs(j, slot, v):
                u = G - 1 - v
                k = j * G + v
                if v == 0:
                    pe.wait_ge(weighted_ready, j + 1)
                    pe.wait_ge(sel_ready, j + 1)
                wait_past(pe, total_out, k - 1)
                pe.matmul(ps[:, 4 + v % 2, 0:FW], sel[:, slot % 2, 0, u], weighted[:, slot % 2, u], start=True, stop=False)

            def add_next(j, slot, v):
                u = G - 1 - v
                k = j * G + v
                if starts(k):
                    pe.wait_ge(zeroed, 1)
                else:
                    pe.wait_ge(total_out, k)
                before = total[:, slot, u + 1] if v else total[:, (slot + D - 1) % D, 0]
                pe.matmul(ps[:, 4 + v % 2, 0:FW], sel[:, slot % 2, 1, u], before, start=False, stop=True).then_inc(total_done, 1)

            def step(j, slot, sums, turns):
                if turns:
                    turn(j + 1, (slot + 1) % D, 0)
                for v in range(G):
                    if sums:
                        sum_runs(j - 1, (slot + D - 1) % D, v)
                    if turns and v < G - 1:
                        turn(j + 1, (slot + 1) % D, v + 1)
                    if sums:
                        add_next(j - 1, (slot + D - 1) % D, v)
                    if turns:
                        score(j + 1, (slot + 1) % D, v)

            def group(j, slot, n):
                step(j, slot, not starts(j), there(j + 1))
            step(-1, D - 1, False, True)
            for_groups(pe, D, group)
            step(NG, NG % D, True, False)

        @block.scalar
        def _(act):
            def rows_out(j, v):
                k = j * G + v
                act.wait_ge(turn_done, k + 1)
                wait_past(act, scored, k - 1)
                act.activation(turned[:, v % 2], ps[:, v % 2, 0:2 * P], ACT.Copy).then_inc(turn_out, 1)

            def sums_out(j, slot, v):
                if v == 0:
                    wait_past(act, result_ready, j - D + 1)
                act.wait_ge(total_done, j * G + v + 1)
                act.activation(total[:, slot, G - 1 - v], ps[:, 4 + v % 2, 0:FW], ACT.Copy).then_inc(total_out, 1)

            def exponentials(j, q):
                act.wait_ge(below_ready, j + 1)
                wait_past(act, total_done, (j - 1) * G)
                act.activation(weighted[:, q, :, FEAT:FW], below[:, q], ACT.Exp).then_inc(exp_done, 1)

            def step(j, slot, sums, turns):
                if turns:
                    rows_out(j + 1, 0)
                for v in range(G):
                    if turns and v < G - 1:
                        rows_out(j + 1, v + 1)
                    if sums:
                        sums_out(j - 1, (slot + D - 1) % D, v)

            def group(j, slot, n):
                exponentials(j, slot % 2)
                step(j, slot, not starts(j), there(j + 1))
                if there(j + 2):
                    relu_by_act(act, ln, j + 2, (slot + 2) % D)
                    standard_deviation(act, ln, j + 2, (slot + 2) % D)
            for j in range(2):
                relu_by_act(act, ln, j, j)
                standard_deviation(act, ln, j, j)
            step(-1, D - 1, False, True)
            for_groups(act, D, group)
            step(NG, NG % D, True, False)


INPUTS = (("x", (NODES, FEAT), F32), ("src", (EPAD,), I32), ("dst", (EPAD + 2,), I32), ("spare_rows", (HALF, 2, P), I32),
          ("attr", (P, TILES, 4), F32),
          ("lens", (LEN_IN, EPAD), F32), ("attr_rows", (EPAD, 4), F32), ("lens_rows", (EPAD, LEN_IN), F32), ("w_a", (P, MUL), F32), ("w_b", (P, MUL), F32),
          ("fc_w1", (LEN_IN, HIDDEN), F32), ("fc_w2", (HIDDEN, 1), F32), ("w_c", (FEAT, FEAT), F32),
          ("a", (HEADS, 2 * HID), F32))


def build(nc):
    io, sh = Shared(), Shared()
    (io.x, io.src, io.dst, io.spare_rows, io.attr, io.lens, io.attr_rows, io.lens_rows, io.w_a, io.w_b, io.fc_w1,
     io.fc_w2, io.w_c, io.a) = [nc.dram_tensor(name, shape, dt, kind="ExternalInput").ap() for name, shape, dt in INPUTS]
    io.nodes = nc.dram_tensor("nodes", (OUT_ROWS, FEAT), F32, kind="ExternalOutput").ap()
    io.table = nc.dram_tensor("edge_table", (EPAD, RECORD), I32, kind="Internal").ap()
    io.src_w = nc.dram_tensor("src_work", (EPAD,), I32, kind="Internal").ap()
    io.dst_w = nc.dram_tensor("dst_work", (EPAD + 2,), I32, kind="Internal").ap()
    io.attr_w = nc.dram_tensor("attr_work", (P, TILES, 4), F32, kind="Internal").ap()
    io.lens_w = nc.dram_tensor("lens_work", (LEN_IN, EPAD), F32, kind="Internal").ap()
    io.first_mask = nc.dram_tensor("first_mask_rows", (EPAD,), F32, kind="Internal").ap()
    io.last_mask = nc.dram_tensor("last_mask_rows", (EPAD,), F32, kind="Internal").ap()
    io.wh = nc.dram_tensor("wh_rows", (EPAD, FW), F32, kind="Internal").ap()
    io.top = nc.dram_tensor("top_rows", (HEADS, EPAD), F32, kind="Internal").ap()
    with ExitStack() as ctx:
        sb = lambda name, shape, dt=F32: ctx.enter_context(nc.sbuf_tensor(name, shape, dt))
        sh.psum = io.psum = ctx.enter_context(nc.psum_tensor("psum", [P, 8, 512], F32))
        order_edges(nc, io)
        sh.iota_i = sb("iota_i", [P, P], I32)
        sh.iota = sb("iota", [P, P])
        sh.ident = sb("ident", [P, P])
        sh.index = [sb(f"index{k}", [P, TILES], I32 if k < END else F32) for k in range(8)]
        sh.coef = sb("coef", [P, TILES, 4])
        sh.w_a = sb("w_a_sb", [P, MUL])
        sh.w_b = sb("w_b_sb", [P, MUL])
        sh.w_c = sb("w_c_sb", [P, 2, FW])
        sh.w_dst = sb("w_dst_sb", [P, 2, HEADS])
        prepare(nc, io, sh)
        layer0(nc, io, sh)
        project(nc, io, sh)
        layer1(nc, io, sh)


def layout(x, src, dst, edge_attr_10, edge_attr_4, L0_gnn_w_00_0, L0_gnn_w_11_0, L0_gnn_w_01_1, L0_gnn_w_10_1,
           L0_gnn_fc_w1, L0_gnn_fc_w2, L1_gnn_W, L1_gnn_a):
    pad = EPAD - EDGES
    attr_rows = np.concatenate([edge_attr_4, np.zeros((pad, 4), edge_attr_4.dtype)])
    lens_rows = np.concatenate([edge_attr_10, np.zeros((pad, LEN_IN), edge_attr_10.dtype)])
    return {
        "x": x,
        "src": np.concatenate([src, np.zeros(pad, src.dtype)]),
        "dst": np.concatenate([np.full(1, -1, dst.dtype), dst, np.full(pad, PAD_NODE, dst.dtype),
                               np.full(1, PAD_NODE + 1, dst.dtype)]),
        "spare_rows": (DUMMY + np.arange(EPAD, dtype=dst.dtype) % (DUMMY_TILES * P)).reshape(2, HALF, P).transpose(1, 0, 2),
        "attr": attr_rows.reshape(TILES, P, 4).transpose(1, 0, 2),
        "attr_rows": attr_rows,
        "lens": lens_rows.T,
        "lens_rows": lens_rows,
        "w_a": np.concatenate([L0_gnn_w_00_0, L0_gnn_w_11_0]),
        "w_b": np.concatenate([L0_gnn_w_01_1, L0_gnn_w_10_1]),
        "fc_w1": L0_gnn_fc_w1,
        "fc_w2": L0_gnn_fc_w2,
        "w_c": L1_gnn_W.transpose(1, 0, 2).reshape(FEAT, FEAT),
        "a": L1_gnn_a,
    }


def kernel(**inputs):
    import concourse.bacc as bacc
    from concourse.bass_utils import run_bass_kernel_spmd

    nc = bacc.Bacc("TRN2", target_bir_lowering=False, num_devices=1)
    build(nc)
    arrays = {k: np.ascontiguousarray(v) for k, v in layout(**{k: np.asarray(v) for k, v in inputs.items()}).items()}
    r = run_bass_kernel_spmd(nc, [arrays], core_ids=[0])
    return r.results[0]["nodes"][:NODES]
```

```python
from contextlib import ExitStack

import numpy as np

import concourse.bass as bass
from concourse import mybir

P = 128
NODES, EDGES, FEAT = 50000, 25000, 256
MUL = 64
HEADS, HID = 8, 32
HIDDEN = 64
TILES = -(-EDGES // P)
EPAD = TILES * P
G = 4
NG = TILES // G
HALF = TILES // 2
GE = G * P
FW = FEAT + HEADS
PAD_NODE = NODES
DUMMY = NODES + 1
DUMMY_TILES = 4 * G
OUT_ROWS = DUMMY + DUMMY_TILES * P
BIG = 1.0e30
EPS = 1e-5
SLOPE = 0.2
LEN_IN = 10
EXP_LN_SET = 6
STEPS = 8
RECORD = 2 + 4 + LEN_IN
RT = HALF // NG
COPY_ROWS = 400
COPY_RUN = 25
COPY_SLOTS = 5
ROUND_ROWS = COPY_ROWS * COPY_SLOTS
COPY_ROUNDS = NODES // ROUND_ROWS
EARLY_ROUNDS = 8
assert TILES % G == 0 and HALF % NG == 0 and COPY_ROWS % COPY_RUN == 0 and COPY_ROUNDS * ROUND_ROWS == NODES

W_SCALE = float(1.0 / np.sqrt(2.0 * MUL) * 1.679177 / np.sqrt(64.0) / np.sqrt(16.0))
W_SCALE_11 = float(W_SCALE / np.sqrt(3.0))
RADIAL_SCALE = float(1.0 / np.sqrt(10.0))

ALU = mybir.AluOpType
ACT = mybir.ActivationFunctionType
AX_X = mybir.AxisListType.X
F32 = mybir.dt.float32
I32 = mybir.dt.int32

SRC, LAST_ROW, FIRST_ROW, DST, END, START, FROM_PREV, FROM_NEXT = range(8)


def wait_past(eng, sem, value):
    if not isinstance(value, int) or value > 0:
        eng.wait_ge(sem, value)


def wait_apart(eng, ticks, sem, value):
    if not isinstance(value, int) or value > 0:
        eng.wait_ge(sem, value)
        eng.sem_inc(ticks)


def for_groups(eng, depth, body):
    end = (NG - 2) // depth * depth
    for g in range(depth):
        body(g, g, 0)
    with eng.Fori(1, end // depth) as n:
        for slot in range(depth):
            body(n * depth + slot, slot, n)
    for g in range(end, NG):
        body(g, g % depth, g // depth)


def after(slot, n, depth, by=1):
    return (slot + by) % depth, n + (slot + by) // depth


def there(g):
    return not isinstance(g, int) or 0 <= g < NG


def over_heads(ap, g=G):
    return ap.unsqueeze(3).broadcast_to([P, g, HEADS, HID])


def tiles_of(g):
    return bass.ds(g * G, G)


def edges_of(g):
    return bass.ds(g * GE, GE)


def copy_nodes(sp, io, sh, first, end):
    def copy(n, slot):
        rows = bass.ds(n * ROUND_ROWS + slot * COPY_ROWS, COPY_ROWS)
        sp.dma_start(io.nodes[rows].rearrange("(a b) c -> a (b c)", b=COPY_RUN),
                     io.x[rows].rearrange("(a b) c -> a (b c)", b=COPY_RUN)).then_inc(sh.copied[slot], 16)
    if first == 0:
        for slot in range(COPY_SLOTS):
            copy(0, slot)
    with sp.Fori(max(first, 1), end) as n:
        for slot in range(COPY_SLOTS):
            wait_apart(sp, sh.copy_ticks, sh.copied[slot], n * 16)
            copy(n, slot)


class Shared:
    pass


def order_edges(nc, io):
    PARTS = 4
    PART = EPAD // PARTS
    with ExitStack() as ctx:
        sb = lambda name, shape, dt=F32: ctx.enter_context(nc.sbuf_tensor(f"order_{name}", shape, dt))
        sem = lambda name: ctx.enter_context(nc.semaphore(f"order_{name}"))
        seen = sb("seen", [HALF, 2, 2, P], I32)
        seen_f = sb("seen_f", [HALF, 2, 2, P])
        falls = sb("falls", [HALF, 2 * P])
        fell = sb("fell", [HALF, 1])
        ones = sb("ones", [HALF, 1])
        unsorted = sb("unsorted", [1, 1], I32)
        part_i = sb("part_i", [P, PART], I32)
        compared = sb("compared", [P, PART])
        twice = sb("twice", [P, EPAD])
        own_i = sb("own_i", [P, TILES], I32)
        own = sb("own", [P, TILES])
        lower = sb("lower", [P, P])
        counts = sb("counts", [P, PARTS + 1])
        rank_f = sb("rank_f", [P, 1])
        rank = sb("rank", [P, 1], I32)
        record = sb("record", [P, RECORD], I32)
        seen_in = sem("seen_in")
        checked = sem("checked")
        counted = sem("counted")
        flag_set = sem("flag_set")
        part_in = sem("part_in")
        part_used = sem("part_used")
        own_in = sem("own_in")
        lower_made = sem("lower_made")
        record_in = sem("record_in")
        dve_step = sem("dve_step")
        ranked = sem("ranked")
        sent = sem("sent")
        table_full = sem("table_full")
        working = sem("working")
        ticks = sem("ticks")
        ctx.enter_context(nc.allow_non_contiguous_dma(reason="single columns of the records, where edges are unsorted"))
        block = ctx.enter_context(nc.Block())

        def is_unsorted(eng):
            eng.wait_ge(flag_set, 1)
            return eng.value_load(unsorted[0:1, 0:1]) > 0

        @block.sync
        def _(sp):
            for k in range(2):
                sp.dma_start(seen[:, k], io.dst[k:k + EPAD].rearrange("(h q p) -> q h p", h=2, p=P)).then_inc(seen_in, 16)
            with sp.If(is_unsorted(sp)):
                for c in range(PARTS):
                    if c:
                        sp.wait_ge(part_used, c)
                    sp.dma_start(part_i[:], io.dst[1 + c * PART:1 + (c + 1) * PART].partition_broadcast(P)).then_inc(part_in, 16)
                sp.dma_start(own_i[:], io.dst[1:1 + EPAD].rearrange("(t p) -> p t", p=P)).then_inc(own_in, 16)
                with sp.Fori(0, TILES) as t:
                    edges = bass.ds(t * P, P)
                    later = bass.ds(t * P + 1, P)
                    sp.dma_start(record[:, 0:1], io.src[edges].unsqueeze(1)).then_inc(record_in, 16)
                    sp.dma_start(record[:, 1:2], io.dst[later].unsqueeze(1)).then_inc(record_in, 16)
                    sp.dma_start(record[:, 2:6].bitcast(F32), io.attr_rows[edges]).then_inc(record_in, 16)
                    sp.dma_start(record[:, 6:RECORD].bitcast(F32), io.lens_rows[edges]).then_inc(record_in, 16)
                    wait_apart(sp, ticks, sent, t * 16 + 16)
                sp.wait_ge(table_full, 1)
                whole = io.table.bitcast(F32)
                sp.dma_start(io.src_w, io.table[:, 0]).then_inc(working, 16)
                sp.dma_start(io.dst_w[1:1 + EPAD], io.table[:, 1]).then_inc(working, 16)
                sp.dma_start(io.attr_w, whole[:, 2:6].rearrange("(t p) c -> p t c", p=P)).then_inc(working, 16)
                for c in range(LEN_IN):
                    sp.dma_start(io.lens_w[c], whole[:, 6 + c]).then_inc(working, 16)
                for at in (0, EPAD + 1):
                    sp.dma_start(io.dst_w[at:at + 1], io.dst[at:at + 1]).then_inc(working, 16)
                sp.wait_ge(working, 16 * (5 + LEN_IN))
            with sp.Else():
                sp.dma_start(io.src_w, io.src).then_inc(working, 16)
                sp.dma_start(io.dst_w, io.dst).then_inc(working, 16)
                sp.dma_start(io.attr_w, io.attr).then_inc(working, 16)
                sp.dma_start(io.lens_w, io.lens).then_inc(working, 16)
                sp.wait_ge(working, 64)

        @block.gpsimd
        def _(pool):
            pool.memset(ones[:], 1.0).then_inc(lower_made, 1)
            pool.memset(lower[:], 1.0).then_inc(lower_made, 1)
            pool.wait_ge(lower_made, 2)
            pool.affine_select(out=lower[:], in_=lower[:], compare_op=ALU.is_gt, fill=0.0, base=0,
                               pattern=[[-1, P]], channel_multiplier=1).then_inc(lower_made, 1)
            with pool.If(is_unsorted(pool)):
                with pool.Fori(0, TILES) as t:
                    wait_apart(pool, ticks, record_in, t * 64 + 64)
                    wait_apart(pool, ticks, ranked, t + 1)
                    pool.indirect_dma_start(io.table, bass.IndirectOffsetOnAxis(ap=rank[:], axis=0), record[:], None,
                                            bounds_check=EPAD - 1, oob_is_err=True).then_inc(sent, 16)
                pool.wait_ge(sent, 16 * TILES)
                pool.sem_inc(table_full)
            with pool.Else():
                pool.sem_inc(ticks)

        @block.tensor
        def _(pe):
            pe.wait_ge(lower_made, 1)
            pe.wait_ge(checked, 1)
            pe.matmul(io.psum[0:1, 0, 0:1], fell[:], ones[:], start=True, stop=True).then_inc(counted, 1)

        @block.vector
        def _(dve):
            steps = [0]

            def chain(ins):
                steps[0] += 1
                ins.then_inc(dve_step, 1)
                dve.wait_ge(dve_step, steps[0])

            dve.wait_ge(seen_in, 32)
            chain(dve.tensor_copy(seen_f[:], seen[:]))
            chain(dve.tensor_tensor(falls[:].rearrange("q (h p) -> q h p", h=2), seen_f[:, 1], seen_f[:, 0], ALU.is_lt))
            dve.tensor_reduce(fell[:], falls[:], AX_X, ALU.add).then_inc(checked, 1)
            dve.wait_ge(counted, 1)
            dve.tensor_copy(unsorted[:], io.psum[0:1, 0, 0:1]).then_inc(flag_set, 1)
            with dve.If(is_unsorted(dve)):
                for c in range(PARTS):
                    dve.wait_ge(part_in, 16 * (c + 1))
                    dve.tensor_scalar(twice[:, c * PART:(c + 1) * PART], part_i[:], 2.0, None, ALU.mult).then_inc(part_used, 1)
                dve.wait_ge(own_in, 16)
                dve.tensor_scalar(own[:], own_i[:], 2.0, None, ALU.mult).then_inc(part_used, 1)
                dve.wait_ge(part_used, PARTS + 1)
                dve.wait_ge(lower_made, 3)
                with dve.Fori(0, TILES) as t:
                    mine = own[:, bass.ds(t, 1)]
                    tile = twice[:, bass.ds(t * P, P)]
                    for c in range(PARTS):
                        dve.tensor_scalar(compared[:], twice[:, c * PART:(c + 1) * PART], mine, 0.0, ALU.is_lt, ALU.add,
                                          accum_out=counts[:, c:c + 1]).then_inc(dve_step, 1)
                        wait_apart(dve, ticks, dve_step, t * STEPS + 3 + c)
                    dve.scalar_tensor_tensor(compared[:, 0:P], tile, mine, lower[:], ALU.is_equal, ALU.mult).then_inc(dve_step, 1)
                    wait_apart(dve, ticks, dve_step, t * STEPS + 3 + PARTS)
                    dve.tensor_reduce(counts[:, PARTS:PARTS + 1], compared[:, 0:P], AX_X, ALU.add).then_inc(dve_step, 1)
                    wait_apart(dve, ticks, dve_step, t * STEPS + 4 + PARTS)
                    dve.tensor_reduce(rank_f[:], counts[:], AX_X, ALU.add).then_inc(dve_step, 1)
                    wait_apart(dve, ticks, dve_step, t * STEPS + 5 + PARTS)
                    dve.tensor_scalar(tile, tile, -1.0, None, ALU.add).then_inc(dve_step, 1)
                    wait_apart(dve, ticks, dve_step, t * STEPS + 6 + PARTS)
                    dve.tensor_copy(rank[:], rank_f[:]).then_inc(ranked, 1)
                    wait_apart(dve, ticks, sent, t * 16 + 16)
            with dve.Else():
                dve.sem_inc(ticks)


def prepare(nc, io, sh):
    with ExitStack() as ctx:
        sb = lambda name, shape, dt=F32: ctx.enter_context(nc.sbuf_tensor(f"prepare_{name}", shape, dt))
        sem = lambda name: ctx.enter_context(nc.semaphore(f"prepare_{name}"))
        raw_place = sb("raw_place", [HALF, 2, P], I32)
        raw = sb("raw", [HALF, 4, 2, P], I32)
        own = sb("own", [HALF, 2, P])
        prv = sb("prv", [HALF, 2, P])
        nxt = sb("nxt", [HALF, 2, P])
        is_first = sb("is_first", [HALF, 2, P])
        is_last = sb("is_last", [HALF, 2, P])
        first_mask = sb("first_mask", [HALF, 2, P])
        last_mask = sb("last_mask", [HALF, 2, P])
        place = sb("place", [HALF, 2, P])
        dummy_i = sb("dummy_i", [HALF, 2, P], I32)
        dummy = sb("dummy", [HALF, 2, P])
        work = sb("work", [HALF, 2, P])
        ends = sb("ends", [HALF, 2, P])
        starts = sb("starts", [HALF, 2, P])
        cols = sb("cols", [HALF, 8, 2, P])
        one = sb("one", [HALF, 2, 1])
        a_all = sb("a_all", [P, HEADS, 2 * HID])
        wprod = sb("wprod", [P, HEADS, HID])
        attr = sb("attr", [P, TILES, 4])
        fc1 = sb("fc1", [2 * LEN_IN, 2 * HIDDEN])
        fc2 = sb("fc2", [P, HIDDEN])
        lens = sb("lens", [2 * LEN_IN, HALF * P])
        lens_slot = sb("lens_slot", [2 * LEN_IN, 2, RT * P])
        hidden = sb("hidden", [P, 2, 2 * RT, HIDDEN])
        radial = sb("radial", [P, 2, 2 * RT, HIDDEN])
        factors = sb("factors", [P, HALF, 2])
        zeros = sb("zeros", [P, FEAT])
        highest = sb("highest", [1, NG], I32)
        rounds = sb("rounds", [1, NG])
        rounds_i = sb("rounds_i", [1, NG], I32)

        edges_in = sem("edges_in")
        weights_in = sem("weights_in")
        lens_in = sem("lens_in")
        fc2_in = sem("fc2_in")
        lens_copied = sem("lens_copied")
        radial_done = sem("radial_done")
        ticks = sem("ticks")
        spare_rows_out = sem("spare_rows_out")
        masks_out = sem("masks_out")
        made = sem("made")
        dve_step = sem("dve_step")
        masks_made = sem("masks_made")
        cols_made = sem("cols_made")
        cols_turned = sem("cols_turned")
        hidden_in = sem("hidden_in")
        hidden_done = sem("hidden_done")
        factor_in = sem("factor_in")
        block = ctx.enter_context(nc.Block())
        ps = sh.psum

        @block.sync
        def _(sp):
            for k, shift in enumerate((None, 0, 1, 2)):
                flat = io.src_w if shift is None else io.dst_w[shift:shift + EPAD]
                sp.dma_start(raw[:, k], flat.rearrange("(h q p) -> q h p", h=2, p=P)).then_inc(edges_in, 16)
            sp.dma_start(dummy_i[:], io.spare_rows).then_inc(edges_in, 16)
            sp.dma_start(highest[:], io.dst_w[1:1 + EPAD].rearrange("(g e) -> g e", e=GE)[:, GE - 1].unsqueeze(0),
                         allow_slow_non_contiguous=True).then_inc(edges_in, 16)
            for h in range(2):
                sp.dma_start(lens[h * LEN_IN:(h + 1) * LEN_IN], io.lens_w[:, h * HALF * P:(h + 1) * HALF * P]).then_inc(lens_in, 16)
            sp.dma_start(fc2[:], io.fc_w2.rearrange("k o -> (k o)").partition_broadcast(P)).then_inc(fc2_in, 16)
            sp.wait_ge(made, 5)
            for h in range(2):
                sp.dma_start(fc1[h * LEN_IN:(h + 1) * LEN_IN, h * HIDDEN:(h + 1) * HIDDEN], io.fc_w1).then_inc(weights_in, 16)
            sp.dma_start(sh.w_a[:], io.w_a).then_inc(weights_in, 16)
            sp.dma_start(sh.w_b[:], io.w_b).then_inc(weights_in, 16)
            sp.dma_start(sh.w_c[:, :, 0:FEAT], io.w_c.rearrange("(c p) n -> p c n", p=P)).then_inc(weights_in, 16)
            sp.dma_start(a_all[:], io.a.partition_broadcast(P)).then_inc(weights_in, 16)
            sp.dma_start(attr[:], io.attr_w).then_inc(weights_in, 16)

            sp.dma_start(io.nodes[PAD_NODE:DUMMY], zeros[0:1]).then_inc(spare_rows_out, 16)
            sp.dma_start(io.nodes[DUMMY:OUT_ROWS].rearrange("(a p) c -> p a c", p=P),
                         zeros[:].unsqueeze(1).broadcast_to([P, DUMMY_TILES, FEAT])).then_inc(spare_rows_out, 16)
            copy_nodes(sp, io, sh, 0, EARLY_ROUNDS)
            sp.wait_ge(masks_made, 2)
            sp.dma_start(io.first_mask.rearrange("(h q p) -> q h p", h=2, p=P), first_mask[:]).then_inc(masks_out, 16)
            sp.dma_start(io.last_mask.rearrange("(h q p) -> q h p", h=2, p=P), last_mask[:]).then_inc(masks_out, 16)
            sp.wait_ge(spare_rows_out, 32)
            sp.wait_ge(masks_out, 32)

        @block.gpsimd
        def _(pool):
            pool.iota(sh.iota_i[:], [[1, P]], base=0, channel_multiplier=0).then_inc(made, 1)
            pool.iota(raw_place[:], [[0, 2], [1, P]], base=0, channel_multiplier=0).then_inc(made, 1)
            pool.memset(sh.ident[:], 0.0).then_inc(made, 1)
            pool.memset(zeros[:], 0.0).then_inc(made, 1)
            pool.memset(fc1[:], 0.0).then_inc(made, 1)
            pool.wait_ge(made, 5)
            pool.affine_select(out=sh.ident[:], in_=sh.ident[:], compare_op=ALU.not_equal, fill=1.0, base=0,
                               pattern=[[-1, P]], channel_multiplier=1).then_inc(made, 1)

            def group(g, slot, n):
                wait_apart(pool, ticks, hidden_done, g + 1)
                wait_apart(pool, ticks, factor_in, g - 1)
                pool.tensor_tensor(radial[:, slot % 2], hidden[:, slot % 2],
                                   fc2[:].unsqueeze(1).broadcast_to([P, 2 * RT, HIDDEN]), ALU.mult).then_inc(radial_done, 1)
            pool.wait_ge(fc2_in, 16)
            for_groups(pool, 4, group)

        @block.vector
        def _(dve):
            steps = [0]

            def chain(ins):
                steps[0] += 1
                ins.then_inc(dve_step, 1)
                dve.wait_ge(dve_step, steps[0])

            dve.wait_ge(made, 2)
            dve.tensor_copy(sh.iota[:], sh.iota_i[:]).then_inc(dve_step, 1)
            dve.tensor_copy(place[:], raw_place[:]).then_inc(dve_step, 1)
            steps[0] += 2
            dve.wait_ge(edges_in, 96)
            dve.tensor_copy(cols[:, SRC], raw[:, 0]).then_inc(dve_step, 1)
            dve.tensor_copy(prv[:], raw[:, 1]).then_inc(dve_step, 1)
            dve.tensor_copy(own[:], raw[:, 2]).then_inc(dve_step, 1)
            steps[0] += 3
            chain(dve.tensor_copy(nxt[:], raw[:, 3]))
            dve.tensor_tensor(is_first[:], own[:], prv[:], ALU.not_equal).then_inc(dve_step, 1)
            dve.tensor_scalar(cols[:, DST], own[:], float(NODES - 1), None, ALU.min).then_inc(dve_step, 1)
            dve.tensor_copy(dummy[:], dummy_i[:]).then_inc(dve_step, 1)
            steps[0] += 3
            chain(dve.tensor_tensor(is_last[:], own[:], nxt[:], ALU.not_equal))
            dve.tensor_scalar(first_mask[:], is_first[:], -BIG, None, ALU.mult).then_inc(masks_made, 1)
            dve.tensor_scalar(last_mask[:], is_last[:], -BIG, None, ALU.mult).then_inc(masks_made, 1)
            chain(dve.tensor_tensor(work[:], own[:], dummy[:], ALU.subtract))
            chain(dve.tensor_tensor(work[:], work[:], is_last[:], ALU.mult))
            chain(dve.tensor_tensor(cols[:, LAST_ROW], work[:], dummy[:], ALU.add))
            chain(dve.tensor_tensor(work[:], own[:], dummy[:], ALU.subtract))
            chain(dve.tensor_tensor(work[:], work[:], is_first[:], ALU.mult))
            chain(dve.tensor_tensor(cols[:, FIRST_ROW], work[:], dummy[:], ALU.add))
            chain(dve.tensor_scalar(work[:], is_last[:], -999.0, 999.0, ALU.mult, ALU.add))
            chain(dve.tensor_tensor(work[:], work[:], place[:], ALU.add))
            chain(dve.memset(work[:, :, P - 1:P], float(P - 1)))
            for h in range(2):
                chain(dve.tensor_tensor_scan(ends[:, h, ::-1], work[:, h, ::-1], work[:, h, ::-1], 999.0, ALU.min, ALU.min))
            chain(dve.scalar_tensor_tensor(work[:], place[:], 1.0, is_first[:], ALU.add, ALU.mult))
            chain(dve.memset(work[:, :, 0:1], 1.0))
            for h in range(2):
                chain(dve.tensor_tensor_scan(starts[:, h, :], work[:, h, :], work[:, h, :], 0.0, ALU.max, ALU.max))
            chain(dve.tensor_scalar(starts[:], starts[:], -1.0, None, ALU.add))
            chain(dve.tensor_copy(cols[:, END], ends[:]))
            chain(dve.tensor_copy(cols[:, START], starts[:]))
            for col, flag, near, into, at in ((FROM_PREV, is_first, 0, ends, P - 1), (FROM_NEXT, is_last, P - 1, starts, 0)):
                chain(dve.memset(cols[:, col], -1.0))
                chain(dve.tensor_scalar(one[:], flag[:, :, near:near + 1], -1.0, 1.0, ALU.mult, ALU.add))
                chain(dve.scalar_tensor_tensor(one[:], into[:, :, near:near + 1], 1.0, one[:], ALU.add, ALU.mult))
                chain(dve.tensor_scalar(cols[:, col, :, at:at + 1], one[:], -1.0, None, ALU.add))
            dve.tensor_copy(one[:], one[:]).then_inc(cols_made, 1)
            chain(dve.tensor_scalar(rounds[:], highest[:], 1.0 / ROUND_ROWS, 1.5, ALU.mult, ALU.add))
            chain(dve.tensor_scalar(rounds_i[:], rounds[:], float(COPY_ROUNDS), None, ALU.min))
            chain(dve.tensor_scalar(sh.copies_needed[:], rounds_i[:], 16.0, None, ALU.mult))

            dve.wait_ge(weights_in, 112)
            chain(dve.tensor_scalar(sh.w_a[0:MUL], sh.w_a[0:MUL], W_SCALE, None, ALU.mult))
            chain(dve.tensor_scalar(sh.w_a[MUL:P], sh.w_a[MUL:P], W_SCALE_11, None, ALU.mult))
            chain(dve.tensor_scalar(sh.w_b[:], sh.w_b[:], W_SCALE, None, ALU.mult))
            for c in range(2):
                wc = sh.w_c[:, c, 0:FEAT].rearrange("p (h d) -> p h d", h=HEADS)
                for k, out in ((0, sh.w_c[:, c, FEAT:FW]), (1, sh.w_dst[:, c])):
                    chain(dve.tensor_tensor(wprod[:], wc, a_all[:, :, k * HID:(k + 1) * HID], ALU.mult))
                    chain(dve.tensor_reduce(out, wprod[:], AX_X, ALU.add))

            def group(g, slot, n):
                dve.wait_ge(radial_done, g + 1)
                dve.tensor_reduce(factors[:, bass.ds(g * RT, RT)], radial[:, slot % 2], AX_X, ALU.add).then_inc(factor_in, 1)
            for_groups(dve, 4, group)

            for half in range(4):
                dve.wait_ge(cols_turned, half + 1)
                for k in (2 * half, 2 * half + 1):
                    at = k % 2 * TILES
                    dve.tensor_copy(sh.index[k][:], ps[:, half, at:at + TILES])

            dve.wait_ge(factor_in, NG)
            halves = lambda ap: ap.rearrange("p (h t) c -> p h t c", h=2)
            dve.tensor_tensor(halves(sh.coef[:]), halves(attr[:]),
                              factors[:].rearrange("p t h -> p h t").unsqueeze(3).broadcast_to([P, 2, HALF, 4]), ALU.mult)

        @block.tensor
        def _(pe):
            pe.wait_ge(weights_in, 112)

            def group(g, slot, n):
                pe.wait_ge(lens_copied, g + 1)
                wait_past(pe, hidden_done, g - 1)
                for t in range(RT):
                    last = pe.matmul(ps[:, 4 + slot % 2, t * 2 * HIDDEN:(t + 1) * 2 * HIDDEN],
                                     lens_slot[:, slot % 2, t * P:(t + 1) * P], fc1[:], start=True, stop=True)
                last.then_inc(hidden_in, 1)
            for_groups(pe, 4, group)
            pe.wait_ge(made, 6)
            pe.wait_ge(cols_made, 1)
            for k in range(8):
                for h in range(2):
                    at = (k % 2 * 2 + h) * HALF
                    last = pe.transpose(ps[:, k // 2, at:at + HALF], cols[:, k, h], sh.ident[0:HALF, 0:HALF])
                if k % 2:
                    last.then_inc(cols_turned, 1)

        @block.scalar
        def _(act):
            def copy_lens(g, slot):
                act.activation(lens_slot[:, slot % 2], lens[:, bass.ds(g * RT * P, RT * P)], ACT.Copy).then_inc(lens_copied, 1)

            def group(g, slot, n):
                act.wait_ge(hidden_in, g + 1)
                if there(g + 2):
                    copy_lens(g + 2, slot)
                wait_past(act, radial_done, g - 1)
                act.activation(hidden[:, slot % 2].rearrange("p t k -> p (t k)"), ps[:, 4 + slot % 2, 0:2 * RT * HIDDEN], ACT.Silu, scale=RADIAL_SCALE).then_inc(hidden_done, 1)
            act.wait_ge(lens_in, 32)
            copy_lens(0, 0)
            copy_lens(1, 1)
            for_groups(act, 4, group)


def start_stats(ctx, nc, depth, phase):
    ln = Shared()
    ln.depth = depth
    sb = lambda name, shape, dt=F32: ctx.enter_context(nc.sbuf_tensor(f"{phase}_{name}", shape, dt))
    sem = lambda name: ctx.enter_context(nc.semaphore(f"{phase}_{name}"))
    ln.rows = sb("rows", [P, depth, G, FEAT])
    ln.parts = sb("parts", [P, depth, G, 6])
    ln.mean_var = sb("mean_var", [P, depth, G, 2])
    ln.minus_mean = sb("minus_mean", [P, depth, G])
    ln.spare = sb("spare", [P, 1])
    ln.var_eps = sb("var_eps", [P, depth, G])
    ln.log_var = sb("log_var", [P, G])
    ln.guess = sb("guess", [P, depth, G])
    ln.factor = sb("factor", [P, G])
    ln.rstd = sb("rstd", [P, depth, G])
    ln.rows_in = [sem(f"rows_in{s}") for s in range(depth)]
    ln.parts_done = sem("parts_done")
    ln.mean_done = sem("mean_done")
    ln.var_ready = sem("var_ready")
    ln.log_done = sem("log_done")
    ln.guess_ready = sem("guess_ready")
    ln.newton_step = sem("newton_step")
    ln.rstd_ready = sem("rstd_ready")
    ln.relu_done = sem("relu_done")
    ln.bound = None
    return ln


def gather_rows(pool, ln, table, index_slot, slot, tiles=range(G)):
    for u in tiles:
        pool.indirect_dma_start(ln.rows[:, slot, u], None, table,
                                bass.IndirectOffsetOnAxis(ap=index_slot[:, u:u + 1], axis=0),
                                bounds_check=ln.bound, oob_is_err=False).then_inc(ln.rows_in[slot], 16)


def statistics(dve, ln, j, slot, n, by_act=False):
    dve.wait_ge(ln.rows_in[slot], n * 16 * G + 16 * G)
    for u in range(G):
        last = dve.bn_stats(ln.parts[:, slot, u], ln.rows[:, slot, u])
    last.then_inc(ln.parts_done, 1)
    dve.wait_ge(ln.parts_done, j + 1)
    dve.memset(ln.spare[:], 0.0)
    for u in range(G):
        last = dve.bn_aggr(ln.mean_var[:, slot, u], ln.parts[:, slot, u])
    last.then_inc(ln.mean_done, 1)
    dve.wait_ge(ln.mean_done, j + 1)
    wait_past(dve, ln.guess_ready, j - ln.depth + 1)
    if by_act:
        dve.tensor_scalar(ln.minus_mean[:, slot], ln.mean_var[:, slot, :, 0], -1.0, None, ALU.mult)
    dve.tensor_scalar(ln.var_eps[:, slot], ln.mean_var[:, slot, :, 1], EPS, None, ALU.add).then_inc(ln.var_ready, 1)


def relu(dve, ln, slot):
    for u in range(G):
        last = dve.tensor_scalar(ln.rows[:, slot, u], ln.rows[:, slot, u], ln.mean_var[:, slot, u, 0:1], 0.0,
                                 ALU.subtract, ALU.max)
    last.then_inc(ln.relu_done, 1)


def relu_by_act(act, ln, j, slot):
    act.wait_ge(ln.var_ready, j + 1)
    for u in range(G):
        last = act.activation(ln.rows[:, slot, u], ln.rows[:, slot, u], ACT.Relu, bias=ln.minus_mean[:, slot, u:u + 1])
    last.then_inc(ln.relu_done, 1)


def load_exp_and_ln(nc, act):
    act.add_instruction(mybir.InstLoadActFuncSet(name=nc.get_next_instruction_name(), act_func_set_id=EXP_LN_SET, ins=[], outs=[]))


def guess_inverse_std(act, ln, j, slot):
    act.wait_ge(ln.var_ready, j + 1)
    wait_past(act, ln.guess_ready, j)
    act.activation(ln.log_var[:], ln.var_eps[:, slot], ACT.Ln).then_inc(ln.log_done, 1)
    act.wait_ge(ln.log_done, j + 1)
    wait_past(act, ln.rstd_ready, j - ln.depth + 1)
    act.activation(ln.guess[:, slot], ln.log_var[:], ACT.Exp, scale=-0.5).then_inc(ln.guess_ready, 1)


def inverse_std(dve, ln, j, slot):
    dve.wait_ge(ln.guess_ready, j + 1)
    wait_past(dve, ln.rstd_ready, j)
    dve.scalar_tensor_tensor(ln.factor[:], ln.var_eps[:, slot], -0.5, ln.guess[:, slot], ALU.mult, ALU.mult).then_inc(ln.newton_step, 1)
    dve.wait_ge(ln.newton_step, j * 2 + 1)
    dve.tensor_tensor(ln.factor[:], ln.factor[:], ln.guess[:, slot], ALU.mult).then_inc(ln.newton_step, 1)
    dve.wait_ge(ln.newton_step, j * 2 + 2)
    dve.scalar_tensor_tensor(ln.rstd[:, slot], ln.factor[:], 1.5, ln.guess[:, slot], ALU.add, ALU.mult).then_inc(ln.rstd_ready, 1)


def layer0(nc, io, sh):
    D = 4
    UW = 4 * P
    with ExitStack() as ctx:
        sb = lambda name, shape, dt=F32: ctx.enter_context(nc.sbuf_tensor(f"layer0_{name}", shape, dt))
        sem = lambda name: ctx.enter_context(nc.semaphore(f"layer0_{name}"))
        ln = start_stats(ctx, nc, D, "layer0")
        src_slot = sb("src_slot", [P, D, G], I32)
        dst_slot = sb("dst_slot", [P, D, G], I32)
        needed_slot = sb("needed_slot", [1, D], I32)
        scaled = sb("scaled", [P, 2, G, 4])
        by_part = sb("by_part", [P, G, MUL, 3])
        prod = sb("prod", [P, 2, G, UW])
        sel = sb("sel", [P, 2, 2, G, P])
        summed = sb("summed", [P, 2, UW])
        msg = sb("msg", [P, D, G, FEAT])
        src_copied = sem("src_copied")
        dst_copied = sem("dst_copied")
        scattered = [sem(f"scattered{s}") for s in range(D)]
        scaled_done = sem("scaled_done")
        parts_made = sem("parts_made")
        zeroed = sem("zeroed")
        prod_ready = sem("prod_ready")
        sum_done = sem("sum_done")
        sum_out = sem("sum_out")
        msg_done = sem("msg_done")
        msg_out = sem("msg_out")
        ticks = sem("ticks")
        block = ctx.enter_context(nc.Block())
        ps = sh.psum
        acc = [ps[:, q] for q in range(2)]

        @block.sync
        def _(sp):
            copy_nodes(sp, io, sh, EARLY_ROUNDS, COPY_ROUNDS)

        @block.gpsimd
        def _(pool):
            ln.bound = pool.to_reg(NODES - 1)
            out_bound = pool.to_reg(OUT_ROWS - 1)

            def copy_sources(g, slot):
                wait_apart(pool, ticks, ln.var_ready, g - D + 1)
                pool.tensor_copy(src_slot[:, slot], sh.index[SRC][:, tiles_of(g)]).then_inc(src_copied, 1)

            def copy_targets(g, slot, n):
                wait_apart(pool, ticks, scattered[slot], n * 16 * G)
                pool.tensor_copy(needed_slot[:, slot:slot + 1], sh.copies_needed[:, bass.ds(g, 1)])
                pool.tensor_copy(dst_slot[:, slot], sh.index[LAST_ROW][:, tiles_of(g)]).then_inc(dst_copied, 1)

            def scatter(slot, u):
                pool.indirect_dma_start(io.nodes, bass.IndirectOffsetOnAxis(ap=dst_slot[:, slot, u:u + 1], axis=0),
                                        msg[:, slot, u], None, bounds_check=out_bound,
                                        compute_op=ALU.add).then_inc(scattered[slot], 16)

            def group(g, slot, n):
                near, back = (slot + 3) % D, (slot + 1) % D
                if there(g + 3):
                    wait_apart(pool, ticks, prod_ready, g)
                    wait_apart(pool, ticks, src_copied, g + 4)
                if there(g - 3):
                    wait_apart(pool, ticks, dst_copied, g - 2)
                    wait_apart(pool, ticks, msg_out, (g - 2) * G)
                    needed = pool.value_load(needed_slot[:, back:back + 1], min_val=16, max_val=16 * COPY_ROUNDS)
                    for copied in sh.copied:
                        wait_apart(pool, ticks, copied, needed)
                for u in range(G):
                    if there(g + 3):
                        gather_rows(pool, ln, io.x, src_slot[:, near], near, (u,))
                    if u == 1 and there(g + 4):
                        copy_sources(g + 4, slot)
                    if u == 2 and there(g - 2):
                        copy_targets(g - 2, *after(slot, n - 1, D, 2))
                    if there(g - 3):
                        scatter(back, u)
            pool.memset(msg[:, D - 1, G - 1], 0.0).then_inc(zeroed, 1)
            for g in range(D):
                copy_sources(g, g)
            for g in range(3):
                wait_apart(pool, ticks, src_copied, g + 1)
                gather_rows(pool, ln, io.x, src_slot[:, g], g)
            for_groups(pool, D, group)
            for g in range(NG, NG + 3):
                group(g, g % D, g // D)
            for slot in range(D):
                pool.wait_ge(scattered[slot], 16 * G * len(range(slot, NG, D)))

        @block.vector
        def _(dve):
            def products(g, slot, q):
                inverse_std(dve, ln, g, slot)
                dve.wait_ge(ln.relu_done, g + 1)
                wait_past(dve, msg_done, (g - 1) * G)
                dve.wait_ge(ln.rstd_ready, g + 1)
                dve.tensor_tensor(scaled[:, q], sh.coef[:, tiles_of(g)],
                                  ln.rstd[:, slot].unsqueeze(2).broadcast_to([P, G, 4]), ALU.mult).then_inc(scaled_done, 1)
                for k, col in enumerate((END, FROM_PREV)):
                    dve.tensor_tensor(sel[:, q, k], sh.iota[:].unsqueeze(1).broadcast_to([P, G, P]),
                                      sh.index[col][:, tiles_of(g)].unsqueeze(2).broadcast_to([P, G, P]), ALU.is_equal)
                dve.wait_ge(scaled_done, g + 1)
                s0 = ln.rows[:, slot, :, 0:MUL]
                s1 = ln.rows[:, slot, :, MUL:FEAT].rearrange("p g (i m) -> p g i m", m=3)
                c0 = scaled[:, q, :, 0:1]
                c1 = scaled[:, q, :, 1:4]
                out = prod[:, q]
                mixed = out[:, :, P:UW].rearrange("p g (m k i) -> p g m k i", m=3, k=2)
                dve.tensor_tensor(by_part[:], s1, c1.unsqueeze(2).broadcast_to([P, G, MUL, 3]), ALU.mult).then_inc(parts_made, 1)
                dve.tensor_tensor(out[:, :, 0:MUL], s0, c0.broadcast_to([P, G, MUL]), ALU.mult)
                dve.tensor_tensor(mixed[:, :, :, 0], s0.unsqueeze(2).broadcast_to([P, G, 3, MUL]),
                                  c1.unsqueeze(3).broadcast_to([P, G, 3, MUL]), ALU.mult)
                dve.tensor_tensor(mixed[:, :, :, 1], s1.rearrange("p g i m -> p g m i"),
                                  c0.unsqueeze(3).broadcast_to([P, G, 3, MUL]), ALU.mult)
                dve.wait_ge(parts_made, g + 1)
                dve.tensor_reduce(out[:, :, MUL:P], by_part[:], AX_X, ALU.add).then_inc(prod_ready, 1)

            def group(g, slot, n):
                if there(g + 1):
                    statistics(dve, ln, g + 1, *after(slot, n, D), by_act=True)
                products(g, slot, slot % 2)
            statistics(dve, ln, 0, 0, 0, by_act=True)
            for_groups(dve, D, group)

        @block.tensor
        def _(pe):
            def sum_runs(g, q, u):
                k = g * G + u
                if u == 0:
                    pe.wait_ge(prod_ready, g + 1)
                wait_past(pe, sum_out, k - 1)
                for c in range(UW // P):
                    last = pe.matmul(acc[u % 2][:, c * P:(c + 1) * P], prod[:, q, u, c * P:(c + 1) * P],
                                     sel[:, q, 0, u], start=(c == 0), stop=True, skip_group_check=True)
                last.then_inc(sum_done, 1)

            def messages(g, slot, u):
                k = g * G + u
                out = ps[:, 4 + u % 2, 0:FEAT]
                vec = out[:, MUL:FEAT].rearrange("p (o m) -> p m o", m=3)
                part = lambda c: summed[:, u % 2, c * P:(c + 1) * P]
                pe.wait_ge(sum_out, k + 1)
                pe.matmul(out[:, 0:MUL], part(0), sh.w_a[:], start=True, stop=False, skip_group_check=True)
                for m in range(3):
                    pe.matmul(vec[:, m], part(1 + m), sh.w_b[:], start=False, stop=False, skip_group_check=True)
                if isinstance(k, int) and k == 0:
                    pe.wait_ge(zeroed, 1)
                else:
                    pe.wait_ge(msg_out, k)
                before = msg[:, slot, u - 1] if u else msg[:, (slot + D - 1) % D, G - 1]
                pe.matmul(out, sel[:, slot % 2, 1, u], before, start=False, stop=True,
                          skip_group_check=True).then_inc(msg_done, 1)

            def group(g, slot, n):
                for u in range(G):
                    if u < G - 1:
                        sum_runs(g, slot % 2, u + 1)
                    elif there(g + 1):
                        sum_runs(g + 1, (slot + 1) % 2, 0)
                    messages(g, slot, u)
            sum_runs(0, 0, 0)
            for_groups(pe, D, group)

        @block.scalar
        def _(act):
            load_exp_and_ln(nc, act)
            def sums_out(g, u):
                k = g * G + u
                act.wait_ge(sum_done, k + 1)
                wait_past(act, msg_done, k - 1)
                act.activation(summed[:, u % 2], acc[u % 2], ACT.Copy).then_inc(sum_out, 1)

            def group(g, slot, n):
                for u in range(G):
                    if u < G - 1:
                        sums_out(g, u + 1)
                    elif there(g + 1):
                        sums_out(g + 1, 0)
                    if u == 0:
                        wait_past(act, scattered[slot], n * 16 * G)
                    act.wait_ge(msg_done, g * G + u + 1)
                    act.activation(msg[:, slot, u], ps[:, 4 + u % 2, 0:FEAT], ACT.Copy).then_inc(msg_out, 1)
                    if u == 0 and there(g + 2):
                        relu_by_act(act, ln, g + 2, (slot + 2) % D)
                        guess_inverse_std(act, ln, g + 2, (slot + 2) % D)
            for g in range(2):
                relu_by_act(act, ln, g, g)
                guess_inverse_std(act, ln, g, g)
            sums_out(0, 0)
            for_groups(act, D, group)


def project(nc, io, sh):
    D = 4
    with ExitStack() as ctx:
        sb = lambda name, shape, dt=F32: ctx.enter_context(nc.sbuf_tensor(f"project_{name}", shape, dt))
        sem = lambda name: ctx.enter_context(nc.semaphore(f"project_{name}"))
        ln = start_stats(ctx, nc, D, "project")
        src_slot = sb("src_slot", [P, D, G], I32)
        turned = sb("turned", [P, 2, 2 * P])
        wh = sb("wh", [P, D, G, FW])
        mask = sb("mask", [HEADS, D, GE])
        top = sb("top", [HEADS, D, GE])
        src_copied = sem("src_copied")
        mask_in = [sem(f"mask_in{s}") for s in range(D)]
        wh_stored = [sem(f"wh_stored{s}") for s in range(D)]
        top_stored = [sem(f"top_stored{s}") for s in range(D)]
        turn_done = sem("turn_done")
        turn_out = sem("turn_out")
        wh_done = sem("wh_done")
        wh_out = sem("wh_out")
        score_turned = sem("score_turned")
        top_done = sem("top_done")
        ticks = sem("ticks")
        block = ctx.enter_context(nc.Block())
        ps = sh.psum

        @block.sync
        def _(sp):
            def load_mask(g, slot):
                wait_apart(sp, ticks, top_done, g - D + 1)
                sp.dma_start(mask[:, slot], io.first_mask[edges_of(g)].partition_broadcast(HEADS)).then_inc(mask_in[slot], 16)

            def group(g, slot, n):
                if there(g + 2):
                    load_mask(g + 2, (slot + 2) % D)
                wait_apart(sp, ticks, wh_out, (g + 1) * G)
                sp.dma_start(io.wh[edges_of(g)].rearrange("(u p) f -> p u f", p=P), wh[:, slot]).then_inc(wh_stored[slot], 16)
                wait_apart(sp, ticks, top_done, g + 1)
                sp.dma_start(io.top[:, edges_of(g)], top[:, slot]).then_inc(top_stored[slot], 16)
            for g in range(2):
                load_mask(g, g)
            for_groups(sp, D, group)
            for slot in range(D):
                sp.wait_ge(wh_stored[slot], 16 * len(range(slot, NG, D)))
                sp.wait_ge(top_stored[slot], 16 * len(range(slot, NG, D)))

        @block.gpsimd
        def _(pool):
            ln.bound = pool.to_reg(NODES - 1)

            def gather(g, slot):
                wait_apart(pool, ticks, turn_done, (g - D + 1) * G)
                pool.tensor_copy(src_slot[:, slot], sh.index[SRC][:, tiles_of(g)]).then_inc(src_copied, 1)
                wait_apart(pool, ticks, src_copied, g + 1)
                gather_rows(pool, ln, io.nodes, src_slot[:, slot], slot)

            def group(g, slot, n):
                if there(g + 3):
                    gather(g + 3, (slot + 3) % D)
            for g in range(3):
                gather(g, g)
            for_groups(pool, D, group)

        @block.vector
        def _(dve):
            def running_max(g, slot, n):
                dve.wait_ge(score_turned, (g + 1) * G)
                dve.wait_ge(mask_in[slot], n * 16 + 16)
                wait_past(dve, top_stored[slot], n * 16)
                if isinstance(g, int) and g == 0:
                    initial = -BIG
                else:
                    dve.wait_ge(top_done, g)
                    initial = top[:, (slot + D - 1) % D, GE - 1:GE]
                dve.tensor_tensor_scan(top[:, slot], mask[:, slot], ps[0:HEADS, 6 + slot % 2], initial,
                                       ALU.add, ALU.max).then_inc(top_done, 1)

            def group(g, slot, n):
                if there(g + 2):
                    statistics(dve, ln, g + 2, *after(slot, n, D, 2))
                    relu(dve, ln, (slot + 2) % D)
                if there(g + 1):
                    wait_past(dve, wh_out, (g - 2) * G)
                    inverse_std(dve, ln, g + 1, (slot + 1) % D)
                if there(g - 1):
                    running_max(g - 1, *after(slot, n - 1, D, D - 1))
            for g in range(2):
                statistics(dve, ln, g, g, 0)
                relu(dve, ln, g)
            inverse_std(dve, ln, 0, 0)
            for_groups(dve, D, group)
            running_max(NG - 1, (NG - 1) % D, (NG - 1) // D)

        @block.tensor
        def _(pe):
            def turn(g, slot, u):
                if u == 0:
                    pe.wait_ge(ln.relu_done, g + 1)
                wait_past(pe, turn_out, g * G + u - 1)
                for c in range(2):
                    last = pe.transpose(ps[:, u % 2, c * P:(c + 1) * P], ln.rows[:, slot, u, c * P:(c + 1) * P], sh.ident[:])
                last.then_inc(turn_done, 1)

            def product(g, slot, u):
                k = g * G + u
                pe.wait_ge(turn_out, k + 1)
                wait_past(pe, wh_out, k - 1)
                for c in range(2):
                    last = pe.matmul(ps[:, 2 + u % 2, 0:FW], turned[:, u % 2, c * P:(c + 1) * P], sh.w_c[:, c],
                                     start=(c == 0), stop=(c == 1))
                last.then_inc(wh_done, 1)

            def turn_score(g, slot, u):
                if u == 0:
                    wait_past(pe, top_done, g - 1)
                pe.wait_ge(wh_out, g * G + u + 1)
                pe.transpose(ps[0:HEADS, 6 + slot % 2, u * P:(u + 1) * P], wh[:, slot, u, FEAT:FW],
                             sh.ident[:]).then_inc(score_turned, 1)

            def group(g, slot, n):
                for u in range(G):
                    if u < G - 1:
                        turn(g, slot, u + 1)
                    elif there(g + 1):
                        turn(g + 1, (slot + 1) % D, 0)
                    product(g, slot, u)
                    if u:
                        turn_score(g, slot, u - 1)
                    elif there(g - 1):
                        turn_score(g - 1, (slot + D - 1) % D, G - 1)
            turn(0, 0, 0)
            for_groups(pe, D, group)
            turn_score(NG - 1, (NG - 1) % D, G - 1)

        @block.scalar
        def _(act):
            load_exp_and_ln(nc, act)
            def rows_out(g, u):
                k = g * G + u
                act.wait_ge(turn_done, k + 1)
                wait_past(act, wh_done, k - 1)
                act.activation(turned[:, u % 2], ps[:, u % 2, 0:2 * P], ACT.Copy).then_inc(turn_out, 1)

            def group(g, slot, n):
                for u in range(G):
                    if u < G - 1:
                        rows_out(g, u + 1)
                    elif there(g + 1):
                        rows_out(g + 1, 0)
                    if u == 0:
                        act.wait_ge(ln.rstd_ready, g + 1)
                        wait_past(act, wh_stored[slot], n * 16)
                        wait_past(act, score_turned, (g - D + 1) * G)
                    act.wait_ge(wh_done, g * G + u + 1)
                    act.activation(wh[:, slot, u], ps[:, 2 + u % 2, 0:FW], ACT.Copy,
                                   scale=ln.rstd[:, slot, u:u + 1]).then_inc(wh_out, 1)
                    if u == 1 and there(g + 2):
                        guess_inverse_std(act, ln, g + 2, (slot + 2) % D)
            for g in range(2):
                guess_inverse_std(act, ln, g, g)
            rows_out(0, 0)
            for_groups(act, D, group)


def layer1(nc, io, sh):
    D = 4
    with ExitStack() as ctx:
        sb = lambda name, shape, dt=F32: ctx.enter_context(nc.sbuf_tensor(f"layer1_{name}", shape, dt))
        sem = lambda name: ctx.enter_context(nc.semaphore(f"layer1_{name}"))
        ln = start_stats(ctx, nc, D, "layer1")
        dst_slot = sb("dst_slot", [P, D, G], I32)
        out_slot = sb("out_slot", [P, D, G], I32)
        turned = sb("turned", [P, 2, 2 * P])
        wh = sb("wh", [P, D, G, FW])
        mask = sb("mask", [HEADS, D, GE])
        top = sb("top", [HEADS, D, GE])
        run_top = sb("run_top", [HEADS, D, GE])
        sel = sb("sel", [P, 2, 2, G, P])
        dst_score = sb("dst_score", [P, G, HEADS])
        logit = sb("logit", [P, G, 2 * HEADS])
        leaky = sb("leaky", [P, G, 2 * HEADS])
        below = sb("below", [P, 2, G, HEADS])
        weighted = sb("weighted", [P, 2, G, FW])
        total = sb("total", [P, D, G, FW])
        denom = sb("denom", [P, G, HEADS])
        inv = sb("inv", [P, G, HEADS])
        result = sb("result", [P, D, G, FEAT])
        dst_copied = sem("dst_copied")
        out_copied = sem("out_copied")
        wh_in = [sem(f"wh_in{s}") for s in range(D)]
        tops_in = [sem(f"tops_in{s}") for s in range(D)]
        scattered = [sem(f"scattered{s}") for s in range(D)]
        turn_done = sem("turn_done")
        turn_out = sem("turn_out")
        scored = sem("scored")
        top_done = sem("top_done")
        sel_ready = sem("sel_ready")
        score_step = sem("score_step")
        below_ready = sem("below_ready")
        exp_done = sem("exp_done")
        weighted_ready = sem("weighted_ready")
        zeroed = sem("zeroed")
        total_done = sem("total_done")
        total_out = sem("total_out")
        result_step = sem("result_step")
        result_ready = sem("result_ready")
        ticks = sem("ticks")
        block = ctx.enter_context(nc.Block())
        ps = sh.psum
        scores = [ps[:, b, 0:G * 2 * HEADS].rearrange("p (u k) -> p u k", u=G) for b in (2, 3)]

        group_of = lambda j: (NG - 1) - j
        starts = lambda j: isinstance(j, int) and j == 0

        @block.sync
        def _(sp):
            def load(j, slot):
                wait_apart(sp, ticks, weighted_ready, j - D + 1)
                edges = edges_of(group_of(j))
                sp.dma_start(mask[:, slot], io.last_mask[edges].partition_broadcast(HEADS)).then_inc(tops_in[slot], 16)
                sp.dma_start(top[:, slot], io.top[:, edges]).then_inc(tops_in[slot], 16)
                sp.dma_start(wh[:, slot], io.wh[edges].rearrange("(u p) f -> p u f", p=P)).then_inc(wh_in[slot], 16)

            def group(j, slot, n):
                if there(j + 3):
                    load(j + 3, (slot + 3) % D)
            for j in range(3):
                load(j, j)
            for_groups(sp, D, group)

        @block.gpsimd
        def _(pool):
            ln.bound = pool.to_reg(NODES - 1)
            out_bound = pool.to_reg(OUT_ROWS - 1)

            def copy_targets(j, slot):
                wait_apart(pool, ticks, ln.var_ready, j - D + 1)
                pool.tensor_copy(dst_slot[:, slot], sh.index[DST][:, tiles_of(group_of(j))]).then_inc(dst_copied, 1)

            def copy_firsts(j, slot, n):
                wait_apart(pool, ticks, scattered[slot], n * 16 * G)
                pool.tensor_copy(out_slot[:, slot], sh.index[FIRST_ROW][:, tiles_of(group_of(j))]).then_inc(out_copied, 1)

            def scatter(slot, u):
                pool.indirect_dma_start(io.nodes, bass.IndirectOffsetOnAxis(ap=out_slot[:, slot, u:u + 1], axis=0),
                                        result[:, slot, u], None, bounds_check=out_bound,
                                        compute_op=ALU.add).then_inc(scattered[slot], 16)

            def group(j, slot, n):
                near, back = (slot + 3) % D, (slot + 1) % D
                if there(j + 3):
                    wait_apart(pool, ticks, turn_done, j * G)
                    wait_apart(pool, ticks, dst_copied, j + 4)
                if there(j - 3):
                    wait_apart(pool, ticks, out_copied, j - 2)
                    wait_apart(pool, ticks, result_ready, j - 2)
                for v in range(G):
                    if there(j + 3):
                        gather_rows(pool, ln, io.nodes, dst_slot[:, near], near, (v,))
                    if v == 1 and there(j + 4):
                        copy_targets(j + 4, slot)
                    if v == 2 and there(j - 2):
                        copy_firsts(j - 2, *after(slot, n - 1, D, 2))
                    if there(j - 3):
                        scatter(back, G - 1 - v)
            pool.memset(total[:, D - 1, 0], 0.0).then_inc(zeroed, 1)
            for j in range(D):
                copy_targets(j, j)
            for j in range(3):
                wait_apart(pool, ticks, dst_copied, j + 1)
                gather_rows(pool, ln, io.nodes, dst_slot[:, j], j)
            for_groups(pool, D, group)
            for j in range(NG, NG + 3):
                group(j, j % D, j // D)
            for slot in range(D):
                pool.wait_ge(scattered[slot], 16 * G * len(range(slot, NG, D)))

        @block.vector
        def _(dve):
            def prepare_group(j, slot, n):
                statistics(dve, ln, j, slot, n, by_act=True)
                dve.wait_ge(tops_in[slot], n * 32 + 32)
                wait_past(dve, scored, (j - D + 1) * G)
                if starts(j):
                    initial = -BIG
                else:
                    dve.wait_ge(top_done, j)
                    initial = run_top[:, (slot + D - 1) % D, 0:1]
                dve.tensor_tensor_scan(run_top[:, slot, ::-1], mask[:, slot, ::-1], top[:, slot, ::-1], initial,
                                       ALU.add, ALU.max).then_inc(top_done, 1)

            def logits(j, slot, n):
                inverse_std(dve, ln, j, slot)
                dve.wait_ge(scored, (j + 1) * G)
                dve.wait_ge(wh_in[slot], n * 16 + 16)
                dve.wait_ge(ln.rstd_ready, j + 1)
                dve.tensor_tensor(dst_score[:], scores[slot % 2][:, :, 0:HEADS],
                                  ln.rstd[:, slot].unsqueeze(2).broadcast_to([P, G, HEADS]), ALU.mult).then_inc(score_step, 1)
                dve.wait_ge(score_step, j * 3 + 1)
                dve.tensor_tensor(logit[:, :, 0:HEADS], wh[:, slot, :, FEAT:FW], dst_score[:], ALU.add)
                dve.tensor_tensor(logit[:, :, HEADS:2 * HEADS], scores[slot % 2][:, :, HEADS:2 * HEADS], dst_score[:],
                                  ALU.add).then_inc(score_step, 1)
                dve.wait_ge(score_step, j * 3 + 2)
                dve.scalar_tensor_tensor(leaky[:], logit[:], SLOPE, logit[:], ALU.mult, ALU.max).then_inc(score_step, 1)
                dve.wait_ge(score_step, j * 3 + 3)
                dve.tensor_tensor(below[:, slot % 2], leaky[:, :, 0:HEADS], leaky[:, :, HEADS:2 * HEADS],
                                  ALU.subtract).then_inc(below_ready, 1)

            def selections(j, q):
                wait_apart(dve, ticks, total_done, (j - 1) * G)
                for k, col in enumerate((START, FROM_NEXT)):
                    last = dve.tensor_tensor(sel[:, q, k], sh.iota[:].unsqueeze(1).broadcast_to([P, G, P]),
                                             sh.index[col][:, tiles_of(group_of(j))].unsqueeze(2).broadcast_to([P, G, P]),
                                             ALU.is_equal)
                last.then_inc(sel_ready, 1)

            def weigh(j, slot):
                dve.wait_ge(exp_done, j + 1)
                out = weighted[:, slot % 2]
                dve.tensor_tensor(out[:, :, 0:FEAT].rearrange("p g (h d) -> p g h d", h=HEADS),
                                  wh[:, slot, :, 0:FEAT].rearrange("p g (h d) -> p g h d", h=HEADS),
                                  over_heads(out[:, :, FEAT:FW]), ALU.mult).then_inc(weighted_ready, 1)

            def quotients(j, slot, n):
                dve.wait_ge(total_out, (j + 1) * G)
                dve.tensor_scalar(denom[:], total[:, slot, :, FEAT:FW], 1e-30, None, ALU.max).then_inc(result_step, 1)
                dve.wait_ge(result_step, j * 2 + 1)
                dve.reciprocal(inv[:], denom[:]).then_inc(result_step, 1)
                dve.wait_ge(result_step, j * 2 + 2)
                wait_past(dve, scattered[slot], n * 16 * G)
                dve.tensor_tensor(result[:, slot].rearrange("p g (h d) -> p g h d", h=HEADS),
                                  total[:, slot, :, 0:FEAT].rearrange("p g (h d) -> p g h d", h=HEADS),
                                  over_heads(inv[:]), ALU.mult).then_inc(result_ready, 1)

            def group(j, slot, n):
                logits(j, slot, n)
                if there(j - 2):
                    quotients(j - 2, *after(slot, n - 1, D, 2))
                selections(j, slot % 2)
                if there(j + 2):
                    prepare_group(j + 2, *after(slot, n, D, 2))
                weigh(j, slot)
            for j in range(2):
                prepare_group(j, j, 0)
            for_groups(dve, D, group)
            for j in (NG - 2, NG - 1):
                quotients(j, j % D, j // D)

        @block.tensor
        def _(pe):
            def turn(j, slot, v):
                if v == 0:
                    pe.wait_ge(ln.relu_done, j + 1)
                wait_past(pe, turn_out, j * G + v - 1)
                u = G - 1 - v
                for c in range(2):
                    last = pe.transpose(ps[:, v % 2, c * P:(c + 1) * P], ln.rows[:, slot, u, c * P:(c + 1) * P], sh.ident[:])
                last.then_inc(turn_done, 1)

            def score(j, slot, v):
                u = G - 1 - v
                if v == 0:
                    wait_past(pe, below_ready, j - 1)
                    pe.wait_ge(top_done, j + 1)
                pe.wait_ge(turn_out, j * G + v + 1)
                for c in range(2):
                    pe.matmul(scores[slot % 2][:, u, 0:HEADS], turned[:, v % 2, c * P:(c + 1) * P], sh.w_dst[:, c],
                              start=(c == 0), stop=(c == 1))
                pe.transpose(scores[slot % 2][:, u, HEADS:2 * HEADS], run_top[:, slot, u * P:(u + 1) * P],
                             sh.ident[0:HEADS, 0:HEADS]).then_inc(scored, 1)

            def sum_runs(j, slot, v):
                u = G - 1 - v
                k = j * G + v
                if v == 0:
                    pe.wait_ge(weighted_ready, j + 1)
                    pe.wait_ge(sel_ready, j + 1)
                wait_past(pe, total_out, k - 1)
                pe.matmul(ps[:, 4 + v % 2, 0:FW], sel[:, slot % 2, 0, u], weighted[:, slot % 2, u], start=True, stop=False)

            def add_next(j, slot, v):
                u = G - 1 - v
                k = j * G + v
                if starts(k):
                    pe.wait_ge(zeroed, 1)
                else:
                    pe.wait_ge(total_out, k)
                before = total[:, slot, u + 1] if v else total[:, (slot + D - 1) % D, 0]
                pe.matmul(ps[:, 4 + v % 2, 0:FW], sel[:, slot % 2, 1, u], before, start=False, stop=True).then_inc(total_done, 1)

            def step(j, slot, sums, turns):
                if turns:
                    turn(j + 1, (slot + 1) % D, 0)
                for v in range(G):
                    if sums:
                        sum_runs(j - 1, (slot + D - 1) % D, v)
                    if turns and v < G - 1:
                        turn(j + 1, (slot + 1) % D, v + 1)
                    if sums:
                        add_next(j - 1, (slot + D - 1) % D, v)
                    if turns:
                        score(j + 1, (slot + 1) % D, v)

            def group(j, slot, n):
                step(j, slot, there(j - 1), there(j + 1))
            step(-1, D - 1, False, True)
            for_groups(pe, D, group)
            step(NG, NG % D, True, False)

        @block.scalar
        def _(act):
            load_exp_and_ln(nc, act)
            def rows_out(j, v):
                k = j * G + v
                act.wait_ge(turn_done, k + 1)
                wait_past(act, scored, k - 1)
                act.activation(turned[:, v % 2], ps[:, v % 2, 0:2 * P], ACT.Copy).then_inc(turn_out, 1)

            def sums_out(j, slot, v):
                if v == 0:
                    wait_past(act, result_ready, j - D + 1)
                act.wait_ge(total_done, j * G + v + 1)
                act.activation(total[:, slot, G - 1 - v], ps[:, 4 + v % 2, 0:FW], ACT.Copy).then_inc(total_out, 1)

            def exponentials(j, q):
                act.wait_ge(below_ready, j + 1)
                wait_past(act, total_done, (j - 1) * G)
                act.activation(weighted[:, q, :, FEAT:FW], below[:, q], ACT.Exp).then_inc(exp_done, 1)

            def step(j, slot, sums, turns):
                if turns:
                    rows_out(j + 1, 0)
                for v in range(G):
                    if turns and v < G - 1:
                        rows_out(j + 1, v + 1)
                    if sums:
                        sums_out(j - 1, (slot + D - 1) % D, v)
                    if v == 1 and there(j):
                        exponentials(j, slot % 2)
                    if v == 2 and there(j) and there(j + 2):
                        relu_by_act(act, ln, j + 2, (slot + 2) % D)
                        guess_inverse_std(act, ln, j + 2, (slot + 2) % D)

            def group(j, slot, n):
                step(j, slot, there(j - 1), there(j + 1))
            for j in range(2):
                relu_by_act(act, ln, j, j)
                guess_inverse_std(act, ln, j, j)
            step(-1, D - 1, False, True)
            for_groups(act, D, group)
            step(NG, NG % D, True, False)


INPUTS = (("x", (NODES, FEAT), F32), ("src", (EPAD,), I32), ("dst", (EPAD + 2,), I32), ("spare_rows", (HALF, 2, P), I32),
          ("attr", (P, TILES, 4), F32),
          ("lens", (LEN_IN, EPAD), F32), ("attr_rows", (EPAD, 4), F32), ("lens_rows", (EPAD, LEN_IN), F32), ("w_a", (P, MUL), F32), ("w_b", (P, MUL), F32),
          ("fc_w1", (LEN_IN, HIDDEN), F32), ("fc_w2", (HIDDEN, 1), F32), ("w_c", (FEAT, FEAT), F32),
          ("a", (HEADS, 2 * HID), F32))


def build(nc):
    io, sh = Shared(), Shared()
    (io.x, io.src, io.dst, io.spare_rows, io.attr, io.lens, io.attr_rows, io.lens_rows, io.w_a, io.w_b, io.fc_w1,
     io.fc_w2, io.w_c, io.a) = [nc.dram_tensor(name, shape, dt, kind="ExternalInput").ap() for name, shape, dt in INPUTS]
    io.nodes = nc.dram_tensor("nodes", (OUT_ROWS, FEAT), F32, kind="ExternalOutput").ap()
    io.table = nc.dram_tensor("edge_table", (EPAD, RECORD), I32, kind="Internal").ap()
    io.src_w = nc.dram_tensor("src_work", (EPAD,), I32, kind="Internal").ap()
    io.dst_w = nc.dram_tensor("dst_work", (EPAD + 2,), I32, kind="Internal").ap()
    io.attr_w = nc.dram_tensor("attr_work", (P, TILES, 4), F32, kind="Internal").ap()
    io.lens_w = nc.dram_tensor("lens_work", (LEN_IN, EPAD), F32, kind="Internal").ap()
    io.first_mask = nc.dram_tensor("first_mask_rows", (EPAD,), F32, kind="Internal").ap()
    io.last_mask = nc.dram_tensor("last_mask_rows", (EPAD,), F32, kind="Internal").ap()
    io.wh = nc.dram_tensor("wh_rows", (EPAD, FW), F32, kind="Internal").ap()
    io.top = nc.dram_tensor("top_rows", (HEADS, EPAD), F32, kind="Internal").ap()
    with ExitStack() as ctx:
        sb = lambda name, shape, dt=F32: ctx.enter_context(nc.sbuf_tensor(name, shape, dt))
        sh.psum = io.psum = ctx.enter_context(nc.psum_tensor("psum", [P, 8, 512], F32))
        order_edges(nc, io)
        sh.copied = [ctx.enter_context(nc.semaphore(f"nodes_copied{s}")) for s in range(COPY_SLOTS)]
        sh.copy_ticks = ctx.enter_context(nc.semaphore("copy_ticks"))
        sh.copies_needed = sb("copies_needed", [1, NG], I32)
        sh.iota_i = sb("iota_i", [P, P], I32)
        sh.iota = sb("iota", [P, P])
        sh.ident = sb("ident", [P, P])
        sh.index = [sb(f"index{k}", [P, TILES], I32 if k < END else F32) for k in range(8)]
        sh.coef = sb("coef", [P, TILES, 4])
        sh.w_a = sb("w_a_sb", [P, MUL])
        sh.w_b = sb("w_b_sb", [P, MUL])
        sh.w_c = sb("w_c_sb", [P, 2, FW])
        sh.w_dst = sb("w_dst_sb", [P, 2, HEADS])
        prepare(nc, io, sh)
        layer0(nc, io, sh)
        project(nc, io, sh)
        layer1(nc, io, sh)


def layout(x, src, dst, edge_attr_10, edge_attr_4, L0_gnn_w_00_0, L0_gnn_w_11_0, L0_gnn_w_01_1, L0_gnn_w_10_1,
           L0_gnn_fc_w1, L0_gnn_fc_w2, L1_gnn_W, L1_gnn_a):
    pad = EPAD - EDGES
    attr_rows = np.concatenate([edge_attr_4, np.zeros((pad, 4), edge_attr_4.dtype)])
    lens_rows = np.concatenate([edge_attr_10, np.zeros((pad, LEN_IN), edge_attr_10.dtype)])
    return {
        "x": x,
        "src": np.concatenate([src, np.zeros(pad, src.dtype)]),
        "dst": np.concatenate([np.full(1, -1, dst.dtype), dst, np.full(pad, PAD_NODE, dst.dtype),
                               np.full(1, PAD_NODE + 1, dst.dtype)]),
        "spare_rows": (DUMMY + np.arange(EPAD, dtype=dst.dtype) % (DUMMY_TILES * P)).reshape(2, HALF, P).transpose(1, 0, 2),
        "attr": attr_rows.reshape(TILES, P, 4).transpose(1, 0, 2),
        "attr_rows": attr_rows,
        "lens": lens_rows.T,
        "lens_rows": lens_rows,
        "w_a": np.concatenate([L0_gnn_w_00_0, L0_gnn_w_11_0]),
        "w_b": np.concatenate([L0_gnn_w_01_1, L0_gnn_w_10_1]),
        "fc_w1": L0_gnn_fc_w1,
        "fc_w2": L0_gnn_fc_w2,
        "w_c": L1_gnn_W.transpose(1, 0, 2).reshape(FEAT, FEAT),
        "a": L1_gnn_a,
    }


def kernel(**inputs):
    import concourse.bacc as bacc
    from concourse.bass_utils import run_bass_kernel_spmd

    nc = bacc.Bacc("TRN2", target_bir_lowering=False, num_devices=1)
    build(nc)
    arrays = {k: np.ascontiguousarray(v) for k, v in layout(**{k: np.asarray(v) for k, v in inputs.items()}).items()}
    r = run_bass_kernel_spmd(nc, [arrays], core_ids=[0])
    return r.results[0]["nodes"][:NODES]
```
